# Optimizing a Trainium2 kernel written in Bass

```python
import numpy as np
import jax
import jax.numpy as jnp

def _softmax(x, axis=-1):
    return jax.nn.softmax(x, axis=axis)

def _gelu(x):
    return jax.nn.gelu(x, approximate=True)

def _silu(x):
    return jax.nn.silu(x)

def _sigmoid(x):
    return jax.nn.sigmoid(x)

def _layernorm(x, axis=-1, eps=1e-05):
    m = jnp.mean(x, axis=axis, keepdims=True)
    v = jnp.var(x, axis=axis, keepdims=True)
    return (x - m) / jnp.sqrt(v + eps)

def _scatter_add(tgt, idx, src, axis=0):
    return tgt.at[idx].add(src)

def _segment_sum(src, seg, n):
    return jax.ops.segment_sum(src, seg, n)
kernel_name = 'mk_xattn_ffn_d1_seqx_r8_6b2e9e'

def setup_inputs(seed: int=0):
    np.random.seed(seed)
    _w = jnp.asarray

    def _rec_inputs():
        import jax
        import jax.numpy as jnp
        _rk = jax.random.key(seed)
        x = 7.22e-05 + 1 * jax.random.normal(jax.random.fold_in(_rk, 1), (32, 128, 128), jnp.float32)
        _lenS = 128 - jax.random.randint(jax.random.fold_in(_rk, 7), (32,), 0, max(1, 128 // 4) + 1, jnp.int32)
        _lenS2 = 128 - jax.random.randint(jax.random.fold_in(_rk, 8), (32,), 0, max(1, 128 // 4) + 1, jnp.int32)
        _ctx_1024P = jax.random.normal(jax.random.fold_in(_rk, 11), (32, 16, 128), jnp.float32)
        _ctx_1024c = jax.random.dirichlet(jax.random.fold_in(_rk, 511), 0.3 * jnp.ones((16,), jnp.float32), (32, 128))
        _ctx_1024t = jnp.einsum('bsk,bkd->bsd', _ctx_1024c, _ctx_1024P)
        _ctx_1024t = _ctx_1024t * jax.lax.rsqrt(jnp.mean(jnp.square(_ctx_1024t)) + 1e-12) * 0.953939
        ctx_1024 = 4.13588e-05 + 0.999923 * (_ctx_1024t + 0.3 * jax.random.normal(jax.random.fold_in(_rk, 611), (32, 128, 128), jnp.float32))
        return (x, ctx_1024)
    x, ctx_1024 = _rec_inputs()

    def _L0_xattn_setup():
        import jax, jax.numpy as jnp
        import numpy as np
        D_MODEL = 128
        NUM_HEADS = 16
        HEAD_DIM = D_MODEL // NUM_HEADS
        MAX_SEQ = 64

        def rope_tables(seq_len, dim):
            inv_freq = 1.0 / 10000.0 ** (jnp.arange(0, dim, 2, dtype=jnp.float32) / dim)
            t = jnp.arange(seq_len, dtype=jnp.float32)
            freqs = jnp.einsum('i,j->ij', t, inv_freq)
            emb = jnp.concatenate([freqs, freqs], axis=-1)
            return (jnp.cos(emb), jnp.sin(emb))

        def rotate_half(x):
            x1, x2 = jnp.split(x, 2, axis=-1)
            return jnp.concatenate([-x2, x1], axis=-1)
        key = jax.random.key(seed)
        ks = jax.random.split(key, 12)
        B, S, D = (16, 64, D_MODEL)
        s = 1.0 / np.sqrt(D)
        inp = {'query': jax.random.normal(ks[0], (B, S, D), jnp.float32), 'key': jax.random.normal(ks[1], (B, S, D), jnp.float32), 'value': jax.random.normal(ks[2], (B, S, D), jnp.float32), 'Wq': jax.random.normal(ks[3], (D, D), jnp.float32) * s, 'bq': jnp.zeros((D,), jnp.float32), 'Wk': jax.random.normal(ks[4], (D, D), jnp.float32) * s, 'bk': jnp.zeros((D,), jnp.float32), 'Wv': jax.random.normal(ks[5], (D, D), jnp.float32) * s, 'bv': jnp.zeros((D,), jnp.float32), 'Wo': jax.random.normal(ks[6], (D, D), jnp.float32) * s, 'bo': jnp.zeros((D,), jnp.float32)}
        return inp
    _L0_xattn_all = _L0_xattn_setup()
    _L0_xattn_in = {k: v for k, v in _L0_xattn_all.items() if k in ('Wq', 'bq', 'Wk', 'bk', 'Wv', 'bv', 'Wo', 'bo')}
    del _L0_xattn_all

    def _L0_ffn_setup():
        import jax, jax.numpy as jnp
        import numpy as np
        DIM = 128
        DEPTH = 2
        HEADS = 8
        DIM_HEAD = 64
        WINDOW = 64
        INNER = HEADS * DIM_HEAD
        HID = int(DIM * 4 * 2 / 3)
        B, N = (2, 1024)
        QK_SCALE = 8.0

        def shift_token(t):
            t1, t2 = jnp.split(t, 2, axis=-1)
            t2 = jnp.pad(t2, ((0, 0), (1, 0), (0, 0)))[:, :-1]
            return jnp.concatenate([t1, t2], axis=-1)

        def l2norm(t):
            return t / jnp.clip(jnp.linalg.norm(t, axis=-1, keepdims=True), 1e-12)

        def rotate_half(x):
            x1, x2 = jnp.split(x, 2, axis=-1)
            return jnp.concatenate([-x2, x1], axis=-1)

        def rotary_xpos(q, k):
            n = q.shape[-2]
            half_idx = jnp.arange(0, DIM_HEAD, 2, dtype=jnp.float32)
            inv_freq = 1.0 / 10000.0 ** (half_idx / DIM_HEAD)
            t = jnp.arange(n, dtype=jnp.float32)
            freqs = t[:, None] * inv_freq[None, :]
            freqs = jnp.concatenate([freqs, freqs], axis=-1)
            base = (half_idx + 0.4 * DIM_HEAD) / (1.4 * DIM_HEAD)
            power = (t - n // 2) / float(WINDOW // 2)
            scale = base[None, :] ** power[:, None]
            scale = jnp.concatenate([scale, scale], axis=-1)
            cos, sin = (jnp.cos(freqs), jnp.sin(freqs))
            q = q * cos * scale + rotate_half(q) * sin * scale
            k = k * cos / scale + rotate_half(k) * sin / scale
            return (q, k)

        def local_attention(q, k, v):
            b, h, n, d = q.shape
            w = n // WINDOW
            bq = q.reshape(b, h, w, WINDOW, d) * QK_SCALE
            bk = k.reshape(b, h, w, WINDOW, d)
            bv = v.reshape(b, h, w, WINDOW, d)

            def look_around(t):
                p = jnp.pad(t, ((0, 0), (0, 0), (1, 0), (0, 0), (0, 0)))
                return jnp.concatenate([p[:, :, :w], p[:, :, 1:]], axis=3)
            bk, bv = (look_around(bk), look_around(bv))
            bt = jnp.arange(n).reshape(w, WINDOW)
            btp = jnp.pad(bt, ((1, 0), (0, 0)), constant_values=-1)
            btk = jnp.concatenate([btp[:w], btp[1:]], axis=1)
            sim = jnp.einsum('bhwid,bhwjd->bhwij', bq, bk)
            i = bt[:, :, None]
            j = btk[:, None, :]
            mask = (i < j) | (i > j + WINDOW) | (j == -1)
            sim = jnp.where(mask, -jnp.finfo(sim.dtype).max, sim)
            attn = jax.nn.softmax(sim, axis=-1)
            out = jnp.einsum('bhwij,bhwjd->bhwid', attn, bv)
            return out.reshape(b, h, n, d)

        def _layer(x, wqkv, qs, ksc, wo, lg, lb, w1, b1, w2, b2):
            b, n, _ = x.shape
            h = shift_token(x)
            qkv = h @ wqkv
            q, k, v = jnp.split(qkv, 3, axis=-1)
            to_heads = lambda t: t.reshape(b, n, HEADS, DIM_HEAD).transpose(0, 2, 1, 3)
            q, k, v = (to_heads(q), to_heads(k), to_heads(v))
            q = l2norm(q) * qs
            k = l2norm(k) * ksc
            q, k = rotary_xpos(q, k)
            o = local_attention(q, k, v)
            o = o.transpose(0, 2, 1, 3).reshape(b, n, INNER)
            x = x + o @ wo
            h = shift_token(x)
            mu = h.mean(-1, keepdims=True)
            var = h.var(-1, keepdims=True)
            h = (h - mu) / jnp.sqrt(var + 1e-05) * lg + lb
            h = h @ w1 + b1
            a, g = jnp.split(h, 2, axis=-1)
            h = a * jax.nn.gelu(g, approximate=False)
            x = x + h @ w2 + b2
            return x
        key = jax.random.key(seed)
        ks = jax.random.split(key, 6)
        return {'x': jax.random.normal(ks[0], (B, N, DIM), jnp.float32), 'wqkv': jax.random.normal(ks[1], (DEPTH, DIM, 3 * INNER), jnp.float32) * 0.02, 'q_scale': jnp.ones((DEPTH, DIM_HEAD), jnp.float32), 'k_scale': jnp.ones((DEPTH, DIM_HEAD), jnp.float32), 'wo': jax.random.normal(ks[2], (DEPTH, INNER, DIM), jnp.float32) * 0.02, 'ln_g': jnp.ones((DEPTH, DIM), jnp.float32), 'ln_b': jnp.zeros((DEPTH, DIM), jnp.float32), 'w1': jax.random.normal(ks[3], (DEPTH, DIM, 2 * HID), jnp.float32) * 0.02, 'b1': jnp.zeros((DEPTH, 2 * HID), jnp.float32), 'w2': jax.random.normal(ks[4], (DEPTH, HID, DIM), jnp.float32) * 0.02, 'b2': jnp.zeros((DEPTH, DIM), jnp.float32)}
    _L0_ffn_all = _L0_ffn_setup()
    _L0_ffn_in = {k: v for k, v in _L0_ffn_all.items() if k in ('wqkv', 'q_scale', 'k_scale', 'wo', 'ln_g', 'ln_b', 'w1', 'b1', 'w2', 'b2')}
    del _L0_ffn_all
    return {'x': x, 'ctx_1024': ctx_1024, 'L0_xattn_Wq': _L0_xattn_in['Wq'], 'L0_xattn_bq': _L0_xattn_in['bq'], 'L0_xattn_Wk': _L0_xattn_in['Wk'], 'L0_xattn_bk': _L0_xattn_in['bk'], 'L0_xattn_Wv': _L0_xattn_in['Wv'], 'L0_xattn_bv': _L0_xattn_in['bv'], 'L0_xattn_Wo': _L0_xattn_in['Wo'], 'L0_xattn_bo': _L0_xattn_in['bo'], 'L0_ffn_wqkv': _L0_ffn_in['wqkv'], 'L0_ffn_q_scale': _L0_ffn_in['q_scale'], 'L0_ffn_k_scale': _L0_ffn_in['k_scale'], 'L0_ffn_wo': _L0_ffn_in['wo'], 'L0_ffn_ln_g': _L0_ffn_in['ln_g'], 'L0_ffn_ln_b': _L0_ffn_in['ln_b'], 'L0_ffn_w1': _L0_ffn_in['w1'], 'L0_ffn_b1': _L0_ffn_in['b1'], 'L0_ffn_w2': _L0_ffn_in['w2'], 'L0_ffn_b2': _L0_ffn_in['b2']}

def reference(x, ctx_1024, L0_xattn_Wq, L0_xattn_bq, L0_xattn_Wk, L0_xattn_bk, L0_xattn_Wv, L0_xattn_bv, L0_xattn_Wo, L0_xattn_bo, L0_ffn_wqkv, L0_ffn_q_scale, L0_ffn_k_scale, L0_ffn_wo, L0_ffn_ln_g, L0_ffn_ln_b, L0_ffn_w1, L0_ffn_b1, L0_ffn_w2, L0_ffn_b2):
    import jax
    import jax.numpy as jnp

    def _L0_xattn_ref(query, key, value, Wq, bq, Wk, bk, Wv, bv, Wo, bo):
        import jax, jax.numpy as jnp
        import numpy as np
        D_MODEL = 128
        NUM_HEADS = 16
        HEAD_DIM = D_MODEL // NUM_HEADS
        MAX_SEQ = 64

        def rope_tables(seq_len, dim):
            inv_freq = 1.0 / 10000.0 ** (jnp.arange(0, dim, 2, dtype=jnp.float32) / dim)
            t = jnp.arange(seq_len, dtype=jnp.float32)
            freqs = jnp.einsum('i,j->ij', t, inv_freq)
            emb = jnp.concatenate([freqs, freqs], axis=-1)
            return (jnp.cos(emb), jnp.sin(emb))

        def rotate_half(x):
            x1, x2 = jnp.split(x, 2, axis=-1)
            return jnp.concatenate([-x2, x1], axis=-1)
        B, S, D = query.shape
        H, Hd = (NUM_HEADS, HEAD_DIM)
        scale = Hd ** (-0.5)

        def proj(x, W, b):
            y = jnp.einsum('bsd,ed->bse', x, W) + b
            return y.reshape(B, S, H, Hd).transpose(0, 2, 1, 3)
        q = proj(query, Wq, bq)
        k = proj(key, Wk, bk)
        v = proj(value, Wv, bv)
        cos, sin = rope_tables(S, Hd)
        cos = cos[None, None]
        sin = sin[None, None]
        q = q * cos + rotate_half(q) * sin
        k = k * cos + rotate_half(k) * sin
        attn = jnp.einsum('bhqd,bhkd->bhqk', q, k) * scale
        attn_w = jax.nn.softmax(attn, axis=-1)
        out = jnp.einsum('bhqk,bhkd->bhqd', attn_w, v)
        out = out.transpose(0, 2, 1, 3).reshape(B, S, D)
        out = jnp.einsum('bsd,ed->bse', out, Wo) + bo
        return out

    def _L0_ffn_ref(x, wqkv, q_scale, k_scale, wo, ln_g, ln_b, w1, b1, w2, b2):
        import jax, jax.numpy as jnp
        import numpy as np
        DIM = 128
        DEPTH = 2
        HEADS = 8
        DIM_HEAD = 64
        WINDOW = 64
        INNER = HEADS * DIM_HEAD
        HID = int(DIM * 4 * 2 / 3)
        B, N = (2, 1024)
        QK_SCALE = 8.0

        def shift_token(t):
            t1, t2 = jnp.split(t, 2, axis=-1)
            t2 = jnp.pad(t2, ((0, 0), (1, 0), (0, 0)))[:, :-1]
            return jnp.concatenate([t1, t2], axis=-1)

        def l2norm(t):
            return t / jnp.clip(jnp.linalg.norm(t, axis=-1, keepdims=True), 1e-12)

        def rotate_half(x):
            x1, x2 = jnp.split(x, 2, axis=-1)
            return jnp.concatenate([-x2, x1], axis=-1)

        def rotary_xpos(q, k):
            n = q.shape[-2]
            half_idx = jnp.arange(0, DIM_HEAD, 2, dtype=jnp.float32)
            inv_freq = 1.0 / 10000.0 ** (half_idx / DIM_HEAD)
            t = jnp.arange(n, dtype=jnp.float32)
            freqs = t[:, None] * inv_freq[None, :]
            freqs = jnp.concatenate([freqs, freqs], axis=-1)
            base = (half_idx + 0.4 * DIM_HEAD) / (1.4 * DIM_HEAD)
            power = (t - n // 2) / float(WINDOW // 2)
            scale = base[None, :] ** power[:, None]
            scale = jnp.concatenate([scale, scale], axis=-1)
            cos, sin = (jnp.cos(freqs), jnp.sin(freqs))
            q = q * cos * scale + rotate_half(q) * sin * scale
            k = k * cos / scale + rotate_half(k) * sin / scale
            return (q, k)

        def local_attention(q, k, v):
            b, h, n, d = q.shape
            w = n // WINDOW
            bq = q.reshape(b, h, w, WINDOW, d) * QK_SCALE
            bk = k.reshape(b, h, w, WINDOW, d)
            bv = v.reshape(b, h, w, WINDOW, d)

            def look_around(t):
                p = jnp.pad(t, ((0, 0), (0, 0), (1, 0), (0, 0), (0, 0)))
                return jnp.concatenate([p[:, :, :w], p[:, :, 1:]], axis=3)
            bk, bv = (look_around(bk), look_around(bv))
            bt = jnp.arange(n).reshape(w, WINDOW)
            btp = jnp.pad(bt, ((1, 0), (0, 0)), constant_values=-1)
            btk = jnp.concatenate([btp[:w], btp[1:]], axis=1)
            sim = jnp.einsum('bhwid,bhwjd->bhwij', bq, bk)
            i = bt[:, :, None]
            j = btk[:, None, :]
            mask = (i < j) | (i > j + WINDOW) | (j == -1)
            sim = jnp.where(mask, -jnp.finfo(sim.dtype).max, sim)
            attn = jax.nn.softmax(sim, axis=-1)
            out = jnp.einsum('bhwij,bhwjd->bhwid', attn, bv)
            return out.reshape(b, h, n, d)

        def _layer(x, wqkv, qs, ksc, wo, lg, lb, w1, b1, w2, b2):
            b, n, _ = x.shape
            h = shift_token(x)
            qkv = h @ wqkv
            q, k, v = jnp.split(qkv, 3, axis=-1)
            to_heads = lambda t: t.reshape(b, n, HEADS, DIM_HEAD).transpose(0, 2, 1, 3)
            q, k, v = (to_heads(q), to_heads(k), to_heads(v))
            q = l2norm(q) * qs
            k = l2norm(k) * ksc
            q, k = rotary_xpos(q, k)
            o = local_attention(q, k, v)
            o = o.transpose(0, 2, 1, 3).reshape(b, n, INNER)
            x = x + o @ wo
            h = shift_token(x)
            mu = h.mean(-1, keepdims=True)
            var = h.var(-1, keepdims=True)
            h = (h - mu) / jnp.sqrt(var + 1e-05) * lg + lb
            h = h @ w1 + b1
            a, g = jnp.split(h, 2, axis=-1)
            h = a * jax.nn.gelu(g, approximate=False)
            x = x + h @ w2 + b2
            return x
        for l in range(DEPTH):
            x = _layer(x, wqkv[l], q_scale[l], k_scale[l], wo[l], ln_g[l], ln_b[l], w1[l], b1[l], w2[l], b2[l])
        return x
    x = x + _L0_xattn_ref(_layernorm(x, axis=-1), ctx_1024, ctx_1024, L0_xattn_Wq, L0_xattn_bq, L0_xattn_Wk, L0_xattn_bk, L0_xattn_Wv, L0_xattn_bv, L0_xattn_Wo, L0_xattn_bo)
    x = x + _L0_ffn_ref(_layernorm(x, axis=-1), L0_ffn_wqkv, L0_ffn_q_scale, L0_ffn_k_scale, L0_ffn_wo, L0_ffn_ln_g, L0_ffn_ln_b, L0_ffn_w1, L0_ffn_b1, L0_ffn_w2, L0_ffn_b2)
    return x

_drawn_inputs = setup_inputs


def setup_inputs(seed=0):
    import zlib

    import numpy as np

    out = dict(_drawn_inputs(seed))
    spreads = {'L0_xattn_bq': (0.0, 0.409),
     'L0_xattn_bk': (0.0, 0.8),
     'L0_xattn_bv': (0.0, 0.1),
     'L0_xattn_bo': (0.0, 0.1),
     'L0_ffn_q_scale': (1.0, 0.6),
     'L0_ffn_k_scale': (1.0, 0.6),
     'L0_ffn_ln_g': (1.0, 0.6),
     'L0_ffn_ln_b': (0.0, 0.8),
     'L0_ffn_b1': (0.0, 0.8),
     'L0_ffn_b2': (0.0, 0.671)}
    factors = {'L0_ffn_w1': 6.608, 'L0_ffn_w2': 6.542}
    for name, (base, spread) in spreads.items():
        noise = np.random.default_rng([zlib.crc32(name.encode()), seed]).standard_normal(out[name].shape)
        drawn = base * np.exp(spread * noise) if base else spread * noise
        out[name] = jnp.asarray(drawn.astype(out[name].dtype))
    for name, factor in factors.items():
        out[name] = (out[name] * factor).astype(out[name].dtype)
    return out
```

```python
from contextlib import ExitStack

import concourse.bass as bass
from concourse import mybir

fp32 = mybir.dt.float32
bf16 = mybir.dt.bfloat16
ALU = mybir.AluOpType
ACT = mybir.ActivationFunctionType
AX = mybir.AxisListType

LEAD = 4


class Signal:

    def __init__(self, sem, per):
        self.sem, self.per = sem, per


def after(signal, g, k=None):
    return (g + LEAD) * signal.per + (signal.per if k is None else k)


def pipeline(eng, step, count, lags):
    head = lags + lags % 2
    for t in range(head):
        step(t, t % 2, lambda lag, t=t: lag <= t)
    with eng.Fori(head // 2, count // 2) as pair:
        step(2 * pair, 0, lambda lag: True)
        step(2 * pair + 1, 1, lambda lag: True)
    for t in range(count, count + lags):
        step(t, t % 2, lambda lag, t=t: t - lag < count)


def build(nc, ins, out):
    x, ctx_in = ins["x"], ins["ctx_1024"]
    NS, T, D = x.shape
    HX, DX = 16, 8
    HL, DL = 8, 64
    LAYERS = ins["L0_ffn_wqkv"].shape[0]
    INNER = HL * DL
    HID = ins["L0_ffn_w2"].shape[1]
    NJ = (HID + 127) // 128
    REST = HID - 128 * (NJ - 1)
    CH = 4
    EPS = 1e-5
    SCALE_X = float(DX) ** -0.5
    SCALE_L = 8.0
    LAGS_X, LAGS_L, LAGS_F = 4, 2, 2

    with ExitStack() as ctx:
        def sb(name, shape, dt=fp32):
            return ctx.enter_context(nc.sbuf_tensor(name, shape, dt))

        def signal(name, per=1):
            return Signal(ctx.enter_context(nc.semaphore(name)), per)

        x_all = sb("x_all", [128, NS, D])
        y_all = sb("y_all", [128, NS, D])
        ident = sb("ident", [128, 128])
        identb = sb("identb", [128, 128], bf16)
        shiftm = sb("shiftm", [128, 128])
        bandm = sb("bandm", [128, CH * 128], bf16)
        ropex = sb("ropex", [128, 2, DX])
        ropel = sb("ropel", [128, 4, DL])
        scales = sb("scales", [128, 4, DL])
        tab = sb("tab", [128, 4, DL])
        hmask = sb("hmask", [128, HX])
        nhalf = sb("nhalf", [128, 2 * HL])
        wx_in = sb("wx_in", [128, 4, D])
        wx = sb("wx", [128, 4, D])
        biasx = sb("biasx", [128, 3 * D])
        box = sb("box", [128, D])
        wqkv = sb("wqkv", [128, 3 * INNER])
        wol = sb("wol", [128, INNER // 128, D])
        w1 = sb("w1", [128, 2 * HID])
        w2 = sb("w2", [128, NJ, D])
        b1 = sb("b1", [128, 2, NJ])
        lgb = sb("lgb", [128, 2])
        ctxb = sb("ctxb", [128, 2, D])
        st = sb("st", [128, 2, 2, 6])
        mv = sb("mv", [128, 2, 2])
        ve = sb("ve", [128, 2, 1])
        rstd = sb("rstd", [128, 2, 1])
        st2 = sb("st2", [128, 2, 6])
        mv2 = sb("mv2", [128, 2, 2])
        ve2 = sb("ve2", [128, 2, 1])
        rstd2 = sb("rstd2", [128, 2, 1])
        xn = sb("xn", [128, 2, D])
        hT = sb("hT", [128, 2, 2, 128])
        raw = sb("raw", [128, 2, 2, INNER])
        sq = sb("sq", [128, 2 * INNER])
        ss = sb("ss", [128, 2, 2 * HL])
        ssc = sb("ssc", [128, 2 * HL])
        rn = sb("rn", [128, 2, 2 * HL])
        t1 = sb("t1", [128, 2, 2, INNER])
        t2 = sb("t2", [128, 2, 2, INNER])
        rot = sb("rot", [128, 2, 2 * INNER])
        qkT = sb("qkT", [128, 2, 2 * INNER])
        kx = sb("kx", [128, 2, HX, 128])
        vx = sb("vx", [128, 2, HX, DX + 1])
        vl = sb("vl", [128, 2, HL, DL + 1])
        top = sb("top", [128, 2, HX])
        prob = sb("prob", [128, 2, HX, 128])
        probT = sb("probT", [128, HX, 128])
        rsum = sb("rsum", [128, HX])
        o_sb = sb("o_sb", [128, INNER])
        oT = sb("oT", [128, INNER])
        yb = sb("yb", [128, 2, D])
        gate = sb("gate", [128, 2, NJ, 128])
        hid = sb("hid", [128, 2, NJ, 128])
        ps = ctx.enter_context(nc.psum_tensor("ps", [128, 8, 512], fp32))

        S = lambda n: ctx.enter_context(nc.semaphore(n))
        shift_zero, const_in, wx_loaded, setup_v, setup_t, setup_e = S("shift_zero"), S("const_in"), S("wx_loaded"), S("setup_v"), S("setup_t"), S("setup_e")
        x_in = [S("x_in0"), S("x_in1")]
        ctx_in_sem = [S("ctx_in0"), S("ctx_in1")]
        wl_in, wf_in, tab_ready, out_add, out_done = S("wl_in"), S("wf_in"), S("tab_ready"), S("out_add"), S("out_done")
        settled = S("settled")
        x_stat, x_mv, x_ve, x_rstd, x_norm = (signal(n) for n in ("x_stat", "x_mv", "x_ve", "x_rstd", "x_norm"))
        x_tr, x_trc, x_proj = signal("x_tr"), signal("x_trc"), signal("x_proj")
        x_bias = signal("x_bias", 2)
        x_t, x_rot, x_bo = signal("x_t", 3), signal("x_rot"), signal("x_bo")
        x_qkt, x_qc, x_kx = signal("x_qkt"), signal("x_qc"), signal("x_kx")
        x_s, x_max, x_sub, x_exp = (signal(n, HX // CH) for n in ("x_s", "x_max", "x_sub", "x_exp"))
        x_pt, x_ptc, x_pv = (signal(n, HX // CH) for n in ("x_pt", "x_ptc", "x_pv"))
        x_rsum, x_o, x_ot, x_otc, x_wo, x_res = (signal(n) for n in ("x_rsum", "x_o", "x_ot", "x_otc", "x_wo", "x_res"))
        x_stat2, x_mv2, x_ve2, x_rstd2 = (signal(n) for n in ("x_stat2", "x_mv2", "x_ve2", "x_rstd2"))
        y_in = signal("y_in")
        l_yb, l_ht, l_htc = signal("l_yb"), signal("l_ht"), signal("l_htc", 2)
        l_qkv = signal("l_qkv", 3)
        l_raw, l_sq, l_v, l_ss, l_ssc, l_rn = (signal(n) for n in ("l_raw", "l_sq", "l_v", "l_ss", "l_ssc", "l_rn"))
        l_t2, l_t1, l_add, l_rot = signal("l_t2", 2), signal("l_t1"), signal("l_add"), signal("l_rot")
        l_qkt, l_qktc = signal("l_qkt"), signal("l_qktc")
        l_s, l_max, l_sub, l_exp, l_pt, l_ptc, l_pv, l_rsum, l_o = (
            signal(n, HL // CH) for n in ("l_s", "l_max", "l_sub", "l_exp", "l_pt", "l_ptc", "l_pv", "l_rsum", "l_o"))
        l_ot, l_otc, l_wo = signal("l_ot"), signal("l_otc"), signal("l_wo")
        y_attn = signal("y_attn")
        f_yb, f_sh, f_stat, f_mv, f_ve, f_rstd = (signal(n) for n in ("f_yb", "f_sh", "f_stat", "f_mv", "f_ve", "f_rstd"))
        f_norm, f_t, f_tc, f_w1 = signal("f_norm", 2), signal("f_t"), signal("f_tc"), signal("f_w1", 2)
        f_gate, f_hid, f_w2 = signal("f_gate", NJ), signal("f_hid", NJ), signal("f_w2")

        def begin(eng, *signals):
            for s in signals:
                eng.sem_inc(s.sem, LEAD * s.per)

        def rows(j):
            return 128 if j < NJ - 1 else REST

        def bc(ap, shape):
            return ap.to_broadcast(shape)

        def settle(eng):
            eng.sem_inc(settled, 1)

        block = ctx.enter_context(nc.Block())

        consts = [(ident[:, :], ins["c_ident"]), (shiftm[:, :], ins["c_shift"]),
                  (sq[:, 0:128], ins["c_band"]), (ropex[:, :, :], ins["c_ropex"]), (ropel[:, :, :], ins["c_ropel"]),
                  (hmask[:, :], ins["c_hmask"])]
        N_CONST = len(consts) + 4
        N_WL, N_WF_IN = 2 + 6, 4 + 2 * NJ + 2
        N_SETUP = 7

        @block.sync
        def _(eng):
            for i, name in enumerate(("Wq", "Wk", "Wv", "Wo")):
                eng.dma_start(wx_in[:, i, :], ins["L0_xattn_" + name]).then_inc(wx_loaded, 16)
            for dst, src in consts:
                eng.dma_start(dst, src).then_inc(const_in, 16)
            for i, name in enumerate(("bq", "bk", "bv")):
                eng.dma_start(biasx[:, i * D:(i + 1) * D],
                              ins["L0_xattn_" + name].partition_broadcast(128)).then_inc(const_in, 16)
            eng.dma_start(box[:, :], ins["L0_xattn_bo"].partition_broadcast(128)).then_inc(const_in, 16)

            def load(t, p):
                eng.dma_start(x_all[:, bass.ds(t, 1), :], x[bass.ds(t, 1), :, :].rearrange("s t d -> t s d"))\
                   .then_inc(x_in[p], 16)
                eng.dma_start(ctxb[:, p:p + 1, :], ctx_in[bass.ds(t, 1), :, :].rearrange("s t d -> t s d"))\
                   .then_inc(ctx_in_sem[p], 16)
            load(0, 0)
            load(1, 1)
            with eng.Fori(1, NS // 2) as pair:
                for p in range(2):
                    t = 2 * pair + p
                    eng.wait_ge(x_in[p], 16 * pair)
                    settle(eng)
                    eng.wait_ge(ctx_in_sem[p], 16 * pair)
                    settle(eng)
                    eng.wait_ge(x_tr.sem, after(x_tr, t - 2))
                    settle(eng)
                    load(t, p)

            with eng.Fori(0, LAYERS) as layer:
                def of(name):
                    return ins["L0_ffn_" + name][bass.ds(layer, 1)]
                eng.wait_ge(l_qkv.sem, after(l_qkv, layer * NS - 1))
                settle(eng)
                eng.wait_ge(l_wo.sem, after(l_wo, layer * NS - 1))
                settle(eng)
                eng.wait_ge(tab_ready, layer * 4)
                settle(eng)
                eng.dma_start(wqkv[:, :], of("wqkv").rearrange("a d n -> d (a n)")).then_inc(wl_in, 16)
                eng.dma_start(wol[:, :, :], of("wo").rearrange("a (c p) n -> p (a c) n", p=128)).then_inc(wl_in, 16)
                H2 = DL // 2
                for i, name in ((0, "q_scale"), (2, "k_scale")):
                    row = of(name).rearrange("a d -> (a d)")
                    eng.dma_start(scales[:, i, :], row.partition_broadcast(128)).then_inc(wl_in, 16)
                    eng.dma_start(scales[:, i + 1, 0:H2], row[H2:DL].partition_broadcast(128)).then_inc(wl_in, 16)
                    eng.dma_start(scales[:, i + 1, H2:DL], row[0:H2].partition_broadcast(128)).then_inc(wl_in, 16)
                eng.wait_ge(f_w1.sem, after(f_w1, layer * NS - 1))
                settle(eng)
                eng.wait_ge(f_w2.sem, after(f_w2, layer * NS - 1))
                settle(eng)
                eng.wait_ge(f_hid.sem, after(f_hid, layer * NS - 1))
                settle(eng)
                eng.wait_ge(f_tc.sem, after(f_tc, layer * NS - 1))
                settle(eng)
                eng.dma_start(w1[:, :], of("w1").rearrange("a d n -> d (a n)")).then_inc(wf_in, 16)
                w2row = of("w2").rearrange("a k n -> (a k) n")
                eng.dma_start(w2[:, 0:NJ - 1, :], w2row[0:128 * (NJ - 1), :].rearrange("(j p) n -> p j n", p=128))\
                   .then_inc(wf_in, 16)
                eng.dma_start(w2[0:REST, NJ - 1, :], w2row[128 * (NJ - 1):HID, :]).then_inc(wf_in, 16)
                eng.dma_start(w2[REST:REST + 1, NJ - 1, :], of("b2")).then_inc(wf_in, 16)
                b1row = of("b1").rearrange("a n -> (a n)")
                for half in range(2):
                    for j in range(NJ):
                        lo = half * HID + 128 * j
                        eng.dma_start(b1[0:rows(j), half, j:j + 1],
                                      b1row[lo:lo + rows(j)].rearrange("(n a) -> n a", a=1)).then_inc(wf_in, 16)
                for i, name in enumerate(("ln_g", "ln_b")):
                    eng.dma_start(lgb[:, i:i + 1], of(name).rearrange("a d -> d a")).then_inc(wf_in, 16)

            OUT_CHUNKS = 4
            n = NS // OUT_CHUNKS
            for c in range(OUT_CHUNKS):
                eng.wait_ge(out_add, c + 1)
                eng.dma_start(out[c * n:(c + 1) * n, :, :].rearrange("s t d -> t s d"),
                              x_all[:, c * n:(c + 1) * n, :]).then_inc(out_done, 16)
            eng.wait_ge(out_done, 16 * OUT_CHUNKS)

        @block.tensor
        def _(eng):
            begin(eng, x_tr, x_proj, x_qkt, x_s, x_pt, x_pv, x_ot, x_wo,
                  l_ht, l_qkv, l_qkt, l_s, l_pt, l_pv, l_ot, l_wo, f_sh, f_t, f_w1, f_w2)
            eng.wait_ge(wx_loaded, 64)
            eng.wait_ge(const_in, 16 * N_CONST)
            for i in range(4):
                mm = eng.transpose(ps[:, 0, i * 128:(i + 1) * 128], wx_in[:, i, :], ident[:, :])
            mm.then_inc(setup_t, 1)
            eng.wait_ge(setup_e, 1)

            def step_x(t, p, active):
                p1, p2, p3 = (p - 1) % 2, (p - 2) % 2, (p - 3) % 2
                NC = HX // CH

                def tokens_T():
                    g = t - 1
                    eng.wait_ge(x_norm.sem, after(x_norm, g))
                    eng.wait_ge(ctx_in_sem[p1], 8 * (g - p1 + 2))
                    eng.wait_ge(x_trc.sem, after(x_trc, g - 1))
                    eng.transpose(ps[:, 0, 0:128], xn[:, p1, :], ident[:, :])
                    eng.transpose(ps[:, 0, 128:256], ctxb[:, p1, :], ident[:, :]).then_inc(x_tr.sem, 1)

                def project():
                    g = t - 1
                    eng.wait_ge(x_trc.sem, after(x_trc, g))
                    eng.wait_ge(x_bias.sem, after(x_bias, g - 1))
                    eng.matmul(ps[:, 1, 0:128], hT[:, p1, 0, :], wx[:, 0, :], start=True, stop=True)
                    eng.matmul(ps[:, 1, 128:384], hT[:, p1, 1, :], wx[:, 1:3, :].rearrange("p a b -> p (a b)"),
                               start=True, stop=True).then_inc(x_proj.sem, 1)

                def qk_T():
                    g = t - 2
                    eng.wait_ge(x_rot.sem, after(x_rot, g))
                    eng.wait_ge(x_kx.sem, after(x_kx, g - 1))
                    eng.wait_ge(x_qc.sem, after(x_qc, g - 1))
                    eng.transpose(ps[:, 2, 0:128], rot[:, p2, 0:128], ident[:, :])
                    eng.transpose(ps[:, 2, 128:256], rot[:, p2, 128:256], ident[:, :]).then_inc(x_qkt.sem, 1)

                def scores(c):
                    g = t - 2
                    if c == 0:
                        eng.wait_ge(x_qc.sem, after(x_qc, g))
                        eng.wait_ge(x_kx.sem, after(x_kx, g))
                    eng.wait_ge(x_sub.sem, after(x_sub, g - 1, c + 3))
                    eng.matmul(ps[:, 3 + c % 2, :], qkT[:, p2, 0:128],
                               kx[:, p2, c * CH:(c + 1) * CH, :].rearrange("p a b -> p (a b)"),
                               start=True, stop=True).then_inc(x_s.sem, 1)

                def prob_T(c):
                    g = t - 3
                    eng.wait_ge(x_exp.sem, after(x_exp, g, c + 1))
                    eng.wait_ge(x_ptc.sem, after(x_ptc, g - 1, c + 3))
                    for h in range(CH):
                        mm = eng.transpose(ps[:, 5 + c % 2, h * 128:(h + 1) * 128],
                                           prob[:, p3, c * CH + h, :], ident[:, :])
                    mm.then_inc(x_pt.sem, 1)

                def weigh(c):
                    g = t - 3
                    eng.wait_ge(x_ptc.sem, after(x_ptc, g, c + 1))
                    if c == 0:
                        eng.wait_ge(x_bias.sem, after(x_bias, g))
                        eng.wait_ge(x_res.sem, after(x_res, g - 1))
                    for h in range(c * CH, (c + 1) * CH):
                        mm = eng.matmul(ps[:, 7, h * (DX + 1):(h + 1) * (DX + 1)], probT[:, h, :],
                                        vx[:, p3, h, :], start=True, stop=True)
                    mm.then_inc(x_pv.sem, 1)

                def o_T():
                    g = t - 3
                    eng.wait_ge(x_o.sem, after(x_o, g))
                    eng.transpose(ps[:, 7, 256:384], o_sb[:, 0:128], ident[:, :]).then_inc(x_ot.sem, 1)

                def project_out():
                    g = t - 3
                    eng.wait_ge(x_otc.sem, after(x_otc, g))
                    eng.matmul(ps[:, 7, 384:512], oT[:, 0:128], wx[:, 3, :], start=True, stop=True)\
                       .then_inc(x_wo.sem, 1)

                if active(1):
                    tokens_T()
                if active(3):
                    prob_T(0)
                    prob_T(1)
                if active(2):
                    qk_T()
                if active(3):
                    weigh(0)
                    prob_T(2)
                if active(1):
                    project()
                if active(3):
                    weigh(1)
                    prob_T(3)
                if active(2):
                    scores(0)
                if active(3):
                    weigh(2)
                if active(2):
                    scores(1)
                if active(3):
                    weigh(3)
                    o_T()
                if active(2):
                    scores(2)
                if active(3):
                    project_out()
                if active(2):
                    scores(3)

            pipeline(eng, step_x, NS, LAGS_X)

            with eng.Fori(0, LAYERS) as layer:
                base = layer * NS

                def step_l(t, p, active):
                    p1, p2 = (p - 1) % 2, p

                    def tokens_T():
                        g = base + t
                        eng.wait_ge(l_yb.sem, after(l_yb, g))
                        eng.wait_ge(l_htc.sem, after(l_htc, g - 1))
                        eng.transpose(ps[:, 0, 0:128], yb[:, p, :], ident[:, :]).then_inc(l_ht.sem, 1)

                    def project():
                        g = base + t
                        eng.wait_ge(l_htc.sem, after(l_htc, g))
                        eng.wait_ge(l_raw.sem, after(l_raw, g - 1))
                        eng.wait_ge(l_sq.sem, after(l_sq, g - 1))
                        eng.wait_ge(l_v.sem, after(l_v, g - 1))
                        for c in range(3):
                            eng.matmul(ps[:, 1 + c, :], hT[:, p, 0, :], wqkv[:, c * INNER:(c + 1) * INNER],
                                       start=True, stop=True).then_inc(l_qkv.sem, 1)

                    def qk_T():
                        g = base + t - 1
                        eng.wait_ge(l_rot.sem, after(l_rot, g))
                        eng.wait_ge(l_sub.sem, after(l_sub, g - 1))
                        for b in range(2 * INNER // 128):
                            mm = eng.transpose(ps[:, 4 + b // 4, (b % 4) * 128:(b % 4 + 1) * 128],
                                               rot[:, p1, b * 128:(b + 1) * 128], ident[:, :])
                        mm.then_inc(l_qkt.sem, 1)

                    def scores():
                        g = base + t - 1
                        eng.wait_ge(l_qktc.sem, after(l_qktc, g))
                        for c in range(2):
                            eng.matmul(ps[:, 4 + c, :], identb[:, :], bandm[:, :], start=True, stop=True)
                        for h in range(HL):
                            r, c, s = DL * (h % 2), h % 2, h // 2
                            q = qkT[r:r + DL, p1, s * 128:(s + 1) * 128]
                            k = qkT[r:r + DL, p1, INNER + s * 128:INNER + (s + 1) * 128]
                            mm = eng.matmul(ps[:, 4 + c, s * 128:(s + 1) * 128], q, k,
                                            start=False, stop=True, skip_group_check=True)
                            if s == CH - 1:
                                mm.then_inc(l_s.sem, 1)

                    def prob_T(c):
                        g = base + t - 2
                        eng.wait_ge(l_exp.sem, after(l_exp, g, c + 1))
                        if c == 0:
                            eng.wait_ge(l_otc.sem, after(l_otc, g - 1))
                        else:
                            eng.wait_ge(y_attn.sem, after(y_attn, g - 1))
                        for h in range(c * CH, (c + 1) * CH):
                            mm = eng.transpose(ps[:, 6 + c, (h % CH) * 128:(h % CH + 1) * 128],
                                               prob[:, p2, h, :], ident[:, :])
                        mm.then_inc(l_pt.sem, 1)

                    def weigh(c):
                        g = base + t - 2
                        eng.wait_ge(l_ptc.sem, after(l_ptc, g, c + 1))
                        if c == 0:
                            eng.wait_ge(l_v.sem, after(l_v, g))
                        for s in range(CH):
                            mm = eng.matmul(ps[:, 6 + c, s * (DL + 1):(s + 1) * (DL + 1)],
                                            probT[:, c * CH + s, :], vl[:, p2, 2 * s + c, :], start=True, stop=True)
                        mm.then_inc(l_pv.sem, 1)

                    def o_T():
                        g = base + t - 2
                        eng.wait_ge(l_o.sem, after(l_o, g))
                        for b in range(INNER // 128):
                            mm = eng.transpose(ps[:, 6, b * 128:(b + 1) * 128],
                                               o_sb[:, b * 128:(b + 1) * 128], ident[:, :])
                        mm.then_inc(l_ot.sem, 1)

                    def project_out():
                        g = base + t - 2
                        eng.wait_ge(l_otc.sem, after(l_otc, g))
                        NB = INNER // 128
                        for b in range(NB):
                            mm = eng.matmul(ps[:, 7, 0:128], oT[:, b * 128:(b + 1) * 128], wol[:, b, :],
                                            start=(b == 0), stop=(b == NB - 1))
                        mm.then_inc(l_wo.sem, 1)

                    if active(0):
                        tokens_T()
                    if active(2):
                        prob_T(0)
                        prob_T(1)
                    if active(0):
                        project()
                    if active(2):
                        weigh(0)
                    if active(1):
                        qk_T()
                    if active(2):
                        weigh(1)
                        o_T()
                    if active(1):
                        scores()
                    if active(2):
                        project_out()

                eng.wait_ge(wl_in, (layer + 1) * (16 * N_WL))
                eng.wait_ge(setup_v, N_SETUP)
                pipeline(eng, step_l, NS, LAGS_L)

                def step_f(t, p, active):
                    p1, p2 = (p - 1) % 2, p

                    def shift():
                        g = base + t
                        eng.wait_ge(f_yb.sem, after(f_yb, g))
                        eng.wait_ge(f_norm.sem, after(f_norm, g - 2))
                        eng.matmul(ps[:, 5 * p, 0:D // 2], shiftm[:, :], yb[:, p, D // 2:D], start=True, stop=True)\
                           .then_inc(f_sh.sem, 1)

                    def tokens_T():
                        g = base + t - 1
                        eng.wait_ge(f_norm.sem, after(f_norm, g))
                        eng.wait_ge(f_tc.sem, after(f_tc, g - 1))
                        eng.transpose(ps[:, 1, 0:128], xn[:, p1, :], ident[:, :]).then_inc(f_t.sem, 1)

                    def expand():
                        g = base + t - 1
                        eng.wait_ge(f_tc.sem, after(f_tc, g))
                        eng.wait_ge(f_hid.sem, after(f_hid, g - 2))
                        for half, b in ((1, 3), (0, 2)):
                            for j in range(NJ):
                                lo = half * HID + 128 * j
                                mm = eng.matmul(ps[0:rows(j), b + 4 * p1 - (p1 and 0), j * 128:(j + 1) * 128],
                                                w1[:, lo:lo + rows(j)], hT[:, p1, 0, :], start=True, stop=True)
                            mm.then_inc(f_w1.sem, 1)

                    def contract():
                        g = base + t - 2
                        eng.wait_ge(f_hid.sem, after(f_hid, g))
                        eng.wait_ge(y_in.sem, after(y_in, base + NS + t - 3))
                        for j in range(NJ):
                            k = rows(j) + (j == NJ - 1)
                            mm = eng.matmul(ps[:, 4, 0:128], hid[0:k, p2, j, :], w2[0:k, j, :],
                                            start=(j == 0), stop=(j == NJ - 1))
                        mm.then_inc(f_w2.sem, 1)

                    if active(1):
                        tokens_T()
                    if active(0):
                        shift()
                    if active(2):
                        contract()
                    if active(1):
                        expand()

                eng.wait_ge(wf_in, (layer + 1) * (16 * N_WF_IN))
                pipeline(eng, step_f, NS, LAGS_F)

        @block.scalar
        def _(eng):
            begin(eng, x_trc, x_qc, x_exp, x_ptc, x_otc, l_htc, l_raw, l_sq, l_v, l_qktc, l_exp, l_ptc, l_otc,
                  f_tc, f_gate)
            eng.wait_ge(setup_t, 1)
            eng.activation(wx[:, :, :].rearrange("p a b -> p (a b)"), ps[:, 0, :], ACT.Copy).then_inc(setup_e, 1)

            def step_x(t, p, active):
                p1, p2, p3 = (p - 1) % 2, (p - 2) % 2, (p - 3) % 2

                def tokens_T():
                    g = t - 1
                    eng.wait_ge(x_tr.sem, after(x_tr, g))
                    eng.wait_ge(x_proj.sem, after(x_proj, g - 2))
                    eng.activation(hT[:, p1, :, :].rearrange("p a b -> p (a b)"), ps[:, 0, 0:256], ACT.Copy)\
                       .then_inc(x_trc.sem, 1)

                def q_T():
                    g = t - 2
                    eng.wait_ge(x_qkt.sem, after(x_qkt, g))
                    eng.wait_ge(x_kx.sem, after(x_kx, g))
                    eng.wait_ge(x_s.sem, after(x_s, g - 2))
                    eng.activation(qkT[:, p2, 0:128], ps[:, 2, 0:128], ACT.Copy).then_inc(x_qc.sem, 1)

                def exps(c):
                    g = t - 2
                    eng.wait_ge(x_sub.sem, after(x_sub, g, c + 1))
                    s = prob[:, p2, c * CH:(c + 1) * CH, :].rearrange("p a b -> p (a b)")
                    eng.activation(s, s, ACT.Exp, scale=SCALE_X).then_inc(x_exp.sem, 1)

                def prob_T(c):
                    g = t - 3
                    eng.wait_ge(x_pt.sem, after(x_pt, g, c + 1))
                    eng.wait_ge(x_pv.sem, after(x_pv, g - 1, c + 1))
                    eng.activation(probT[:, c * CH:(c + 1) * CH, :].rearrange("p a b -> p (a b)"),
                                   ps[:, 5 + c % 2, :], ACT.Copy).then_inc(x_ptc.sem, 1)

                def o_T():
                    g = t - 3
                    eng.wait_ge(x_ot.sem, after(x_ot, g))
                    eng.wait_ge(x_wo.sem, after(x_wo, g - 1))
                    eng.activation(oT[:, 0:128], ps[:, 7, 256:384], ACT.Copy).then_inc(x_otc.sem, 1)

                if active(1):
                    tokens_T()
                if active(3):
                    prob_T(0)
                    prob_T(1)
                if active(2):
                    q_T()
                if active(3):
                    prob_T(2)
                    prob_T(3)
                if active(2):
                    exps(0)
                    exps(1)
                if active(3):
                    o_T()
                if active(2):
                    exps(2)
                    exps(3)

            pipeline(eng, step_x, NS, LAGS_X)

            with eng.Fori(0, LAYERS) as layer:
                base = layer * NS

                def step_l(t, p, active):
                    p1, p2 = (p - 1) % 2, p

                    def tokens_T():
                        g = base + t
                        eng.wait_ge(l_ht.sem, after(l_ht, g))
                        eng.wait_ge(l_qkv.sem, after(l_qkv, g - 2))
                        H = D // 2
                        eng.activation(hT[0:H, p, 0, :], ps[0:H, 0, 0:128], ACT.Copy).then_inc(l_htc.sem, 1)
                        eng.activation(hT[H:D, p, 0, 1:128], ps[H:D, 0, 0:127], ACT.Copy).then_inc(l_htc.sem, 1)

                    def prob_T(c):
                        g = base + t - 2
                        eng.wait_ge(l_pt.sem, after(l_pt, g, c + 1))
                        eng.wait_ge(l_pv.sem, after(l_pv, g - 1, c + 1))
                        eng.activation(probT[:, c * CH:(c + 1) * CH, :].rearrange("p a b -> p (a b)"),
                                       ps[:, 6 + c, :], ACT.Copy).then_inc(l_ptc.sem, 1)

                    def qkv():
                        g = base + t
                        qk = ps[:, 1:3, :].rearrange("p a b -> p (a b)")
                        eng.wait_ge(l_qkv.sem, after(l_qkv, g, 2))
                        eng.wait_ge(l_t1.sem, after(l_t1, g - 2))
                        eng.wait_ge(l_t2.sem, after(l_t2, g - 2))
                        eng.activation(raw[:, p, :, :].rearrange("p a b -> p (a b)"), qk, ACT.Copy)\
                           .then_inc(l_raw.sem, 1)
                        eng.wait_ge(l_ss.sem, after(l_ss, g - 1))
                        eng.activation(sq[:, :], qk, ACT.Square).then_inc(l_sq.sem, 1)
                        eng.wait_ge(l_qkv.sem, after(l_qkv, g, 3))
                        eng.wait_ge(l_pv.sem, after(l_pv, g - 2))
                        eng.activation(vl[:, p, :, 0:DL], ps[:, 3, :].rearrange("p (h d) -> p h d", d=DL), ACT.Copy)\
                           .then_inc(l_v.sem, 1)

                    def qk_T():
                        g = base + t - 1
                        eng.wait_ge(l_qkt.sem, after(l_qkt, g))
                        eng.wait_ge(l_s.sem, after(l_s, g - 2))
                        eng.activation(qkT[:, p1, :], ps[:, 4:6, :].rearrange("p a b -> p (a b)"), ACT.Copy)\
                           .then_inc(l_qktc.sem, 1)

                    def exps(c):
                        g = base + t - 1
                        eng.wait_ge(l_sub.sem, after(l_sub, g, c + 1))
                        s = prob[:, p1, c * CH:(c + 1) * CH, :].rearrange("p a b -> p (a b)")
                        eng.activation(s, s, ACT.Exp, scale=SCALE_L).then_inc(l_exp.sem, 1)

                    def o_T():
                        g = base + t - 2
                        eng.wait_ge(l_ot.sem, after(l_ot, g))
                        eng.wait_ge(l_wo.sem, after(l_wo, g - 1))
                        eng.activation(oT[:, :], ps[:, 6, :], ACT.Copy).then_inc(l_otc.sem, 1)

                    if active(0):
                        tokens_T()
                    if active(2):
                        prob_T(0)
                        prob_T(1)
                    if active(0):
                        qkv()
                    if active(1):
                        qk_T()
                    if active(2):
                        o_T()
                    if active(1):
                        exps(0)
                        exps(1)

                eng.wait_ge(shift_zero, layer + 1)
                pipeline(eng, step_l, NS, LAGS_L)

                def step_f(t, p, active):
                    p1 = (p - 1) % 2

                    def tokens_T():
                        g = base + t - 1
                        eng.wait_ge(f_t.sem, after(f_t, g))
                        eng.wait_ge(f_w1.sem, after(f_w1, g - 2))
                        eng.activation(hT[:, p1, 0, :], ps[:, 1, 0:128], ACT.Identity, scale=lgb[:, 0:1],
                                       bias=lgb[:, 1:2]).then_inc(f_tc.sem, 1)

                    def gates():
                        g = base + t - 1
                        eng.wait_ge(f_w1.sem, after(f_w1, g, 1))
                        eng.wait_ge(f_hid.sem, after(f_hid, g - 2))
                        for j in range(NJ):
                            eng.activation(gate[0:rows(j), p1, j, :], ps[0:rows(j), 3 + 4 * p1, j * 128:(j + 1) * 128],
                                           ACT.Gelu, bias=b1[0:rows(j), 1, j:j + 1]).then_inc(f_gate.sem, 1)

                    if active(1):
                        tokens_T()
                        gates()

                eng.wait_ge(wf_in, (layer + 1) * (16 * N_WF_IN))
                pipeline(eng, step_f, NS, LAGS_F)

        @block.vector
        def _(eng):
            begin(eng, x_stat, x_mv, x_ve, x_norm, x_bias, x_rot, x_kx, x_max, x_sub, x_rsum, x_o, x_res,
                  x_stat2, x_mv2, x_ve2, y_in, l_ss, l_t1, l_add, l_rot, l_max, l_sub, l_rsum, l_o, y_attn,
                  f_stat, f_mv, f_ve, f_norm, f_hid)
            eng.memset(nhalf[:, :], -0.5).then_inc(setup_v, 1)
            eng.memset(vx[:, :, :, :], 1.0).then_inc(setup_v, 1)
            eng.memset(vl[:, :, :, :], 1.0).then_inc(setup_v, 1)
            eng.memset(hid[:, :, :, :], 1.0).then_inc(setup_v, 1)
            eng.memset(rot[:, :, :], 0.0).then_inc(setup_v, 1)
            eng.wait_ge(const_in, 16 * N_CONST)
            eng.tensor_copy(identb[:, :], ident[:, :]).then_inc(setup_v, 1)
            eng.tensor_copy(bandm[:, :].rearrange("p (a b) -> p a b", a=CH),
                            bc(sq[:, 0:128].unsqueeze(1), [128, CH, 128])).then_inc(setup_v, 1)
            eng.wait_ge(setup_v, N_SETUP)

            def step_x(t, p, active):
                p1, p2, p3 = (p - 1) % 2, (p - 2) % 2, (p - 3) % 2

                def stats():
                    g = t
                    eng.wait_ge(x_in[p], 8 * (g - p + 2))
                    settle(eng)
                    eng.bn_stats(st[:, p, 0, :], x_all[:, bass.ds(t, 1), :]).then_inc(x_stat.sem, 1)
                    eng.wait_ge(x_stat.sem, after(x_stat, g))
                    settle(eng)
                    eng.bn_aggr(mv[:, p, :], st[:, p, 0, :]).then_inc(x_mv.sem, 1)
                    eng.wait_ge(x_mv.sem, after(x_mv, g))
                    eng.wait_ge(x_rstd.sem, after(x_rstd, g - 2))
                    eng.tensor_scalar(ve[:, p, :], mv[:, p, 1:2], EPS, None, ALU.add).then_inc(x_ve.sem, 1)

                def normalise():
                    g = t - 1
                    eng.wait_ge(x_rstd.sem, after(x_rstd, g))
                    eng.wait_ge(x_tr.sem, after(x_tr, g - 2))
                    eng.tensor_scalar(xn[:, p1, :].unsqueeze(1), x_all[:, bass.ds(t - 1, 1), :], mv[:, p1, 0:1],
                                      rstd[:, p1, :], ALU.subtract, ALU.mult).then_inc(x_norm.sem, 1)

                def bias():
                    g = t - 1
                    eng.wait_ge(x_proj.sem, after(x_proj, g))
                    eng.wait_ge(x_t.sem, after(x_t, g - 1))
                    eng.wait_ge(x_pv.sem, after(x_pv, g - 2))
                    eng.tensor_tensor(raw[:, 0, 0, 0:256], ps[:, 1, 0:256], biasx[:, 0:256], ALU.add)\
                       .then_inc(x_bias.sem, 1)
                    eng.tensor_tensor(vx[:, p1, :, 0:DX], ps[:, 1, 256:384].rearrange("p (h d) -> p h d", d=DX),
                                      biasx[:, 256:384].rearrange("p (h d) -> p h d", d=DX), ALU.add)\
                       .then_inc(x_bias.sem, 1)

                def rotate():
                    g = t - 2
                    eng.wait_ge(x_t.sem, after(x_t, g))
                    eng.wait_ge(x_qkt.sem, after(x_qkt, g - 2))
                    eng.tensor_tensor(rot[:, p2, 0:256], t1[:, p2, 0, 0:256], t2[:, p2, 0, 0:256], ALU.add)\
                       .then_inc(x_rot.sem, 1)

                def spread_k():
                    g = t - 2
                    eng.wait_ge(x_qkt.sem, after(x_qkt, g))
                    eng.wait_ge(x_s.sem, after(x_s, g - 2))
                    eng.tensor_tensor(kx[:, p2, :, :], bc(ps[:, 2, 128:256].unsqueeze(1), [128, HX, 128]),
                                      bc(hmask[:, :].unsqueeze(2), [128, HX, 128]), ALU.mult).then_inc(x_kx.sem, 1)

                def softmax(c):
                    g = t - 2
                    s = ps[:, 3 + c % 2, :].rearrange("p (h k) -> p h k", k=128)
                    m = top[:, p2, c * CH:(c + 1) * CH]
                    eng.wait_ge(x_s.sem, after(x_s, g, c + 1))
                    eng.tensor_reduce(m, s, AX.X, ALU.max).then_inc(x_max.sem, 1)
                    eng.wait_ge(x_max.sem, after(x_max, g, c + 1))
                    eng.wait_ge(x_pt.sem, after(x_pt, g - 2, c + 1))
                    eng.tensor_tensor(prob[:, p2, c * CH:(c + 1) * CH, :], s, bc(m.unsqueeze(2), [128, CH, 128]),
                                      ALU.subtract).then_inc(x_sub.sem, 1)

                def o_norm():
                    g = t - 3
                    o = ps[:, 7, 0:HX * (DX + 1)].rearrange("p (h d) -> p h d", d=DX + 1)
                    eng.wait_ge(x_pv.sem, after(x_pv, g))
                    eng.reciprocal(rsum[:, :].unsqueeze(2), o[:, :, DX:DX + 1]).then_inc(x_rsum.sem, 1)
                    eng.wait_ge(x_rsum.sem, after(x_rsum, g))
                    eng.wait_ge(x_ot.sem, after(x_ot, g - 1))
                    eng.tensor_tensor(o_sb[:, 0:128].rearrange("p (h d) -> p h d", d=DX), o[:, :, 0:DX],
                                      bc(rsum[:, :].unsqueeze(2), [128, HX, DX]), ALU.mult).then_inc(x_o.sem, 1)

                def residual():
                    g = t - 3
                    eng.wait_ge(x_wo.sem, after(x_wo, g))
                    eng.wait_ge(x_bo.sem, after(x_bo, g))
                    xi = x_all[:, bass.ds(t - 3, 1), :]
                    eng.tensor_tensor(xi, ps[:, 7, 384:512].unsqueeze(1), xi, ALU.add).then_inc(x_res.sem, 1)
                    eng.wait_ge(x_res.sem, after(x_res, g))
                    settle(eng)
                    eng.bn_stats(st2[:, p3, :], xi).then_inc(x_stat2.sem, 1)
                    eng.wait_ge(x_stat2.sem, after(x_stat2, g))
                    settle(eng)
                    eng.bn_aggr(mv2[:, p3, :], st2[:, p3, :]).then_inc(x_mv2.sem, 1)
                    eng.wait_ge(x_mv2.sem, after(x_mv2, g))
                    eng.wait_ge(x_rstd2.sem, after(x_rstd2, g - 2))
                    eng.tensor_scalar(ve2[:, p3, :], mv2[:, p3, 1:2], EPS, None, ALU.add).then_inc(x_ve2.sem, 1)

                def normalise_y():
                    g = t - 4
                    eng.wait_ge(x_rstd2.sem, after(x_rstd2, g))
                    eng.tensor_scalar(y_all[:, bass.ds(t - 4, 1), :], x_all[:, bass.ds(t - 4, 1), :],
                                      mv2[:, p, 0:1], rstd2[:, p, :], ALU.subtract, ALU.mult).then_inc(y_in.sem, 1)

                if active(1):
                    normalise()
                if active(2):
                    rotate()
                    spread_k()
                if active(0):
                    stats()
                if active(1):
                    bias()
                if active(2):
                    softmax(0)
                    softmax(1)
                if active(3):
                    o_norm()
                if active(4):
                    normalise_y()
                if active(2):
                    softmax(2)
                if active(3):
                    residual()
                if active(2):
                    softmax(3)

            pipeline(eng, step_x, NS, LAGS_X)

            with eng.Fori(0, LAYERS) as layer:
                base = layer * NS
                eng.memset(hT[:, :, 0, 0:1], 0.0).then_inc(shift_zero, 1)
                eng.wait_ge(wl_in, (layer + 1) * (16 * N_WL))
                eng.wait_ge(l_t2.sem, after(l_t2, base - 1))
                for i, j in ((0, 0), (1, 1), (2, 2), (3, 3)):
                    eng.tensor_tensor(tab[:, i, :], ropel[:, i, :], scales[:, j, :], ALU.mult).then_inc(tab_ready, 1)
                eng.wait_ge(tab_ready, (layer + 1) * 4)

                def step_l(t, p, active):
                    p1, p2 = (p - 1) % 2, p

                    def rotate():
                        g = base + t - 1
                        eng.wait_ge(l_raw.sem, after(l_raw, g))
                        r = raw[:, p1, :, :].rearrange("p a (h d) -> p a h d", d=DL)
                        cosb = bc(tab[:, 0:4:2, :].unsqueeze(2), [128, 2, HL, DL])
                        u = t1[:, 0, :, :].rearrange("p a (h d) -> p a h d", d=DL)
                        eng.tensor_tensor(u, r, cosb, ALU.mult).then_inc(l_t1.sem, 1)
                        eng.wait_ge(l_t1.sem, after(l_t1, g))
                        eng.wait_ge(l_t2.sem, after(l_t2, g))
                        flat = t1[:, 0, :, :].rearrange("p a b -> p (a b)")
                        eng.tensor_tensor(flat, flat, t2[:, p1, :, :].rearrange("p a b -> p (a b)"), ALU.add)\
                           .then_inc(l_add.sem, 1)
                        eng.wait_ge(l_add.sem, after(l_add, g))
                        eng.wait_ge(l_rn.sem, after(l_rn, g))
                        eng.wait_ge(l_qkt.sem, after(l_qkt, g - 2))
                        eng.tensor_tensor(rot[:, p1, :].rearrange("p (h d) -> p h d", d=DL),
                                          flat.rearrange("p (h d) -> p h d", d=DL),
                                          bc(rn[:, p1, :].unsqueeze(2), [128, 2 * HL, DL]), ALU.mult)\
                           .then_inc(l_rot.sem, 1)

                    def squares():
                        g = base + t
                        eng.wait_ge(l_sq.sem, after(l_sq, g))
                        eng.wait_ge(l_ssc.sem, after(l_ssc, g - 2))
                        eng.tensor_reduce(ss[:, p, :], sq[:, :].rearrange("p (h d) -> p h d", d=DL), AX.X, ALU.add)\
                           .then_inc(l_ss.sem, 1)

                    def softmax(c):
                        g = base + t - 1
                        s = ps[:, 4 + c, :].rearrange("p (h k) -> p h k", k=128)
                        m = top[:, p1, c * CH:(c + 1) * CH]
                        eng.wait_ge(l_s.sem, after(l_s, g, c + 1))
                        eng.tensor_reduce(m, s, AX.X, ALU.max).then_inc(l_max.sem, 1)
                        eng.wait_ge(l_max.sem, after(l_max, g, c + 1))
                        eng.wait_ge(l_pt.sem, after(l_pt, g - 2, c + 1))
                        eng.tensor_tensor(prob[:, p1, c * CH:(c + 1) * CH, :], s, bc(m.unsqueeze(2), [128, CH, 128]),
                                          ALU.subtract).then_inc(l_sub.sem, 1)

                    def o_norm(c):
                        g = base + t - 2
                        o = ps[:, 6 + c, 0:CH * (DL + 1)].rearrange("p (h d) -> p h d", d=DL + 1)
                        rs = rsum[:, c * CH:(c + 1) * CH].unsqueeze(2)
                        eng.wait_ge(l_pv.sem, after(l_pv, g, c + 1))
                        eng.reciprocal(rs, o[:, :, DL:DL + 1]).then_inc(l_rsum.sem, 1)
                        eng.wait_ge(l_rsum.sem, after(l_rsum, g, c + 1))
                        eng.wait_ge(l_ot.sem, after(l_ot, g - 1))
                        eng.tensor_tensor(o_sb[:, :].rearrange("p (s c d) -> p c s d", c=2, d=DL)[:, c, :, :],
                                          o[:, :, 0:DL], bc(rs, [128, CH, DL]), ALU.mult).then_inc(l_o.sem, 1)

                    def residual():
                        g = base + t - 2
                        yi = y_all[:, bass.ds(t - 2, 1), :]
                        eng.wait_ge(l_wo.sem, after(l_wo, g))
                        eng.wait_ge(l_yb.sem, after(l_yb, g))
                        eng.tensor_tensor(yi, ps[:, 7, 0:128].unsqueeze(1), yi, ALU.add).then_inc(y_attn.sem, 1)

                    if active(1):
                        rotate()
                    if active(2):
                        o_norm(0)
                        o_norm(1)
                    if active(0):
                        squares()
                    if active(1):
                        softmax(0)
                    if active(2):
                        residual()
                    if active(1):
                        softmax(1)

                pipeline(eng, step_l, NS, LAGS_L)

                def step_f(t, p, active):
                    p1, p2 = (p - 1) % 2, p
                    H = D // 2

                    def stats():
                        g = base + t
                        eng.wait_ge(f_sh.sem, after(f_sh, g))
                        settle(eng)
                        eng.bn_stats(st[:, p, 0, :], yb[:, p, 0:H])
                        eng.bn_stats(st[:, p, 1, :], ps[:, 5 * p, 0:H]).then_inc(f_stat.sem, 1)
                        eng.wait_ge(f_stat.sem, after(f_stat, g))
                        settle(eng)
                        eng.bn_aggr(mv[:, p, :], st[:, p, :, :].rearrange("p a b -> p (a b)")).then_inc(f_mv.sem, 1)
                        eng.wait_ge(f_mv.sem, after(f_mv, g))
                        eng.wait_ge(f_rstd.sem, after(f_rstd, g - 2))
                        eng.tensor_scalar(ve[:, p, :], mv[:, p, 1:2], EPS, None, ALU.add).then_inc(f_ve.sem, 1)

                    def normalise():
                        g = base + t - 1
                        eng.wait_ge(f_rstd.sem, after(f_rstd, g))
                        eng.wait_ge(f_t.sem, after(f_t, g - 2))
                        eng.tensor_scalar(xn[:, p1, 0:H], yb[:, p1, 0:H], mv[:, p1, 0:1], rstd[:, p1, :],
                                          ALU.subtract, ALU.mult).then_inc(f_norm.sem, 1)
                        eng.tensor_scalar(xn[:, p1, H:D], ps[:, 5 * p1, 0:H], mv[:, p1, 0:1], rstd[:, p1, :],
                                          ALU.subtract, ALU.mult).then_inc(f_norm.sem, 1)

                    def gated():
                        g = base + t - 1
                        eng.wait_ge(f_w1.sem, after(f_w1, g))
                        eng.wait_ge(f_w2.sem, after(f_w2, g - 2))
                        for j in range(NJ):
                            n = rows(j)
                            eng.wait_ge(f_gate.sem, after(f_gate, g, j + 1))
                            eng.scalar_tensor_tensor(hid[0:n, p1, j, :], ps[0:n, 2 + 4 * p1, j * 128:(j + 1) * 128],
                                                     b1[0:n, 0, j:j + 1], gate[0:n, p1, j, :], ALU.add, ALU.mult)\
                               .then_inc(f_hid.sem, 1)

                    def residual():
                        g = base + t - 2
                        yi = y_all[:, bass.ds(t - 2, 1), :]
                        eng.wait_ge(f_w2.sem, after(f_w2, g))
                        eng.wait_ge(f_yb.sem, after(f_yb, g))
                        eng.tensor_tensor(yi, ps[:, 4, 0:128].unsqueeze(1), yi, ALU.add).then_inc(y_in.sem, 1)

                    if active(1):
                        normalise()
                    if active(0):
                        stats()
                    if active(2):
                        residual()
                    if active(1):
                        gated()

                eng.wait_ge(wf_in, (layer + 1) * (16 * N_WF_IN))
                pipeline(eng, step_f, NS, LAGS_F)

            n = NS // 4
            eng.wait_ge(y_in.sem, after(y_in, (LAYERS + 1) * NS - 1))
            for c in range(4):
                part = x_all[:, c * n:(c + 1) * n, :]
                eng.tensor_tensor(part, part, y_all[:, c * n:(c + 1) * n, :], ALU.add).then_inc(out_add, 1)

        @block.gpsimd
        def _(eng):
            begin(eng, x_rstd, x_t, x_bo, x_rstd2, l_yb, l_ssc, l_rn, l_t2, f_yb, f_rstd)
            eng.wait_ge(setup_v, N_SETUP)
            eng.wait_ge(const_in, 16 * N_CONST)

            def step_x(t, p, active):
                p1, p2, p3 = (p - 1) % 2, (p - 2) % 2, (p - 3) % 2

                def inv_std():
                    g = t
                    eng.wait_ge(x_ve.sem, after(x_ve, g))
                    eng.wait_ge(x_norm.sem, after(x_norm, g - 2))
                    eng.tensor_tensor(rstd[:, p, :], ve[:, p, :], nhalf[:, 0:1], ALU.pow).then_inc(x_rstd.sem, 1)

                def rotary():
                    g = t - 1
                    eng.wait_ge(x_bias.sem, after(x_bias, g))
                    eng.wait_ge(x_rot.sem, after(x_rot, g - 2))
                    r = raw[:, 0, 0, 0:256].rearrange("p (h d) -> p h d", d=DX)
                    a = t1[:, p1, 0, 0:256].rearrange("p (h d) -> p h d", d=DX)
                    b = t2[:, p1, 0, 0:256].rearrange("p (h d) -> p h d", d=DX)
                    H2, NH = DX // 2, 2 * HX
                    eng.tensor_tensor(a, r, bc(ropex[:, 0:1, :], [128, NH, DX]), ALU.mult).then_inc(x_t.sem, 1)
                    eng.tensor_tensor(b[:, :, 0:H2], r[:, :, H2:DX], bc(ropex[:, 1:2, 0:H2], [128, NH, H2]),
                                      ALU.mult).then_inc(x_t.sem, 1)
                    eng.tensor_tensor(b[:, :, H2:DX], r[:, :, 0:H2], bc(ropex[:, 1:2, H2:DX], [128, NH, H2]),
                                      ALU.mult).then_inc(x_t.sem, 1)

                def add_bo():
                    g = t - 2
                    xi = x_all[:, bass.ds(t - 2, 1), :]
                    eng.wait_ge(x_norm.sem, after(x_norm, g))
                    eng.tensor_tensor(xi, xi, box[:, :].unsqueeze(1), ALU.add).then_inc(x_bo.sem, 1)

                def inv_std2():
                    g = t - 3
                    eng.wait_ge(x_ve2.sem, after(x_ve2, g))
                    eng.wait_ge(y_in.sem, after(y_in, g - 2))
                    eng.tensor_tensor(rstd2[:, p3, :], ve2[:, p3, :], nhalf[:, 0:1], ALU.pow).then_inc(x_rstd2.sem, 1)

                if active(2):
                    add_bo()
                if active(0):
                    inv_std()
                if active(1):
                    rotary()
                if active(3):
                    inv_std2()

            pipeline(eng, step_x, NS, LAGS_X)

            with eng.Fori(0, LAYERS) as layer:
                base = layer * NS

                def step_l(t, p, active):
                    def copy_y():
                        g = base + t
                        eng.wait_ge(y_in.sem, after(y_in, g))
                        eng.wait_ge(l_ht.sem, after(l_ht, g - 2))
                        settle(eng)
                        eng.tensor_copy(yb[:, p:p + 1, :], y_all[:, bass.ds(t, 1), :]).then_inc(l_yb.sem, 1)

                    def rotary():
                        g = base + t
                        H2 = DL // 2
                        eng.wait_ge(l_raw.sem, after(l_raw, g))
                        eng.wait_ge(l_add.sem, after(l_add, g - 2))
                        r = raw[:, p, :, :].rearrange("p a (h d) -> p a h d", d=DL)
                        b = t2[:, p, :, :].rearrange("p a (h d) -> p a h d", d=DL)
                        for dst, src in ((slice(0, H2), slice(H2, DL)), (slice(H2, DL), slice(0, H2))):
                            eng.tensor_tensor(b[:, :, :, dst], r[:, :, :, src],
                                              bc(tab[:, 1:4:2, dst].unsqueeze(2), [128, 2, HL, H2]), ALU.mult)\
                               .then_inc(l_t2.sem, 1)

                    def inv_norm():
                        g = base + t
                        eng.wait_ge(l_ss.sem, after(l_ss, g))
                        settle(eng)
                        eng.tensor_scalar(ssc[:, :], ss[:, p, :], 1e-24, 1.0, ALU.max, ALU.mult).then_inc(l_ssc.sem, 1)
                        eng.wait_ge(l_ssc.sem, after(l_ssc, g))
                        eng.wait_ge(l_rot.sem, after(l_rot, g - 2))
                        eng.tensor_tensor(rn[:, p, :], ssc[:, :], nhalf[:, :], ALU.pow).then_inc(l_rn.sem, 1)

                    if active(0):
                        copy_y()
                        rotary()
                        inv_norm()

                eng.wait_ge(tab_ready, (layer + 1) * 4)
                pipeline(eng, step_l, NS, LAGS_L)

                def step_f(t, p, active):
                    def copy_y():
                        g = base + t
                        eng.wait_ge(y_attn.sem, after(y_attn, g))
                        eng.wait_ge(f_norm.sem, after(f_norm, g - 2))
                        eng.wait_ge(f_sh.sem, after(f_sh, g - 2))
                        settle(eng)
                        eng.tensor_copy(yb[:, p:p + 1, :], y_all[:, bass.ds(t, 1), :]).then_inc(f_yb.sem, 1)

                    def inv_std():
                        g = base + t
                        eng.wait_ge(f_ve.sem, after(f_ve, g))
                        eng.wait_ge(f_norm.sem, after(f_norm, g - 2))
                        eng.tensor_tensor(rstd[:, p, :], ve[:, p, :], nhalf[:, 0:1], ALU.pow).then_inc(f_rstd.sem, 1)

                    if active(0):
                        copy_y()
                        inv_std()

                pipeline(eng, step_f, NS, LAGS_F)


_INS = ["x", "ctx_1024", "L0_xattn_Wq", "L0_xattn_bq", "L0_xattn_Wk", "L0_xattn_bk", "L0_xattn_Wv", "L0_xattn_bv",
        "L0_xattn_Wo", "L0_xattn_bo", "L0_ffn_wqkv", "L0_ffn_q_scale", "L0_ffn_k_scale", "L0_ffn_wo", "L0_ffn_ln_g",
        "L0_ffn_ln_b", "L0_ffn_w1", "L0_ffn_b1", "L0_ffn_w2", "L0_ffn_b2"]


def constants(T, DX, HX, DL):
    import numpy as np

    f = np.float32
    ident = np.eye(128, dtype=f)
    shift = np.eye(128, k=1, dtype=f)
    i, j = np.arange(T)[:, None], np.arange(T)[None, :]
    band = np.where((i < j) | (i > j + 64), f(-1e30), f(0))
    t = np.arange(T, dtype=f)
    inv = (f(1.0) / f(10000.0) ** (np.arange(0, DX, 2, dtype=f) / f(DX))).astype(f)
    ang = t[:, None] * inv[None, :]
    ang = np.concatenate([ang, ang], axis=-1).astype(f)
    sign = np.concatenate([-np.ones(DX // 2, f), np.ones(DX // 2, f)])
    ropex = np.stack([np.cos(ang), np.sin(ang) * sign], axis=1)
    half = np.arange(0, DL, 2, dtype=f)
    inv = (f(1.0) / f(10000.0) ** (half / f(DL))).astype(f)
    ang = t[:, None] * inv[None, :]
    ang = np.concatenate([ang, ang], axis=-1).astype(f)
    base = (half + f(0.4 * DL)) / f(1.4 * DL)
    power = (t - f(T // 2)) / f(32.0)
    scale = (base[None, :] ** power[:, None]).astype(f)
    scale = np.concatenate([scale, scale], axis=-1)
    sign = np.concatenate([-np.ones(DL // 2, f), np.ones(DL // 2, f)])
    cos, sin = np.cos(ang), np.sin(ang) * sign
    ropel = np.stack([cos * scale, sin * scale, cos / scale, sin / scale], axis=1)
    hmask = (np.arange(128)[:, None] // DX == np.arange(HX)[None, :]).astype(f)
    return {"c_ident": ident, "c_shift": shift, "c_band": band, "c_ropex": ropex.astype(f),
            "c_ropel": ropel.astype(f), "c_hmask": hmask}


def kernel(**inputs):
    import numpy as np
    import concourse.bacc as bacc
    from concourse.bass_utils import run_bass_kernel_spmd

    nc = bacc.Bacc("TRN2", target_bir_lowering=False, num_devices=1)
    arrays = {name: np.ascontiguousarray(inputs[name]) for name in _INS}
    arrays.update({k: np.ascontiguousarray(v) for k, v in constants(128, 8, 16, 64).items()})
    ins = {name: nc.dram_tensor(name + "_dram", a.shape, mybir.dt.from_np(a.dtype), kind="ExternalInput").ap()
           for name, a in arrays.items()}
    out = nc.dram_tensor("out_dram", inputs["x"].shape, fp32, kind="ExternalOutput").ap()
    build(nc, ins, out)
    r = run_bass_kernel_spmd(nc, [{name + "_dram": a for name, a in arrays.items()}], core_ids=[0])
    return r.results[0]["out_dram"]
```

```python
from contextlib import ExitStack

import concourse.bass as bass
from concourse import mybir

fp32 = mybir.dt.float32
bf16 = mybir.dt.bfloat16
ALU = mybir.AluOpType
ACT = mybir.ActivationFunctionType
AX = mybir.AxisListType

LEAD = 4


class Signal:

    def __init__(self, sem, per):
        self.sem, self.per = sem, per


def after(signal, g, k=None):
    return (g + LEAD) * signal.per + (signal.per if k is None else k)


def pipeline(eng, step, count, lags):
    head = lags + lags % 2
    for t in range(head):
        step(t, t % 2, lambda lag, t=t: lag <= t)
    with eng.Fori(head // 2, count // 2) as pair:
        step(2 * pair, 0, lambda lag: True)
        step(2 * pair + 1, 1, lambda lag: True)
    for t in range(count, count + lags):
        step(t, t % 2, lambda lag, t=t: t - lag < count)


def build(nc, ins, out):
    x, ctx_in = ins["x"], ins["ctx_1024"]
    NS, T, D = x.shape
    HX, DX = 16, 8
    HL, DL = 8, 64
    LAYERS = ins["L0_ffn_wqkv"].shape[0]
    INNER = HL * DL
    HID = ins["L0_ffn_w2"].shape[1]
    NJ = (HID + 127) // 128
    REST = HID - 128 * (NJ - 1)
    CH = 4
    EPS = 1e-5
    SCALE_X = float(DX) ** -0.5
    SCALE_L = 8.0
    X_STAT, X_PROJ, X_ROT, X_SCORE, X_WEIGH, X_Y = range(6)
    L_PROJ, L_ROT, L_SCORE, L_WEIGH = range(4)
    F_STAT, F_NORM, F_UP, F_DOWN = range(4)

    with ExitStack() as ctx:
        def sb(name, shape, dt=fp32):
            return ctx.enter_context(nc.sbuf_tensor(name, shape, dt))

        def signal(name, per=1):
            return Signal(ctx.enter_context(nc.semaphore(name)), per)

        x_all = sb("x_all", [128, NS, D])
        y_all = sb("y_all", [128, NS, D])
        ident = sb("ident", [128, 128])
        identb = sb("identb", [128, 128], bf16)
        shiftm = sb("shiftm", [128, 128])
        bandm = sb("bandm", [128, CH * 128], bf16)
        ropex = sb("ropex", [128, 2, DX])
        ropel = sb("ropel", [128, 4, DL])
        scales = sb("scales", [128, 4, DL])
        tab = sb("tab", [128, 4, DL])
        hmask = sb("hmask", [128, HX])
        nhalf = sb("nhalf", [128, 2 * HL])
        wx_in = sb("wx_in", [128, 4, D])
        wx = sb("wx", [128, 4, D])
        biasx = sb("biasx", [128, 3 * D])
        box = sb("box", [128, D])
        wqkv = sb("wqkv", [128, 3 * INNER])
        wol = sb("wol", [128, INNER // 128, D])
        w1 = sb("w1", [128, 2 * HID])
        w2 = sb("w2", [128, NJ, D])
        b1 = sb("b1", [128, 2, NJ])
        lgb = sb("lgb", [128, 2])
        ctxb = sb("ctxb", [128, 2, D])
        st = sb("st", [128, 2, 2, 6])
        mv = sb("mv", [128, 2, 2])
        ve = sb("ve", [128, 2, 1])
        rstd = sb("rstd", [128, 2, 1])
        st2 = sb("st2", [128, 2, 6])
        mv2 = sb("mv2", [128, 2, 2])
        ve2 = sb("ve2", [128, 2, 1])
        rstd2 = sb("rstd2", [128, 2, 1])
        xn = sb("xn", [128, 2, D])
        hT = sb("hT", [128, 2, 2, 128])
        raw = sb("raw", [128, 2, 2, INNER])
        sq = sb("sq", [128, 2 * INNER])
        ss = sb("ss", [128, 2, 2 * HL])
        ssc = sb("ssc", [128, 2 * HL])
        rn = sb("rn", [128, 2, 2 * HL])
        t1 = sb("t1", [128, 2, 2, INNER])
        t2 = sb("t2", [128, 2, 2, INNER])
        rot = sb("rot", [128, 2, 2 * INNER])
        qkT = sb("qkT", [128, 2, 2 * INNER])
        kx = sb("kx", [128, 2, HX, 128])
        vx = sb("vx", [128, 2, HX, DX + 1])
        vl = sb("vl", [128, 2, HL, DL + 1])
        top = sb("top", [128, 2, HX])
        prob = sb("prob", [128, 2, HX, 128])
        probT = sb("probT", [128, HX, 128])
        rsum = sb("rsum", [128, HX])
        o_sb = sb("o_sb", [128, INNER])
        oT = sb("oT", [128, INNER])
        yb = sb("yb", [128, 2, D])
        gate = sb("gate", [128, 2, NJ, 128])
        hid = sb("hid", [128, 2, NJ, 128])
        ps = ctx.enter_context(nc.psum_tensor("ps", [128, 8, 512], fp32))

        S = lambda n: ctx.enter_context(nc.semaphore(n))
        shift_zero, const_in, wx_loaded, setup_v, setup_t, setup_e = S("shift_zero"), S("const_in"), S("wx_loaded"), S("setup_v"), S("setup_t"), S("setup_e")
        x_in = [S("x_in0"), S("x_in1")]
        ctx_in_sem = [S("ctx_in0"), S("ctx_in1")]
        wl_in, wf_in, tab_ready, out_add, out_done = S("wl_in"), S("wf_in"), S("tab_ready"), S("out_add"), S("out_done")
        settled = S("settled")
        x_stat, x_mv, x_ve, x_rstd, x_norm = (signal(n) for n in ("x_stat", "x_mv", "x_ve", "x_rstd", "x_norm"))
        x_tr, x_trc, x_proj, x_vproj = (signal(n) for n in ("x_tr", "x_trc", "x_proj", "x_vproj"))
        x_bias, x_v = signal("x_bias"), signal("x_v")
        x_t, x_rot, x_bo = signal("x_t", 3), signal("x_rot"), signal("x_bo")
        x_qkt, x_qc, x_kx = signal("x_qkt"), signal("x_qc"), signal("x_kx")
        x_s, x_max, x_sub, x_exp = (signal(n, HX // CH) for n in ("x_s", "x_max", "x_sub", "x_exp"))
        x_pt, x_ptc, x_pv = (signal(n, HX // CH) for n in ("x_pt", "x_ptc", "x_pv"))
        x_rsum, x_o, x_ot, x_otc, x_wo, x_res = (signal(n) for n in ("x_rsum", "x_o", "x_ot", "x_otc", "x_wo", "x_res"))
        x_stat2, x_mv2, x_ve2, x_rstd2 = (signal(n) for n in ("x_stat2", "x_mv2", "x_ve2", "x_rstd2"))
        y_in = signal("y_in")
        l_yb, l_ht, l_htc = signal("l_yb"), signal("l_ht"), signal("l_htc", 2)
        l_qk, l_vp = signal("l_qk"), signal("l_vp")
        l_raw, l_sq, l_v, l_ss, l_ssc, l_rn = (signal(n) for n in ("l_raw", "l_sq", "l_v", "l_ss", "l_ssc", "l_rn"))
        l_t2, l_t1, l_add, l_rot = signal("l_t2", 2), signal("l_t1"), signal("l_add"), signal("l_rot")
        l_qkt, l_qktc = signal("l_qkt"), signal("l_qktc")
        l_s, l_max, l_sub, l_exp, l_pt, l_ptc, l_pv, l_rsum, l_o = (
            signal(n, HL // CH) for n in ("l_s", "l_max", "l_sub", "l_exp", "l_pt", "l_ptc", "l_pv", "l_rsum", "l_o"))
        l_ot, l_otc, l_wo = signal("l_ot"), signal("l_otc"), signal("l_wo")
        y_attn = signal("y_attn")
        f_yb, f_sh, f_stat, f_mv, f_ve, f_rstd = (signal(n) for n in ("f_yb", "f_sh", "f_stat", "f_mv", "f_ve", "f_rstd"))
        f_norm, f_t, f_tc, f_w1 = signal("f_norm", 2), signal("f_t"), signal("f_tc"), signal("f_w1", 2)
        f_gate, f_hid, f_w2 = signal("f_gate", NJ), signal("f_hid", NJ), signal("f_w2")

        def begin(eng, *signals):
            for s in signals:
                eng.sem_inc(s.sem, LEAD * s.per)

        def rows(j):
            return 128 if j < NJ - 1 else REST

        def bc(ap, shape):
            return ap.to_broadcast(shape)

        def settle(eng):
            eng.sem_inc(settled, 1)

        block = ctx.enter_context(nc.Block())

        consts = [(ident[:, :], ins["c_ident"]), (shiftm[:, :], ins["c_shift"]),
                  (sq[:, 0:128], ins["c_band"]), (ropex[:, :, :], ins["c_ropex"]), (ropel[:, :, :], ins["c_ropel"]),
                  (hmask[:, :], ins["c_hmask"])]
        N_CONST = len(consts) + 4
        N_WL, N_WF_IN = 2 + 6, 4 + 2 * NJ + 2
        N_SETUP = 7

        @block.sync
        def _(eng):
            for i, name in enumerate(("Wq", "Wk", "Wv", "Wo")):
                eng.dma_start(wx_in[:, i, :], ins["L0_xattn_" + name]).then_inc(wx_loaded, 16)
            for dst, src in consts:
                eng.dma_start(dst, src).then_inc(const_in, 16)
            for i, name in enumerate(("bq", "bk", "bv")):
                eng.dma_start(biasx[:, i * D:(i + 1) * D],
                              ins["L0_xattn_" + name].partition_broadcast(128)).then_inc(const_in, 16)
            eng.dma_start(box[:, :], ins["L0_xattn_bo"].partition_broadcast(128)).then_inc(const_in, 16)

            def load(t, p):
                eng.dma_start(x_all[:, bass.ds(t, 1), :], x[bass.ds(t, 1), :, :].rearrange("s t d -> t s d"))\
                   .then_inc(x_in[p], 16)
                eng.dma_start(ctxb[:, p:p + 1, :], ctx_in[bass.ds(t, 1), :, :].rearrange("s t d -> t s d"))\
                   .then_inc(ctx_in_sem[p], 16)
            load(0, 0)
            load(1, 1)
            with eng.Fori(1, NS // 2) as pair:
                for p in range(2):
                    t = 2 * pair + p
                    eng.wait_ge(x_in[p], 16 * pair)
                    settle(eng)
                    eng.wait_ge(ctx_in_sem[p], 16 * pair)
                    settle(eng)
                    eng.wait_ge(x_tr.sem, after(x_tr, t - 2))
                    settle(eng)
                    load(t, p)

            with eng.Fori(0, LAYERS) as layer:
                def of(name):
                    return ins["L0_ffn_" + name][bass.ds(layer, 1)]
                eng.wait_ge(l_qk.sem, after(l_qk, layer * NS - 1))
                settle(eng)
                eng.wait_ge(l_vp.sem, after(l_vp, layer * NS - 1))
                settle(eng)
                eng.wait_ge(l_wo.sem, after(l_wo, layer * NS - 1))
                settle(eng)
                eng.wait_ge(l_t1.sem, after(l_t1, layer * NS - 1))
                settle(eng)
                eng.dma_start(wqkv[:, :], of("wqkv").rearrange("a d n -> d (a n)")).then_inc(wl_in, 16)
                eng.dma_start(wol[:, :, :], of("wo").rearrange("a (c p) n -> p (a c) n", p=128)).then_inc(wl_in, 16)
                H2 = DL // 2
                for i, name in ((0, "q_scale"), (2, "k_scale")):
                    row = of(name).rearrange("a d -> (a d)")
                    eng.dma_start(scales[:, i, :], row.partition_broadcast(128)).then_inc(wl_in, 16)
                    eng.dma_start(scales[:, i + 1, 0:H2], row[H2:DL].partition_broadcast(128)).then_inc(wl_in, 16)
                    eng.dma_start(scales[:, i + 1, H2:DL], row[0:H2].partition_broadcast(128)).then_inc(wl_in, 16)
                eng.wait_ge(f_w1.sem, after(f_w1, layer * NS - 1))
                settle(eng)
                eng.wait_ge(f_w2.sem, after(f_w2, layer * NS - 1))
                settle(eng)
                eng.wait_ge(f_hid.sem, after(f_hid, layer * NS - 1))
                settle(eng)
                eng.wait_ge(f_tc.sem, after(f_tc, layer * NS - 1))
                settle(eng)
                eng.dma_start(w1[:, :], of("w1").rearrange("a d n -> d (a n)")).then_inc(wf_in, 16)
                w2row = of("w2").rearrange("a k n -> (a k) n")
                eng.dma_start(w2[:, 0:NJ - 1, :], w2row[0:128 * (NJ - 1), :].rearrange("(j p) n -> p j n", p=128))\
                   .then_inc(wf_in, 16)
                eng.dma_start(w2[0:REST, NJ - 1, :], w2row[128 * (NJ - 1):HID, :]).then_inc(wf_in, 16)
                eng.dma_start(w2[REST:REST + 1, NJ - 1, :], of("b2")).then_inc(wf_in, 16)
                b1row = of("b1").rearrange("a n -> (a n)")
                for half in range(2):
                    for j in range(NJ):
                        lo = half * HID + 128 * j
                        eng.dma_start(b1[0:rows(j), half, j:j + 1],
                                      b1row[lo:lo + rows(j)].rearrange("(n a) -> n a", a=1)).then_inc(wf_in, 16)
                for i, name in enumerate(("ln_g", "ln_b")):
                    eng.dma_start(lgb[:, i:i + 1], of(name).rearrange("a d -> d a")).then_inc(wf_in, 16)

            OUT_CHUNKS = 4
            n = NS // OUT_CHUNKS
            for c in range(OUT_CHUNKS):
                eng.wait_ge(out_add, c + 1)
                eng.dma_start(out[c * n:(c + 1) * n, :, :].rearrange("s t d -> t s d"),
                              x_all[:, c * n:(c + 1) * n, :]).then_inc(out_done, 16)
            eng.wait_ge(out_done, 16 * OUT_CHUNKS)

        @block.tensor
        def _(eng):
            begin(eng, x_tr, x_proj, x_vproj, x_qkt, x_s, x_pt, x_pv, x_ot, x_wo,
                  l_ht, l_qk, l_vp, l_qkt, l_s, l_pt, l_pv, l_ot, l_wo, f_sh, f_t, f_w1, f_w2)
            eng.wait_ge(wx_loaded, 64)
            eng.wait_ge(const_in, 16 * N_CONST)
            for i in range(4):
                mm = eng.transpose(ps[:, 0, i * 128:(i + 1) * 128], wx_in[:, i, :], ident[:, :])
            mm.then_inc(setup_t, 1)
            eng.wait_ge(setup_e, 1)

            def step_x(t, p, active):
                def project_in():
                    g, b = t - X_PROJ, (p - X_PROJ) % 2
                    eng.wait_ge(x_norm.sem, after(x_norm, g))
                    eng.wait_ge(ctx_in_sem[b], 8 * (g - b + 2))
                    eng.wait_ge(x_trc.sem, after(x_trc, g - 1))
                    eng.transpose(ps[:, 0, 0:128], xn[:, b, :], ident[:, :])
                    eng.transpose(ps[:, 0, 128:256], ctxb[:, b, :], ident[:, :]).then_inc(x_tr.sem, 1)

                def project_qk():
                    g, b = t - X_PROJ, (p - X_PROJ) % 2
                    eng.wait_ge(x_trc.sem, after(x_trc, g))
                    eng.wait_ge(x_bias.sem, after(x_bias, g - 1))
                    eng.wait_ge(x_v.sem, after(x_v, g - 2))
                    eng.matmul(ps[:, 1, 0:128], hT[:, b, 0, :], wx[:, 0, :], start=True, stop=True)
                    eng.matmul(ps[:, 1, 128:256], hT[:, b, 1, :], wx[:, 1, :], start=True, stop=True)\
                       .then_inc(x_proj.sem, 1)

                def project_v():
                    g, b = t - X_ROT, (p - X_ROT) % 2
                    eng.wait_ge(x_v.sem, after(x_v, g - 1))
                    eng.wait_ge(x_bias.sem, after(x_bias, g))
                    eng.matmul(ps[:, 1, 256:384], hT[:, b, 1, :], wx[:, 2, :], start=True, stop=True)\
                       .then_inc(x_vproj.sem, 1)

                def qk_T():
                    g, b = t - X_ROT, (p - X_ROT) % 2
                    eng.wait_ge(x_rot.sem, after(x_rot, g))
                    eng.wait_ge(x_qc.sem, after(x_qc, g - 1))
                    eng.transpose(ps[:, 2, 0:128], rot[:, b, 0:128], ident[:, :])
                    eng.transpose(ps[:, 2, 128:256], rot[:, b, 128:256], ident[:, :]).then_inc(x_qkt.sem, 1)

                def scores(c):
                    g, b = t - X_SCORE, (p - X_SCORE) % 2
                    if c == 0:
                        eng.wait_ge(x_qc.sem, after(x_qc, g))
                        eng.wait_ge(x_kx.sem, after(x_kx, g))
                    eng.wait_ge(x_sub.sem, after(x_sub, g - 1, c + 3))
                    eng.matmul(ps[:, 3 + c % 2, :], qkT[:, b, 0:128],
                               kx[:, b, c * CH:(c + 1) * CH, :].rearrange("p a b -> p (a b)"),
                               start=True, stop=True).then_inc(x_s.sem, 1)

                def prob_T(c):
                    g, b = t - X_WEIGH, (p - X_WEIGH) % 2
                    eng.wait_ge(x_exp.sem, after(x_exp, g, c + 1))
                    eng.wait_ge(x_ptc.sem, after(x_ptc, g - 1, c + 3))
                    for h in range(CH):
                        mm = eng.transpose(ps[:, 5 + c % 2, h * 128:(h + 1) * 128],
                                           prob[:, b, c * CH + h, :], ident[:, :])
                    mm.then_inc(x_pt.sem, 1)

                def weigh(c):
                    g, b = t - X_WEIGH, (p - X_WEIGH) % 2
                    eng.wait_ge(x_ptc.sem, after(x_ptc, g, c + 1))
                    if c == 0:
                        eng.wait_ge(x_v.sem, after(x_v, g))
                        eng.wait_ge(x_res.sem, after(x_res, g - 1))
                    for h in range(c * CH, (c + 1) * CH):
                        mm = eng.matmul(ps[:, 7, h * (DX + 1):(h + 1) * (DX + 1)], probT[:, h, :],
                                        vx[:, b, h, :], start=True, stop=True)
                    mm.then_inc(x_pv.sem, 1)

                def o_T():
                    g = t - X_WEIGH
                    eng.wait_ge(x_o.sem, after(x_o, g))
                    eng.transpose(ps[:, 7, 256:384], o_sb[:, 0:128], ident[:, :]).then_inc(x_ot.sem, 1)

                def project_out():
                    g = t - X_WEIGH
                    eng.wait_ge(x_otc.sem, after(x_otc, g))
                    eng.matmul(ps[:, 7, 384:512], oT[:, 0:128], wx[:, 3, :], start=True, stop=True)\
                       .then_inc(x_wo.sem, 1)

                if active(X_SCORE):
                    scores(0)
                if active(X_WEIGH):
                    prob_T(0)
                if active(X_SCORE):
                    scores(1)
                if active(X_WEIGH):
                    prob_T(1)
                if active(X_PROJ):
                    project_in()
                if active(X_WEIGH):
                    weigh(0)
                if active(X_ROT):
                    qk_T()
                if active(X_SCORE):
                    scores(2)
                if active(X_WEIGH):
                    prob_T(2)
                    weigh(1)
                if active(X_SCORE):
                    scores(3)
                if active(X_WEIGH):
                    prob_T(3)
                    weigh(2)
                if active(X_ROT):
                    project_v()
                if active(X_PROJ):
                    project_qk()
                if active(X_WEIGH):
                    weigh(3)
                    o_T()
                    project_out()

            pipeline(eng, step_x, NS, X_Y)

            with eng.Fori(0, LAYERS) as layer:
                base = layer * NS

                def step_l(t, p, active):
                    def tokens_T():
                        g, b = base + t - L_PROJ, (p - L_PROJ) % 2
                        eng.wait_ge(l_yb.sem, after(l_yb, g))
                        eng.wait_ge(l_htc.sem, after(l_htc, g - 1))
                        eng.transpose(ps[:, 0, 0:128], yb[:, b, :], ident[:, :]).then_inc(l_ht.sem, 1)

                    def project_qk():
                        g, b = base + t - L_PROJ, (p - L_PROJ) % 2
                        eng.wait_ge(l_htc.sem, after(l_htc, g))
                        eng.wait_ge(l_sq.sem, after(l_sq, g - 1))
                        for c in range(2):
                            mm = eng.matmul(ps[:, 1 + c, :], hT[:, b, 0, :], wqkv[:, c * INNER:(c + 1) * INNER],
                                            start=True, stop=True)
                        mm.then_inc(l_qk.sem, 1)

                    def project_v():
                        g, b = base + t - L_ROT, (p - L_ROT) % 2
                        eng.wait_ge(l_htc.sem, after(l_htc, g))
                        eng.wait_ge(l_v.sem, after(l_v, g - 1))
                        eng.matmul(ps[:, 3, :], hT[:, b, 0, :], wqkv[:, 2 * INNER:3 * INNER],
                                   start=True, stop=True).then_inc(l_vp.sem, 1)

                    def qk_T():
                        g, b = base + t - L_SCORE, (p - L_SCORE) % 2
                        eng.wait_ge(l_rot.sem, after(l_rot, g))
                        eng.wait_ge(l_sub.sem, after(l_sub, g - 1))
                        for i in range(2 * INNER // 128):
                            mm = eng.transpose(ps[:, 4 + i // 4, (i % 4) * 128:(i % 4 + 1) * 128],
                                               rot[:, b, i * 128:(i + 1) * 128], ident[:, :])
                        mm.then_inc(l_qkt.sem, 1)

                    def scores():
                        g, b = base + t - L_SCORE, (p - L_SCORE) % 2
                        eng.wait_ge(l_qktc.sem, after(l_qktc, g))
                        for c in range(2):
                            eng.matmul(ps[:, 4 + c, :], identb[:, :], bandm[:, :], start=True, stop=True)
                        for h in range(HL):
                            r, c, s = DL * (h % 2), h % 2, h // 2
                            q = qkT[r:r + DL, b, s * 128:(s + 1) * 128]
                            k = qkT[r:r + DL, b, INNER + s * 128:INNER + (s + 1) * 128]
                            mm = eng.matmul(ps[:, 4 + c, s * 128:(s + 1) * 128], q, k,
                                            start=False, stop=True, skip_group_check=True)
                            if s == CH - 1:
                                mm.then_inc(l_s.sem, 1)

                    def prob_T(c):
                        g, b = base + t - L_WEIGH, (p - L_WEIGH) % 2
                        eng.wait_ge(l_exp.sem, after(l_exp, g, c + 1))
                        if c == 0:
                            eng.wait_ge(l_otc.sem, after(l_otc, g - 1))
                        else:
                            eng.wait_ge(y_attn.sem, after(y_attn, g - 1))
                        for h in range(c * CH, (c + 1) * CH):
                            mm = eng.transpose(ps[:, 6 + c, (h % CH) * 128:(h % CH + 1) * 128],
                                               prob[:, b, h, :], ident[:, :])
                        mm.then_inc(l_pt.sem, 1)

                    def weigh(c):
                        g, b = base + t - L_WEIGH, (p - L_WEIGH) % 2
                        eng.wait_ge(l_ptc.sem, after(l_ptc, g, c + 1))
                        if c == 0:
                            eng.wait_ge(l_v.sem, after(l_v, g))
                        for s in range(CH):
                            mm = eng.matmul(ps[:, 6 + c, s * (DL + 1):(s + 1) * (DL + 1)],
                                            probT[:, c * CH + s, :], vl[:, b, 2 * s + c, :], start=True, stop=True)
                        mm.then_inc(l_pv.sem, 1)

                    def o_T():
                        g = base + t - L_WEIGH
                        eng.wait_ge(l_o.sem, after(l_o, g))
                        for i in range(INNER // 128):
                            mm = eng.transpose(ps[:, 6, i * 128:(i + 1) * 128],
                                               o_sb[:, i * 128:(i + 1) * 128], ident[:, :])
                        mm.then_inc(l_ot.sem, 1)

                    def project_out():
                        g = base + t - L_WEIGH
                        eng.wait_ge(l_otc.sem, after(l_otc, g))
                        NB = INNER // 128
                        for i in range(NB):
                            mm = eng.matmul(ps[:, 7, 0:128], oT[:, i * 128:(i + 1) * 128], wol[:, i, :],
                                            start=(i == 0), stop=(i == NB - 1))
                        mm.then_inc(l_wo.sem, 1)

                    if active(L_SCORE):
                        qk_T()
                    if active(L_WEIGH):
                        prob_T(0)
                        prob_T(1)
                    if active(L_PROJ):
                        tokens_T()
                    if active(L_SCORE):
                        scores()
                    if active(L_WEIGH):
                        weigh(0)
                        weigh(1)
                    if active(L_PROJ):
                        project_qk()
                    if active(L_WEIGH):
                        o_T()
                    if active(L_ROT):
                        project_v()
                    if active(L_WEIGH):
                        project_out()

                eng.wait_ge(wl_in, (layer + 1) * (16 * N_WL))
                eng.wait_ge(setup_v, N_SETUP)
                pipeline(eng, step_l, NS, L_WEIGH)

                def step_f(t, p, active):
                    def shift():
                        g, b = base + t - F_STAT, (p - F_STAT) % 2
                        eng.wait_ge(f_yb.sem, after(f_yb, g))
                        eng.wait_ge(f_norm.sem, after(f_norm, g - 2))
                        eng.matmul(ps[:, 5 * b, 0:D // 2], shiftm[:, :], yb[:, b, D // 2:D], start=True, stop=True)\
                           .then_inc(f_sh.sem, 1)

                    def tokens_T():
                        g, b = base + t - F_NORM, (p - F_NORM) % 2
                        eng.wait_ge(f_norm.sem, after(f_norm, g))
                        eng.wait_ge(f_tc.sem, after(f_tc, g - 1))
                        eng.transpose(ps[:, 1, 0:128], xn[:, b, :], ident[:, :]).then_inc(f_t.sem, 1)

                    def expand():
                        g, b = base + t - F_UP, (p - F_UP) % 2
                        eng.wait_ge(f_tc.sem, after(f_tc, g))
                        eng.wait_ge(f_hid.sem, after(f_hid, g - 2))
                        for half, bank in ((1, 3 + 4 * b), (0, 2 + 4 * b)):
                            for j in range(NJ):
                                lo = half * HID + 128 * j
                                mm = eng.matmul(ps[0:rows(j), bank, j * 128:(j + 1) * 128],
                                                w1[:, lo:lo + rows(j)], hT[:, b, 0, :], start=True, stop=True)
                            mm.then_inc(f_w1.sem, 1)

                    def contract():
                        g, b = base + t - F_DOWN, (p - F_DOWN) % 2
                        eng.wait_ge(f_hid.sem, after(f_hid, g))
                        eng.wait_ge(y_in.sem, after(y_in, g + NS - 1))
                        for j in range(NJ):
                            k = rows(j) + (j == NJ - 1)
                            mm = eng.matmul(ps[:, 4, 0:128], hid[0:k, b, j, :], w2[0:k, j, :],
                                            start=(j == 0), stop=(j == NJ - 1))
                        mm.then_inc(f_w2.sem, 1)

                    if active(F_STAT):
                        shift()
                    if active(F_UP):
                        expand()
                    if active(F_DOWN):
                        contract()
                    if active(F_NORM):
                        tokens_T()

                eng.wait_ge(wf_in, (layer + 1) * (16 * N_WF_IN))
                pipeline(eng, step_f, NS, F_DOWN)

        @block.scalar
        def _(eng):
            begin(eng, x_trc, x_qc, x_exp, x_ptc, x_otc, l_htc, l_raw, l_sq, l_v, l_qktc, l_exp, l_ptc, l_otc,
                  f_tc, f_gate)
            eng.wait_ge(setup_t, 1)
            eng.activation(wx[:, :, :].rearrange("p a b -> p (a b)"), ps[:, 0, :], ACT.Copy).then_inc(setup_e, 1)

            def step_x(t, p, active):
                def tokens_T():
                    g, b = t - X_PROJ, (p - X_PROJ) % 2
                    eng.wait_ge(x_tr.sem, after(x_tr, g))
                    eng.wait_ge(x_proj.sem, after(x_proj, g - 2))
                    eng.wait_ge(x_vproj.sem, after(x_vproj, g - 2))
                    eng.activation(hT[:, b, :, :].rearrange("p a b -> p (a b)"), ps[:, 0, 0:256], ACT.Copy)\
                       .then_inc(x_trc.sem, 1)

                def qk_T():
                    g, b = t - X_ROT, (p - X_ROT) % 2
                    eng.wait_ge(x_qkt.sem, after(x_qkt, g))
                    eng.wait_ge(x_s.sem, after(x_s, g - 2))
                    eng.wait_ge(x_kx.sem, after(x_kx, g - 2))
                    eng.activation(qkT[:, b, 0:256], ps[:, 2, 0:256], ACT.Copy).then_inc(x_qc.sem, 1)

                def exps(c):
                    g, b = t - X_SCORE, (p - X_SCORE) % 2
                    eng.wait_ge(x_sub.sem, after(x_sub, g, c + 1))
                    s = prob[:, b, c * CH:(c + 1) * CH, :].rearrange("p a b -> p (a b)")
                    eng.activation(s, s, ACT.Exp, scale=SCALE_X).then_inc(x_exp.sem, 1)

                def prob_T(c):
                    g = t - X_WEIGH
                    eng.wait_ge(x_pt.sem, after(x_pt, g, c + 1))
                    eng.wait_ge(x_pv.sem, after(x_pv, g - 1, c + 1))
                    eng.activation(probT[:, c * CH:(c + 1) * CH, :].rearrange("p a b -> p (a b)"),
                                   ps[:, 5 + c % 2, :], ACT.Copy).then_inc(x_ptc.sem, 1)

                def o_T():
                    g = t - X_WEIGH
                    eng.wait_ge(x_ot.sem, after(x_ot, g))
                    eng.wait_ge(x_wo.sem, after(x_wo, g - 1))
                    eng.activation(oT[:, 0:128], ps[:, 7, 256:384], ACT.Copy).then_inc(x_otc.sem, 1)

                if active(X_WEIGH):
                    prob_T(0)
                    prob_T(1)
                if active(X_PROJ):
                    tokens_T()
                if active(X_ROT):
                    qk_T()
                if active(X_SCORE):
                    exps(0)
                if active(X_WEIGH):
                    prob_T(2)
                if active(X_SCORE):
                    exps(1)
                if active(X_WEIGH):
                    prob_T(3)
                if active(X_SCORE):
                    exps(2)
                if active(X_WEIGH):
                    o_T()
                if active(X_SCORE):
                    exps(3)

            pipeline(eng, step_x, NS, X_Y)

            with eng.Fori(0, LAYERS) as layer:
                base = layer * NS

                def step_l(t, p, active):
                    def tokens_T():
                        g, b = base + t - L_PROJ, (p - L_PROJ) % 2
                        eng.wait_ge(l_ht.sem, after(l_ht, g))
                        eng.wait_ge(l_vp.sem, after(l_vp, g - 2))
                        H = D // 2
                        eng.activation(hT[0:H, b, 0, :], ps[0:H, 0, 0:128], ACT.Copy).then_inc(l_htc.sem, 1)
                        eng.activation(hT[H:D, b, 0, 1:128], ps[H:D, 0, 0:127], ACT.Copy).then_inc(l_htc.sem, 1)

                    def prob_T(c):
                        g = base + t - L_WEIGH
                        eng.wait_ge(l_pt.sem, after(l_pt, g, c + 1))
                        eng.wait_ge(l_pv.sem, after(l_pv, g - 1, c + 1))
                        eng.activation(probT[:, c * CH:(c + 1) * CH, :].rearrange("p a b -> p (a b)"),
                                       ps[:, 6 + c, :], ACT.Copy).then_inc(l_ptc.sem, 1)

                    def raw_qk():
                        g, b = base + t - L_PROJ, (p - L_PROJ) % 2
                        eng.wait_ge(l_qk.sem, after(l_qk, g))
                        eng.wait_ge(l_t1.sem, after(l_t1, g - 2))
                        eng.wait_ge(l_t2.sem, after(l_t2, g - 2))
                        eng.activation(raw[:, b, :, :].rearrange("p a b -> p (a b)"),
                                       ps[:, 1:3, :].rearrange("p a b -> p (a b)"), ACT.Copy).then_inc(l_raw.sem, 1)

                    def square_qk():
                        g = base + t - L_PROJ
                        eng.wait_ge(l_ss.sem, after(l_ss, g - 1))
                        eng.activation(sq[:, :], ps[:, 1:3, :].rearrange("p a b -> p (a b)"), ACT.Square)\
                           .then_inc(l_sq.sem, 1)

                    def value():
                        g, b = base + t - L_ROT, (p - L_ROT) % 2
                        eng.wait_ge(l_vp.sem, after(l_vp, g))
                        eng.wait_ge(l_pv.sem, after(l_pv, g - 2))
                        eng.activation(vl[:, b, :, 0:DL], ps[:, 3, :].rearrange("p (h d) -> p h d", d=DL), ACT.Copy)\
                           .then_inc(l_v.sem, 1)

                    def qk_T():
                        g, b = base + t - L_SCORE, (p - L_SCORE) % 2
                        eng.wait_ge(l_qkt.sem, after(l_qkt, g))
                        eng.wait_ge(l_s.sem, after(l_s, g - 2))
                        eng.activation(qkT[:, b, :], ps[:, 4:6, :].rearrange("p a b -> p (a b)"), ACT.Copy)\
                           .then_inc(l_qktc.sem, 1)

                    def exps(c):
                        g, b = base + t - L_SCORE, (p - L_SCORE) % 2
                        eng.wait_ge(l_sub.sem, after(l_sub, g, c + 1))
                        s = prob[:, b, c * CH:(c + 1) * CH, :].rearrange("p a b -> p (a b)")
                        eng.activation(s, s, ACT.Exp, scale=SCALE_L).then_inc(l_exp.sem, 1)

                    def o_T():
                        g = base + t - L_WEIGH
                        eng.wait_ge(l_ot.sem, after(l_ot, g))
                        eng.wait_ge(l_wo.sem, after(l_wo, g - 1))
                        eng.activation(oT[:, :], ps[:, 6, :], ACT.Copy).then_inc(l_otc.sem, 1)

                    if active(L_SCORE):
                        qk_T()
                    if active(L_WEIGH):
                        prob_T(0)
                        prob_T(1)
                    if active(L_PROJ):
                        tokens_T()
                    if active(L_SCORE):
                        exps(0)
                        exps(1)
                    if active(L_PROJ):
                        raw_qk()
                    if active(L_WEIGH):
                        o_T()
                    if active(L_PROJ):
                        square_qk()
                    if active(L_ROT):
                        value()

                eng.wait_ge(shift_zero, layer + 1)
                pipeline(eng, step_l, NS, L_WEIGH)

                def step_f(t, p, active):
                    def tokens_T():
                        g, b = base + t - F_NORM, (p - F_NORM) % 2
                        eng.wait_ge(f_t.sem, after(f_t, g))
                        eng.wait_ge(f_w1.sem, after(f_w1, g - 2))
                        eng.activation(hT[:, b, 0, :], ps[:, 1, 0:128], ACT.Identity, scale=lgb[:, 0:1],
                                       bias=lgb[:, 1:2]).then_inc(f_tc.sem, 1)

                    def gates():
                        g, b = base + t - F_UP, (p - F_UP) % 2
                        eng.wait_ge(f_w1.sem, after(f_w1, g, 1))
                        eng.wait_ge(f_hid.sem, after(f_hid, g - 2))
                        for j in range(NJ):
                            eng.activation(gate[0:rows(j), b, j, :], ps[0:rows(j), 3 + 4 * b, j * 128:(j + 1) * 128],
                                           ACT.Gelu, bias=b1[0:rows(j), 1, j:j + 1]).then_inc(f_gate.sem, 1)

                    if active(F_UP):
                        gates()
                    if active(F_NORM):
                        tokens_T()

                eng.wait_ge(wf_in, (layer + 1) * (16 * N_WF_IN))
                pipeline(eng, step_f, NS, F_DOWN)

        @block.vector
        def _(eng):
            begin(eng, x_stat, x_mv, x_ve, x_norm, x_bias, x_v, x_rot, x_max, x_sub, x_rsum, x_o, x_res,
                  x_stat2, x_mv2, x_ve2, y_in, l_ss, l_t1, l_add, l_rot, l_max, l_sub, l_rsum, l_o, y_attn,
                  f_stat, f_mv, f_ve, f_norm, f_hid)
            eng.memset(nhalf[:, :], -0.5).then_inc(setup_v, 1)
            eng.memset(vx[:, :, :, :], 1.0).then_inc(setup_v, 1)
            eng.memset(vl[:, :, :, :], 1.0).then_inc(setup_v, 1)
            eng.memset(hid[:, :, :, :], 1.0).then_inc(setup_v, 1)
            eng.memset(rot[:, :, :], 0.0).then_inc(setup_v, 1)
            eng.wait_ge(const_in, 16 * N_CONST)
            eng.tensor_copy(identb[:, :], ident[:, :]).then_inc(setup_v, 1)
            eng.tensor_copy(bandm[:, :].rearrange("p (a b) -> p a b", a=CH),
                            bc(sq[:, 0:128].unsqueeze(1), [128, CH, 128])).then_inc(setup_v, 1)
            eng.wait_ge(setup_v, N_SETUP)

            def step_x(t, p, active):
                def stats(k):
                    g, b = t - X_STAT, (p - X_STAT) % 2
                    if k == 0:
                        eng.wait_ge(x_in[b], 8 * (g - b + 2))
                        settle(eng)
                        eng.bn_stats(st[:, b, 0, :], x_all[:, bass.ds(t, 1), :]).then_inc(x_stat.sem, 1)
                    if k == 1:
                        eng.wait_ge(x_stat.sem, after(x_stat, g))
                        settle(eng)
                        eng.bn_aggr(mv[:, b, :], st[:, b, 0, :]).then_inc(x_mv.sem, 1)
                    if k == 2:
                        eng.wait_ge(x_mv.sem, after(x_mv, g))
                        eng.wait_ge(x_rstd.sem, after(x_rstd, g - 2))
                        eng.tensor_scalar(ve[:, b, :], mv[:, b, 1:2], EPS, None, ALU.add).then_inc(x_ve.sem, 1)

                def normalise():
                    g, b = t - X_PROJ, (p - X_PROJ) % 2
                    eng.wait_ge(x_rstd.sem, after(x_rstd, g))
                    eng.wait_ge(x_tr.sem, after(x_tr, g - 2))
                    eng.tensor_scalar(xn[:, b, :].unsqueeze(1), x_all[:, bass.ds(g, 1), :], mv[:, b, 0:1],
                                      rstd[:, b, :], ALU.subtract, ALU.mult).then_inc(x_norm.sem, 1)

                def bias_qk():
                    g = t - X_PROJ
                    eng.wait_ge(x_proj.sem, after(x_proj, g))
                    eng.wait_ge(x_t.sem, after(x_t, g - 1))
                    eng.tensor_tensor(raw[:, 0, 0, 0:256], ps[:, 1, 0:256], biasx[:, 0:256], ALU.add)\
                       .then_inc(x_bias.sem, 1)

                def bias_v():
                    g, b = t - X_ROT, (p - X_ROT) % 2
                    eng.wait_ge(x_vproj.sem, after(x_vproj, g))
                    eng.wait_ge(x_pv.sem, after(x_pv, g - 2))
                    eng.tensor_tensor(vx[:, b, :, 0:DX], ps[:, 1, 256:384].rearrange("p (h d) -> p h d", d=DX),
                                      biasx[:, 256:384].rearrange("p (h d) -> p h d", d=DX), ALU.add)\
                       .then_inc(x_v.sem, 1)

                def rotate():
                    g, b = t - X_ROT, (p - X_ROT) % 2
                    eng.wait_ge(x_t.sem, after(x_t, g))
                    eng.wait_ge(x_qkt.sem, after(x_qkt, g - 2))
                    eng.tensor_tensor(rot[:, b, 0:256], t1[:, b, 0, 0:256], t2[:, b, 0, 0:256], ALU.add)\
                       .then_inc(x_rot.sem, 1)

                def maxima(c):
                    g, b = t - X_SCORE, (p - X_SCORE) % 2
                    eng.wait_ge(x_s.sem, after(x_s, g, c + 1))
                    eng.tensor_reduce(top[:, b, c * CH:(c + 1) * CH],
                                      ps[:, 3 + c % 2, :].rearrange("p (h k) -> p h k", k=128), AX.X, ALU.max)\
                       .then_inc(x_max.sem, 1)

                def subtract(c):
                    g, b = t - X_SCORE, (p - X_SCORE) % 2
                    eng.wait_ge(x_max.sem, after(x_max, g, c + 1))
                    eng.wait_ge(x_pt.sem, after(x_pt, g - 2, c + 1))
                    eng.tensor_tensor(prob[:, b, c * CH:(c + 1) * CH, :],
                                      ps[:, 3 + c % 2, :].rearrange("p (h k) -> p h k", k=128),
                                      bc(top[:, b, c * CH:(c + 1) * CH].unsqueeze(2), [128, CH, 128]),
                                      ALU.subtract).then_inc(x_sub.sem, 1)

                def inv_sums():
                    g = t - X_WEIGH
                    eng.wait_ge(x_pv.sem, after(x_pv, g))
                    o = ps[:, 7, 0:HX * (DX + 1)].rearrange("p (h d) -> p h d", d=DX + 1)
                    eng.reciprocal(rsum[:, :].unsqueeze(2), o[:, :, DX:DX + 1]).then_inc(x_rsum.sem, 1)

                def o_norm():
                    g = t - X_WEIGH
                    o = ps[:, 7, 0:HX * (DX + 1)].rearrange("p (h d) -> p h d", d=DX + 1)
                    eng.wait_ge(x_rsum.sem, after(x_rsum, g))
                    eng.wait_ge(x_ot.sem, after(x_ot, g - 1))
                    eng.tensor_tensor(o_sb[:, 0:128].rearrange("p (h d) -> p h d", d=DX), o[:, :, 0:DX],
                                      bc(rsum[:, :].unsqueeze(2), [128, HX, DX]), ALU.mult).then_inc(x_o.sem, 1)

                def residual():
                    g = t - X_WEIGH
                    eng.wait_ge(x_wo.sem, after(x_wo, g))
                    eng.wait_ge(x_bo.sem, after(x_bo, g))
                    xi = x_all[:, bass.ds(g, 1), :]
                    eng.tensor_tensor(xi, ps[:, 7, 384:512].unsqueeze(1), xi, ALU.add).then_inc(x_res.sem, 1)

                def stats2(k):
                    g, b = t - X_Y, (p - X_Y) % 2
                    if k == 0:
                        eng.wait_ge(x_res.sem, after(x_res, g))
                        settle(eng)
                        eng.bn_stats(st2[:, b, :], x_all[:, bass.ds(g, 1), :]).then_inc(x_stat2.sem, 1)
                    if k == 1:
                        eng.wait_ge(x_stat2.sem, after(x_stat2, g))
                        settle(eng)
                        eng.bn_aggr(mv2[:, b, :], st2[:, b, :]).then_inc(x_mv2.sem, 1)
                    if k == 2:
                        eng.wait_ge(x_mv2.sem, after(x_mv2, g))
                        eng.wait_ge(x_rstd2.sem, after(x_rstd2, g - 2))
                        eng.tensor_scalar(ve2[:, b, :], mv2[:, b, 1:2], EPS, None, ALU.add).then_inc(x_ve2.sem, 1)

                def normalise_y():
                    g, b = t - X_Y, (p - X_Y) % 2
                    eng.wait_ge(x_rstd2.sem, after(x_rstd2, g))
                    eng.tensor_scalar(y_all[:, bass.ds(g, 1), :], x_all[:, bass.ds(g, 1), :],
                                      mv2[:, b, 0:1], rstd2[:, b, :], ALU.subtract, ALU.mult).then_inc(y_in.sem, 1)

                if active(X_PROJ):
                    normalise()
                if active(X_STAT):
                    stats(0)
                if active(X_Y):
                    stats2(0)
                if active(X_STAT):
                    stats(1)
                if active(X_Y):
                    stats2(1)
                if active(X_SCORE):
                    maxima(0)
                if active(X_STAT):
                    stats(2)
                if active(X_Y):
                    stats2(2)
                if active(X_SCORE):
                    maxima(1)
                    subtract(0)
                if active(X_ROT):
                    rotate()
                if active(X_SCORE):
                    subtract(1)
                    maxima(2)
                if active(X_Y):
                    normalise_y()
                if active(X_SCORE):
                    maxima(3)
                    subtract(2)
                    subtract(3)
                if active(X_WEIGH):
                    inv_sums()
                if active(X_PROJ):
                    bias_qk()
                if active(X_WEIGH):
                    o_norm()
                if active(X_ROT):
                    bias_v()
                if active(X_WEIGH):
                    residual()

            pipeline(eng, step_x, NS, X_Y)

            with eng.Fori(0, LAYERS) as layer:
                base = layer * NS
                eng.memset(hT[:, :, 0, 0:1], 0.0).then_inc(shift_zero, 1)
                eng.wait_ge(wl_in, (layer + 1) * (16 * N_WL))
                eng.wait_ge(l_t2.sem, after(l_t2, base - 1))
                for i in range(4):
                    eng.tensor_tensor(tab[:, i, :], ropel[:, i, :], scales[:, i, :], ALU.mult).then_inc(tab_ready, 1)
                eng.wait_ge(tab_ready, (layer + 1) * 4)

                def step_l(t, p, active):
                    flat = t1[:, 0, :, :].rearrange("p a b -> p (a b)")

                    def cosines():
                        g, b = base + t - L_ROT, (p - L_ROT) % 2
                        eng.wait_ge(l_raw.sem, after(l_raw, g))
                        eng.wait_ge(l_rot.sem, after(l_rot, g - 1))
                        eng.tensor_tensor(t1[:, 0, :, :].rearrange("p a (h d) -> p a h d", d=DL),
                                          raw[:, b, :, :].rearrange("p a (h d) -> p a h d", d=DL),
                                          bc(tab[:, 0:4:2, :].unsqueeze(2), [128, 2, HL, DL]), ALU.mult)\
                           .then_inc(l_t1.sem, 1)

                    def squares():
                        g, b = base + t - L_ROT, (p - L_ROT) % 2
                        eng.wait_ge(l_sq.sem, after(l_sq, g))
                        eng.wait_ge(l_ssc.sem, after(l_ssc, g - 2))
                        eng.tensor_reduce(ss[:, b, :], sq[:, :].rearrange("p (h d) -> p h d", d=DL), AX.X, ALU.add)\
                           .then_inc(l_ss.sem, 1)

                    def add_sines():
                        g, b = base + t - L_ROT, (p - L_ROT) % 2
                        eng.wait_ge(l_t1.sem, after(l_t1, g))
                        eng.wait_ge(l_t2.sem, after(l_t2, g))
                        eng.tensor_tensor(flat, flat, t2[:, b, :, :].rearrange("p a b -> p (a b)"), ALU.add)\
                           .then_inc(l_add.sem, 1)

                    def unit_norm():
                        g, b = base + t - L_ROT, (p - L_ROT) % 2
                        eng.wait_ge(l_add.sem, after(l_add, g))
                        eng.wait_ge(l_rn.sem, after(l_rn, g))
                        eng.wait_ge(l_qkt.sem, after(l_qkt, g - 2))
                        eng.tensor_tensor(rot[:, b, :].rearrange("p (h d) -> p h d", d=DL),
                                          flat.rearrange("p (h d) -> p h d", d=DL),
                                          bc(rn[:, b, :].unsqueeze(2), [128, 2 * HL, DL]), ALU.mult)\
                           .then_inc(l_rot.sem, 1)

                    def maxima(c):
                        g, b = base + t - L_SCORE, (p - L_SCORE) % 2
                        eng.wait_ge(l_s.sem, after(l_s, g, c + 1))
                        eng.tensor_reduce(top[:, b, c * CH:(c + 1) * CH],
                                          ps[:, 4 + c, :].rearrange("p (h k) -> p h k", k=128), AX.X, ALU.max)\
                           .then_inc(l_max.sem, 1)

                    def subtract(c):
                        g, b = base + t - L_SCORE, (p - L_SCORE) % 2
                        eng.wait_ge(l_max.sem, after(l_max, g, c + 1))
                        eng.wait_ge(l_pt.sem, after(l_pt, g - 2, c + 1))
                        eng.tensor_tensor(prob[:, b, c * CH:(c + 1) * CH, :],
                                          ps[:, 4 + c, :].rearrange("p (h k) -> p h k", k=128),
                                          bc(top[:, b, c * CH:(c + 1) * CH].unsqueeze(2), [128, CH, 128]),
                                          ALU.subtract).then_inc(l_sub.sem, 1)

                    def inv_sums(c):
                        g = base + t - L_WEIGH
                        o = ps[:, 6 + c, 0:CH * (DL + 1)].rearrange("p (h d) -> p h d", d=DL + 1)
                        eng.wait_ge(l_pv.sem, after(l_pv, g, c + 1))
                        eng.reciprocal(rsum[:, c * CH:(c + 1) * CH].unsqueeze(2), o[:, :, DL:DL + 1])\
                           .then_inc(l_rsum.sem, 1)

                    def o_norm(c):
                        g = base + t - L_WEIGH
                        o = ps[:, 6 + c, 0:CH * (DL + 1)].rearrange("p (h d) -> p h d", d=DL + 1)
                        eng.wait_ge(l_rsum.sem, after(l_rsum, g, c + 1))
                        eng.wait_ge(l_ot.sem, after(l_ot, g - 1))
                        eng.tensor_tensor(o_sb[:, :].rearrange("p (s c d) -> p c s d", c=2, d=DL)[:, c, :, :],
                                          o[:, :, 0:DL],
                                          bc(rsum[:, c * CH:(c + 1) * CH].unsqueeze(2), [128, CH, DL]),
                                          ALU.mult).then_inc(l_o.sem, 1)

                    def residual():
                        g = base + t - L_WEIGH
                        yi = y_all[:, bass.ds(t - L_WEIGH, 1), :]
                        eng.wait_ge(l_wo.sem, after(l_wo, g))
                        eng.wait_ge(l_yb.sem, after(l_yb, g))
                        eng.tensor_tensor(yi, ps[:, 7, 0:128].unsqueeze(1), yi, ALU.add).then_inc(y_attn.sem, 1)

                    if active(L_ROT):
                        squares()
                        cosines()
                        add_sines()
                    if active(L_SCORE):
                        maxima(0)
                        maxima(1)
                        subtract(0)
                        subtract(1)
                    if active(L_WEIGH):
                        inv_sums(0)
                        inv_sums(1)
                        o_norm(0)
                        o_norm(1)
                    if active(L_ROT):
                        unit_norm()
                    if active(L_WEIGH):
                        residual()

                pipeline(eng, step_l, NS, L_WEIGH)

                def step_f(t, p, active):
                    H = D // 2

                    def stats(k):
                        g, b = base + t - F_STAT, (p - F_STAT) % 2
                        if k == 0:
                            eng.wait_ge(f_sh.sem, after(f_sh, g))
                            settle(eng)
                            eng.bn_stats(st[:, b, 0, :], yb[:, b, 0:H])
                            eng.bn_stats(st[:, b, 1, :], ps[:, 5 * b, 0:H]).then_inc(f_stat.sem, 1)
                        if k == 1:
                            eng.wait_ge(f_stat.sem, after(f_stat, g))
                            settle(eng)
                            eng.bn_aggr(mv[:, b, :], st[:, b, :, :].rearrange("p a b -> p (a b)"))\
                               .then_inc(f_mv.sem, 1)
                        if k == 2:
                            eng.wait_ge(f_mv.sem, after(f_mv, g))
                            eng.wait_ge(f_rstd.sem, after(f_rstd, g - 2))
                            eng.tensor_scalar(ve[:, b, :], mv[:, b, 1:2], EPS, None, ALU.add).then_inc(f_ve.sem, 1)

                    def normalise():
                        g, b = base + t - F_NORM, (p - F_NORM) % 2
                        eng.wait_ge(f_rstd.sem, after(f_rstd, g))
                        eng.wait_ge(f_t.sem, after(f_t, g - 2))
                        eng.tensor_scalar(xn[:, b, 0:H], yb[:, b, 0:H], mv[:, b, 0:1], rstd[:, b, :],
                                          ALU.subtract, ALU.mult).then_inc(f_norm.sem, 1)
                        eng.tensor_scalar(xn[:, b, H:D], ps[:, 5 * b, 0:H], mv[:, b, 0:1], rstd[:, b, :],
                                          ALU.subtract, ALU.mult).then_inc(f_norm.sem, 1)

                    def gated(j):
                        g, b = base + t - F_UP, (p - F_UP) % 2
                        if j == 0:
                            eng.wait_ge(f_w1.sem, after(f_w1, g))
                            eng.wait_ge(f_w2.sem, after(f_w2, g - 2))
                        n = rows(j)
                        eng.wait_ge(f_gate.sem, after(f_gate, g, j + 1))
                        eng.scalar_tensor_tensor(hid[0:n, b, j, :], ps[0:n, 2 + 4 * b, j * 128:(j + 1) * 128],
                                                 b1[0:n, 0, j:j + 1], gate[0:n, b, j, :], ALU.add, ALU.mult)\
                           .then_inc(f_hid.sem, 1)

                    def residual():
                        g = base + t - F_DOWN
                        yi = y_all[:, bass.ds(t - F_DOWN, 1), :]
                        eng.wait_ge(f_w2.sem, after(f_w2, g))
                        eng.wait_ge(f_yb.sem, after(f_yb, g))
                        eng.tensor_tensor(yi, ps[:, 4, 0:128].unsqueeze(1), yi, ALU.add).then_inc(y_in.sem, 1)

                    if active(F_NORM):
                        normalise()
                    if active(F_STAT):
                        stats(0)
                        stats(1)
                        stats(2)
                    if active(F_UP):
                        gated(0)
                        gated(1)
                        gated(2)
                    if active(F_DOWN):
                        residual()

                assert NJ == 3
                eng.wait_ge(wf_in, (layer + 1) * (16 * N_WF_IN))
                pipeline(eng, step_f, NS, F_DOWN)

            n = NS // 4
            eng.wait_ge(y_in.sem, after(y_in, (LAYERS + 1) * NS - 1))
            for c in range(4):
                part = x_all[:, c * n:(c + 1) * n, :]
                eng.tensor_tensor(part, part, y_all[:, c * n:(c + 1) * n, :], ALU.add).then_inc(out_add, 1)

        @block.gpsimd
        def _(eng):
            begin(eng, x_rstd, x_t, x_kx, x_bo, x_rstd2, l_yb, l_ssc, l_rn, l_t2, f_yb, f_rstd)
            eng.wait_ge(setup_v, N_SETUP)
            eng.wait_ge(const_in, 16 * N_CONST)

            def step_x(t, p, active):
                def inv_std():
                    g, b = t - X_STAT, (p - X_STAT) % 2
                    eng.wait_ge(x_ve.sem, after(x_ve, g))
                    eng.wait_ge(x_norm.sem, after(x_norm, g - 2))
                    eng.tensor_tensor(rstd[:, b, :], ve[:, b, :], nhalf[:, 0:1], ALU.pow).then_inc(x_rstd.sem, 1)

                def rotary():
                    g, b = t - X_ROT, (p - X_ROT) % 2
                    eng.wait_ge(x_bias.sem, after(x_bias, g))
                    eng.wait_ge(x_rot.sem, after(x_rot, g - 2))
                    r = raw[:, 0, 0, 0:256].rearrange("p (h d) -> p h d", d=DX)
                    u = t1[:, b, 0, 0:256].rearrange("p (h d) -> p h d", d=DX)
                    w = t2[:, b, 0, 0:256].rearrange("p (h d) -> p h d", d=DX)
                    H2, NH = DX // 2, 2 * HX
                    eng.tensor_tensor(u, r, bc(ropex[:, 0:1, :], [128, NH, DX]), ALU.mult).then_inc(x_t.sem, 1)
                    eng.tensor_tensor(w[:, :, 0:H2], r[:, :, H2:DX], bc(ropex[:, 1:2, 0:H2], [128, NH, H2]),
                                      ALU.mult).then_inc(x_t.sem, 1)
                    eng.tensor_tensor(w[:, :, H2:DX], r[:, :, 0:H2], bc(ropex[:, 1:2, H2:DX], [128, NH, H2]),
                                      ALU.mult).then_inc(x_t.sem, 1)

                def spread_k():
                    g, b = t - X_ROT, (p - X_ROT) % 2
                    eng.wait_ge(x_qc.sem, after(x_qc, g))
                    eng.wait_ge(x_s.sem, after(x_s, g - 2))
                    eng.tensor_tensor(kx[:, b, :, :], bc(qkT[:, b, 128:256].unsqueeze(1), [128, HX, 128]),
                                      bc(hmask[:, :].unsqueeze(2), [128, HX, 128]), ALU.mult).then_inc(x_kx.sem, 1)

                def add_bo():
                    g = t - X_ROT
                    xi = x_all[:, bass.ds(g, 1), :]
                    eng.wait_ge(x_norm.sem, after(x_norm, g))
                    eng.tensor_tensor(xi, xi, box[:, :].unsqueeze(1), ALU.add).then_inc(x_bo.sem, 1)

                def inv_std2():
                    g, b = t - X_Y, (p - X_Y) % 2
                    eng.wait_ge(x_ve2.sem, after(x_ve2, g))
                    eng.wait_ge(y_in.sem, after(y_in, g - 2))
                    eng.tensor_tensor(rstd2[:, b, :], ve2[:, b, :], nhalf[:, 0:1], ALU.pow).then_inc(x_rstd2.sem, 1)

                if active(X_ROT):
                    rotary()
                    add_bo()
                if active(X_STAT):
                    inv_std()
                if active(X_Y):
                    inv_std2()
                if active(X_ROT):
                    spread_k()

            pipeline(eng, step_x, NS, X_Y)

            with eng.Fori(0, LAYERS) as layer:
                base = layer * NS

                def step_l(t, p, active):
                    def copy_y():
                        g, b = base + t - L_PROJ, (p - L_PROJ) % 2
                        eng.wait_ge(y_in.sem, after(y_in, g))
                        eng.wait_ge(l_ht.sem, after(l_ht, g - 2))
                        settle(eng)
                        eng.tensor_copy(yb[:, b:b + 1, :], y_all[:, bass.ds(t - L_PROJ, 1), :]).then_inc(l_yb.sem, 1)

                    def rotary():
                        g, b = base + t - L_ROT, (p - L_ROT) % 2
                        H2 = DL // 2
                        eng.wait_ge(l_raw.sem, after(l_raw, g))
                        eng.wait_ge(l_add.sem, after(l_add, g - 2))
                        r = raw[:, b, :, :].rearrange("p a (h d) -> p a h d", d=DL)
                        w = t2[:, b, :, :].rearrange("p a (h d) -> p a h d", d=DL)
                        for dst, src in ((slice(0, H2), slice(H2, DL)), (slice(H2, DL), slice(0, H2))):
                            eng.tensor_tensor(w[:, :, :, dst], r[:, :, :, src],
                                              bc(tab[:, 1:4:2, dst].unsqueeze(2), [128, 2, HL, H2]), ALU.mult)\
                               .then_inc(l_t2.sem, 1)

                    def inv_norm():
                        g, b = base + t - L_ROT, (p - L_ROT) % 2
                        eng.wait_ge(l_ss.sem, after(l_ss, g))
                        settle(eng)
                        eng.tensor_scalar(ssc[:, :], ss[:, b, :], 1e-24, 1.0, ALU.max, ALU.mult).then_inc(l_ssc.sem, 1)
                        eng.wait_ge(l_ssc.sem, after(l_ssc, g))
                        eng.wait_ge(l_rot.sem, after(l_rot, g - 2))
                        eng.tensor_tensor(rn[:, b, :], ssc[:, :], nhalf[:, :], ALU.pow).then_inc(l_rn.sem, 1)

                    if active(L_PROJ):
                        copy_y()
                    if active(L_ROT):
                        rotary()
                        inv_norm()

                eng.wait_ge(tab_ready, (layer + 1) * 4)
                pipeline(eng, step_l, NS, L_WEIGH)

                def step_f(t, p, active):
                    def copy_y():
                        g, b = base + t - F_STAT, (p - F_STAT) % 2
                        eng.wait_ge(y_attn.sem, after(y_attn, g))
                        eng.wait_ge(f_norm.sem, after(f_norm, g - 2))
                        eng.wait_ge(f_sh.sem, after(f_sh, g - 2))
                        settle(eng)
                        eng.tensor_copy(yb[:, b:b + 1, :], y_all[:, bass.ds(t - F_STAT, 1), :]).then_inc(f_yb.sem, 1)

                    def inv_std():
                        g, b = base + t - F_STAT, (p - F_STAT) % 2
                        eng.wait_ge(f_ve.sem, after(f_ve, g))
                        eng.wait_ge(f_norm.sem, after(f_norm, g - 2))
                        eng.tensor_tensor(rstd[:, b, :], ve[:, b, :], nhalf[:, 0:1], ALU.pow).then_inc(f_rstd.sem, 1)

                    if active(F_STAT):
                        copy_y()
                        inv_std()

                pipeline(eng, step_f, NS, F_DOWN)


_INS = ["x", "ctx_1024", "L0_xattn_Wq", "L0_xattn_bq", "L0_xattn_Wk", "L0_xattn_bk", "L0_xattn_Wv", "L0_xattn_bv",
        "L0_xattn_Wo", "L0_xattn_bo", "L0_ffn_wqkv", "L0_ffn_q_scale", "L0_ffn_k_scale", "L0_ffn_wo", "L0_ffn_ln_g",
        "L0_ffn_ln_b", "L0_ffn_w1", "L0_ffn_b1", "L0_ffn_w2", "L0_ffn_b2"]


def constants(T, DX, HX, DL):
    import numpy as np

    f = np.float32
    ident = np.eye(128, dtype=f)
    shift = np.eye(128, k=1, dtype=f)
    i, j = np.arange(T)[:, None], np.arange(T)[None, :]
    band = np.where((i < j) | (i > j + 64), f(-1e30), f(0))
    t = np.arange(T, dtype=f)
    inv = (f(1.0) / f(10000.0) ** (np.arange(0, DX, 2, dtype=f) / f(DX))).astype(f)
    ang = t[:, None] * inv[None, :]
    ang = np.concatenate([ang, ang], axis=-1).astype(f)
    sign = np.concatenate([-np.ones(DX // 2, f), np.ones(DX // 2, f)])
    ropex = np.stack([np.cos(ang), np.sin(ang) * sign], axis=1)
    half = np.arange(0, DL, 2, dtype=f)
    inv = (f(1.0) / f(10000.0) ** (half / f(DL))).astype(f)
    ang = t[:, None] * inv[None, :]
    ang = np.concatenate([ang, ang], axis=-1).astype(f)
    base = (half + f(0.4 * DL)) / f(1.4 * DL)
    power = (t - f(T // 2)) / f(32.0)
    scale = (base[None, :] ** power[:, None]).astype(f)
    scale = np.concatenate([scale, scale], axis=-1)
    sign = np.concatenate([-np.ones(DL // 2, f), np.ones(DL // 2, f)])
    cos, sin = np.cos(ang), np.sin(ang) * sign
    ropel = np.stack([cos * scale, sin * scale, cos / scale, sin / scale], axis=1)
    hmask = (np.arange(128)[:, None] // DX == np.arange(HX)[None, :]).astype(f)
    return {"c_ident": ident, "c_shift": shift, "c_band": band, "c_ropex": ropex.astype(f),
            "c_ropel": ropel.astype(f), "c_hmask": hmask}


def kernel(**inputs):
    import numpy as np
    import concourse.bacc as bacc
    from concourse.bass_utils import run_bass_kernel_spmd

    nc = bacc.Bacc("TRN2", target_bir_lowering=False, num_devices=1)
    arrays = {name: np.ascontiguousarray(inputs[name]) for name in _INS}
    arrays.update({k: np.ascontiguousarray(v) for k, v in constants(128, 8, 16, 64).items()})
    ins = {name: nc.dram_tensor(name + "_dram", a.shape, mybir.dt.from_np(a.dtype), kind="ExternalInput").ap()
           for name, a in arrays.items()}
    out = nc.dram_tensor("out_dram", inputs["x"].shape, fp32, kind="ExternalOutput").ap()
    build(nc, ins, out)
    r = run_bass_kernel_spmd(nc, [{name + "_dram": a for name, a in arrays.items()}], core_ids=[0])
    return r.results[0]["out_dram"]
```

```python
from contextlib import ExitStack

import concourse.bass as bass
from concourse import mybir

fp32 = mybir.dt.float32
bf16 = mybir.dt.bfloat16
f32r = mybir.dt.float32r
i32 = mybir.dt.int32
HIGH_BITS = -4096
ALU = mybir.AluOpType
ACT = mybir.ActivationFunctionType
AX = mybir.AxisListType

LEAD = 4


class Signal:

    def __init__(self, sem, per):
        self.sem, self.per = sem, per


def after(signal, g, k=None):
    return (g + LEAD) * signal.per + (signal.per if k is None else k)


UNROLL = 4


def pipeline(eng, step, count, lags):
    head = -(-lags // UNROLL) * UNROLL
    for t in range(head):
        step(t, t % UNROLL, lambda lag, t=t: lag <= t)
    with eng.Fori(head // UNROLL, count // UNROLL) as turn:
        for n in range(UNROLL):
            step(UNROLL * turn + n, n, lambda lag: True)
    for t in range(count, count + lags):
        step(t, t % UNROLL, lambda lag, t=t: t - lag < count)


def build(nc, ins, out):
    x, ctx_in = ins["x"], ins["ctx_1024"]
    NS, T, D = x.shape
    HX, DX = 16, 8
    HL, DL = 8, 64
    LAYERS = ins["L0_ffn_wqkv"].shape[0]
    INNER = HL * DL
    HID = ins["L0_ffn_w2"].shape[1]
    NJ = (HID + 127) // 128
    REST = HID - 128 * (NJ - 1)
    CH = 4
    EPS = 1e-5
    SCALE_X = float(DX) ** -0.5
    SCALE_L = 8.0
    NG, GW, SLOTS = HX // 2, 2 * DX, 6
    KG = SLOTS * GW
    HIGH, MID, LOW = (slice(0, 3), slice(2, 5)), (slice(3, 6, 2), slice(0, 6, 5)), (4, 1)
    X_STAT, X_PROJ, X_ROT, X_PARTS, X_SCORE, X_WEIGH, X_OUT, X_Y = range(8)
    L_PROJ, L_ROT, L_SCORE, L_WEIGH, L_OUT = range(5)
    F_COPY, F_SHIFT, F_STAT, F_NORM, F_UP, F_DOWN = 0, 1, 2, 3, 5, 6

    with ExitStack() as ctx:
        def sb(name, shape, dt=fp32):
            return ctx.enter_context(nc.sbuf_tensor(name, shape, dt))

        def signal(name, per=1):
            return Signal(ctx.enter_context(nc.semaphore(name)), per)

        x_all = sb("x_all", [128, NS, D])
        y_all = sb("y_all", [128, NS, D])
        ident = sb("ident", [128, 128])
        identb = sb("identb", [128, 128], bf16)
        shiftm = sb("shiftm", [128, 128])
        bandm = sb("bandm", [128, CH * 128], bf16)
        ropex = sb("ropex", [128, 2, DX])
        ropel = sb("ropel", [128, 4, DL])
        scales = sb("scales", [128, 4, DL])
        tab = sb("tab", [128, 4, DL])
        gmask = sb("gmask", [128, 2])
        selin = sb("selin", [3 * HX, HX])
        sel = sb("sel", [3 * HX, HX, 128], bf16)
        nhalf = sb("nhalf", [128, 2 * HL])
        wx_in = sb("wx_in", [128, 4, D])
        wx = sb("wx", [128, 4, D])
        biasx = sb("biasx", [128, 3 * D])
        box = sb("box", [128, D])
        wqkv = sb("wqkv", [128, 3 * INNER])
        wol = sb("wol", [128, INNER // 128, D])
        w1 = sb("w1", [128, 2 * HID])
        w2 = sb("w2", [128, NJ, D])
        b1 = sb("b1", [128, 2, NJ])
        lgb = sb("lgb", [128, 2])
        ctxb = sb("ctxb", [128, 2, D])
        st = sb("st", [128, 2, 6])
        mv = sb("mv", [128, 2, 2])
        ve = sb("ve", [128, 2, 1])
        rstd = sb("rstd", [128, 2, 1])
        st2 = sb("st2", [128, 2, 6])
        mv2 = sb("mv2", [128, 2, 2])
        ve2 = sb("ve2", [128, 2, 1])
        rstd2 = sb("rstd2", [128, 2, 1])
        xn = sb("xn", [128, 2, D])
        hT = sb("hT", [128, 2, 2, 128])
        hhi = sb("hhi", [128, 128], i32)
        hr = sb("hr", [128, 2, 2, 128], f32r)
        whi = sb("whi", [128, 3 * INNER], i32)
        wr = sb("wr", [128, 2, 3 * INNER], f32r)
        raw = sb("raw", [128, 2, 2, INNER])
        sq = sb("sq", [128, 2 * INNER])
        ss = sb("ss", [128, 2, 2 * HL])
        ssc = sb("ssc", [128, 2 * HL])
        rn = sb("rn", [128, 2, 2 * HL])
        t1 = sb("t1", [128, 2, 2, INNER])
        t2 = sb("t2", [128, 2, 2, INNER])
        rot = sb("rot", [128, 2, 2 * INNER])
        qkT = sb("qkT", [128, 2, 2 * INNER])
        parts = sb("parts", [128, 2, 2, NG, SLOTS, GW], bf16)
        rest = sb("rest", [128, 2 * D])
        qx = sb("qx", [KG, 2, NG, 128], bf16)
        kx = sb("kx", [KG, 2, NG, 2, 128], bf16)
        topp = sb("topp", [128, 3, HX], bf16)
        topr = sb("topr", [128, HX])
        topT = sb("topT", [3 * HX, 128], bf16)
        vx = sb("vx", [128, 2, 2, HX // 2 * (128 + DX)])
        vdiag = vx[:, :, :, :].rearrange("p b s (i w) -> p b s i w", w=128 + DX)
        vl = sb("vl", [128, 2, HL, DL + 1])
        top = sb("top", [128, 2, HX])
        prob = sb("prob", [128, 2, HL, 128])
        probT = sb("probT", [128, HX, 128])
        rsum = sb("rsum", [128, HL])
        rsx = sb("rsx", [128, 128])
        ox = sb("ox", [128, 2, 128])
        o_sb = sb("o_sb", [128, INNER])
        oT = sb("oT", [128, INNER])
        yb = sb("yb", [128, UNROLL, D])
        gate = sb("gate", [128, 2, NJ, 128])
        hid = sb("hid", [128, 2, NJ, 128])
        ps = ctx.enter_context(nc.psum_tensor("ps", [128, 8, 512], fp32))

        S = lambda n: ctx.enter_context(nc.semaphore(n))
        shift_zero, const_in, wx_loaded = S("shift_zero"), S("const_in"), S("wx_loaded")
        setup_v, setup_p, setup_t, setup_e, setup_a = S("setup_v"), S("setup_p"), S("setup_t"), S("setup_e"), S("setup_a")
        x_in = [S("x_in0"), S("x_in1")]
        ctx_in_sem = [S("ctx_in0"), S("ctx_in1")]
        w_high, w_split = S("w_high"), S("w_split")
        wl_in, wf_in, tab_ready = S("wl_in"), S("wf_in"), S("tab_ready")
        out_add, out_add_p, out_done = S("out_add"), S("out_add_p"), S("out_done")
        settled = S("settled")
        x_stat, x_mv, x_ve, x_rstd, x_norm = (signal(n) for n in ("x_stat", "x_mv", "x_ve", "x_rstd", "x_norm"))
        x_tr, x_trc, x_proj, x_vproj = (signal(n) for n in ("x_tr", "x_trc", "x_proj", "x_vproj"))
        x_bias, x_v = signal("x_bias"), signal("x_v", 2)
        x_t, x_rot, x_bo = signal("x_t", 3), signal("x_rot"), signal("x_bo")
        x_hi, x_rest, x_mid, x_lo = signal("x_hi", 2), signal("x_rest"), signal("x_mid", 2), signal("x_lo", 2)
        x_qkt, x_qkc = signal("x_qkt", 4), signal("x_qkc", 4)
        x_s, x_max = signal("x_s", HX // CH), signal("x_max", HX // CH)
        x_topp, x_topt, x_toptc = signal("x_topp", 4), signal("x_topt"), signal("x_toptc")
        x_st, x_exp, x_pv = (signal(n, HX // CH) for n in ("x_st", "x_exp", "x_pv"))
        x_pvc, x_rsum, x_o, x_wo, x_res = signal("x_pvc", 4), signal("x_rsum"), signal("x_o"), signal("x_wo"), signal("x_res")
        x_stat2, x_mv2, x_ve2, x_rstd2 = (signal(n) for n in ("x_stat2", "x_mv2", "x_ve2", "x_rstd2"))
        y_in = signal("y_in")
        l_yb, l_ht, l_htc = signal("l_yb"), signal("l_ht"), signal("l_htc", 2)
        l_hh, l_hi, l_hr = signal("l_hh"), signal("l_hi"), signal("l_hr")
        l_qk, l_vp = signal("l_qk"), signal("l_vp")
        l_raw, l_sq, l_v, l_ss, l_ssc, l_rn = (signal(n) for n in ("l_raw", "l_sq", "l_v", "l_ss", "l_ssc", "l_rn"))
        l_t2, l_t1, l_add, l_rot = signal("l_t2", 2), signal("l_t1"), signal("l_add"), signal("l_rot")
        l_qkt, l_qktc = signal("l_qkt"), signal("l_qktc")
        l_s, l_max, l_sub, l_exp, l_pt, l_ptc, l_pv, l_rsum, l_o = (
            signal(n, HL // CH) for n in ("l_s", "l_max", "l_sub", "l_exp", "l_pt", "l_ptc", "l_pv", "l_rsum", "l_o"))
        l_ot, l_otc, l_wo = signal("l_ot"), signal("l_otc"), signal("l_wo")
        y_attn = signal("y_attn")
        f_yb, f_sh, f_shc = signal("f_yb"), signal("f_sh"), signal("f_shc")
        f_stat, f_mv, f_ve, f_rstd = (signal(n) for n in ("f_stat", "f_mv", "f_ve", "f_rstd"))
        f_norm, f_t, f_tc, f_w1 = signal("f_norm"), signal("f_t"), signal("f_tc"), signal("f_w1", 2)
        f_gate, f_hid, f_w2 = signal("f_gate", NJ), signal("f_hid", NJ), signal("f_w2")

        def begin(eng, *signals):
            for s in signals:
                eng.sem_inc(s.sem, LEAD * s.per)

        def rows(j):
            return 128 if j < NJ - 1 else REST

        def bc(ap, shape):
            return ap.to_broadcast(shape)

        def settle(eng):
            eng.sem_inc(settled, 1)

        block = ctx.enter_context(nc.Block())

        consts = [(shiftm[:, :], ins["c_shift"]),
                  (sq[:, 0:128], ins["c_band"]), (ropex[:, :, :], ins["c_ropex"]), (ropel[:, :, :], ins["c_ropel"]),
                  (gmask[:, :], ins["c_gmask"]), (selin[:, :], ins["c_sel"])]
        N_CONST = len(consts) + 4
        N_WL, N_WF_IN = 2 + 6, 4 + 2 * NJ + 2
        OUT_CHUNKS, OUT_GPSIMD = 8, 2
        N_SETUP_V, N_SETUP_P, N_SETUP_A = 3, 3, 3

        @block.sync
        def _(eng):
            eng.dma_start(ident[:, :], ins["c_ident"]).then_inc(wx_loaded, 16)
            for i, name in enumerate(("Wq", "Wk", "Wv", "Wo")):
                eng.dma_start(wx_in[:, i, :], ins["L0_xattn_" + name]).then_inc(wx_loaded, 16)
            def load(t, p):
                eng.dma_start(x_all[:, bass.ds(t, 1), :], x[bass.ds(t, 1), :, :].rearrange("s t d -> t s d"))\
                   .then_inc(x_in[p], 16)
                eng.dma_start(ctxb[:, p:p + 1, :], ctx_in[bass.ds(t, 1), :, :].rearrange("s t d -> t s d"))\
                   .then_inc(ctx_in_sem[p], 16)
            load(0, 0)
            load(1, 1)
            for dst, src in consts:
                eng.dma_start(dst, src).then_inc(const_in, 16)
            for i, name in enumerate(("bq", "bk", "bv")):
                eng.dma_start(biasx[:, i * D:(i + 1) * D],
                              ins["L0_xattn_" + name].partition_broadcast(128)).then_inc(const_in, 16)
            eng.dma_start(box[:, :], ins["L0_xattn_bo"].partition_broadcast(128)).then_inc(const_in, 16)
            with eng.Fori(1, NS // 2) as pair:
                for p in range(2):
                    t = 2 * pair + p
                    eng.wait_ge(x_in[p], 16 * pair)
                    settle(eng)
                    eng.wait_ge(ctx_in_sem[p], 16 * pair)
                    settle(eng)
                    eng.wait_ge(x_tr.sem, after(x_tr, t - 2))
                    settle(eng)
                    load(t, p)

            with eng.Fori(0, LAYERS) as layer:
                def of(name):
                    return ins["L0_ffn_" + name][bass.ds(layer, 1)]
                eng.wait_ge(l_qk.sem, after(l_qk, layer * NS - 1))
                settle(eng)
                eng.wait_ge(l_vp.sem, after(l_vp, layer * NS - 1))
                settle(eng)
                eng.wait_ge(l_wo.sem, after(l_wo, layer * NS - 1))
                settle(eng)
                eng.wait_ge(l_t1.sem, after(l_t1, layer * NS - 1))
                settle(eng)
                eng.dma_start(wqkv[:, :], of("wqkv").rearrange("a d n -> d (a n)")).then_inc(wl_in, 16)
                eng.dma_start(wol[:, :, :], of("wo").rearrange("a (c p) n -> p (a c) n", p=128)).then_inc(wl_in, 16)
                H2 = DL // 2
                for i, name in ((0, "q_scale"), (2, "k_scale")):
                    row = of(name).rearrange("a d -> (a d)")
                    eng.dma_start(scales[:, i, :], row.partition_broadcast(128)).then_inc(wl_in, 16)
                    eng.dma_start(scales[:, i + 1, 0:H2], row[H2:DL].partition_broadcast(128)).then_inc(wl_in, 16)
                    eng.dma_start(scales[:, i + 1, H2:DL], row[0:H2].partition_broadcast(128)).then_inc(wl_in, 16)
                eng.wait_ge(f_w1.sem, after(f_w1, layer * NS - 1))
                settle(eng)
                eng.wait_ge(f_w2.sem, after(f_w2, layer * NS - 1))
                settle(eng)
                eng.wait_ge(f_hid.sem, after(f_hid, layer * NS - 1))
                settle(eng)
                eng.wait_ge(f_tc.sem, after(f_tc, layer * NS - 1))
                settle(eng)
                eng.dma_start(w1[:, :], of("w1").rearrange("a d n -> d (a n)")).then_inc(wf_in, 16)
                w2row = of("w2").rearrange("a k n -> (a k) n")
                eng.dma_start(w2[:, 0:NJ - 1, :], w2row[0:128 * (NJ - 1), :].rearrange("(j p) n -> p j n", p=128))\
                   .then_inc(wf_in, 16)
                eng.dma_start(w2[0:REST, NJ - 1, :], w2row[128 * (NJ - 1):HID, :]).then_inc(wf_in, 16)
                eng.dma_start(w2[REST:REST + 1, NJ - 1, :], of("b2")).then_inc(wf_in, 16)
                b1row = of("b1").rearrange("a n -> (a n)")
                for half in range(2):
                    for j in range(NJ):
                        lo = half * HID + 128 * j
                        eng.dma_start(b1[0:rows(j), half, j:j + 1],
                                      b1row[lo:lo + rows(j)].rearrange("(n a) -> n a", a=1)).then_inc(wf_in, 16)
                for i, name in enumerate(("ln_g", "ln_b")):
                    eng.dma_start(lgb[:, i:i + 1], of(name).rearrange("a d -> d a")).then_inc(wf_in, 16)

            n = NS // OUT_CHUNKS
            for c in range(OUT_CHUNKS):
                if c < OUT_CHUNKS - OUT_GPSIMD:
                    eng.wait_ge(out_add, c + 1)
                else:
                    eng.wait_ge(out_add_p, c + 1 - (OUT_CHUNKS - OUT_GPSIMD))
                eng.dma_start(out[c * n:(c + 1) * n, :, :].rearrange("s t d -> t s d"),
                              x_all[:, c * n:(c + 1) * n, :]).then_inc(out_done, 16)
            eng.wait_ge(out_done, 16 * OUT_CHUNKS)

        @block.tensor
        def _(eng):
            begin(eng, x_tr, x_proj, x_vproj, x_qkt, x_s, x_topt, x_st, x_pv, x_wo,
                  l_ht, l_qk, l_vp, l_qkt, l_s, l_pt, l_pv, l_ot, l_wo, f_sh, f_t, f_w1, f_w2)
            eng.wait_ge(wx_loaded, 16 * 5)
            for i in range(4):
                mm = eng.transpose(ps[:, 0, i * 128:(i + 1) * 128], wx_in[:, i, :], ident[:, :])
            mm.then_inc(setup_t, 1)
            eng.wait_ge(setup_e, 1)

            def step_x(t, p, active):
                def bank1_read():
                    if active(X_ROT):
                        eng.wait_ge(x_bias.sem, after(x_bias, t - X_ROT))
                    if active(X_SCORE):
                        eng.wait_ge(x_v.sem, after(x_v, t - X_SCORE))
                    if active(X_Y):
                        eng.wait_ge(x_res.sem, after(x_res, t - X_Y))

                def project_v():
                    g, b = t - X_PARTS, (p - X_PARTS) % 2
                    bank1_read()
                    eng.wait_ge(x_trc.sem, after(x_trc, g))
                    eng.matmul(ps[:, 1, 256:384], hT[:, b, 1, :], wx[:, 2, :], start=True, stop=True)\
                       .then_inc(x_vproj.sem, 1)

                def project_out():
                    g = t - X_OUT
                    bank1_read()
                    eng.wait_ge(x_o.sem, after(x_o, g))
                    eng.matmul(ps[:, 1, 384:512], oT[:, 0:128], wx[:, 3, :], start=True, stop=True)\
                       .then_inc(x_wo.sem, 1)

                def project_in():
                    g, b = t - X_PROJ, (p - X_PROJ) % 2
                    bank1_read()
                    eng.wait_ge(x_norm.sem, after(x_norm, g))
                    eng.wait_ge(ctx_in_sem[b], 8 * (g - b + 2))
                    eng.transpose(ps[:, 1, 0:128], xn[:, b, :], ident[:, :])
                    eng.transpose(ps[:, 1, 128:256], ctxb[:, b, :], ident[:, :]).then_inc(x_tr.sem, 1)

                def project_qk():
                    g, b = t - X_PROJ, (p - X_PROJ) % 2
                    eng.wait_ge(x_trc.sem, after(x_trc, g))
                    eng.matmul(ps[:, 1, 0:128], hT[:, b, 0, :], wx[:, 0, :], start=True, stop=True)
                    eng.matmul(ps[:, 1, 128:256], hT[:, b, 1, :], wx[:, 1, :], start=True, stop=True)\
                       .then_inc(x_proj.sem, 1)

                def parts_T(i):
                    g, b = t - X_PARTS, (p - X_PARTS) % 2
                    eng.wait_ge(x_lo.sem, after(x_lo, g))
                    eng.wait_ge(setup_a, N_SETUP_A)
                    eng.wait_ge(x_qkc.sem, after(x_qkc, g - 1, i + 3))
                    for n in range(4):
                        mm = eng.matmul(ps[0:KG, 2 + i % 2, n * 128:(n + 1) * 128],
                                        parts[:, b, i // 2, (i % 2) * 4 + n, :, :].rearrange("p s d -> p (s d)"),
                                        identb[:, :], start=True, stop=True)
                    mm.then_inc(x_qkt.sem, 1)

                def scores(c):
                    g, b = t - X_SCORE, (p - X_SCORE) % 2
                    eng.wait_ge(x_qkc.sem, after(x_qkc, g, 3 + c // 2))
                    eng.wait_ge(x_max.sem, after(x_max, g - 1, c + 3))
                    for n in range(2):
                        mm = eng.matmul(ps[:, 4 + c % 2, n * 256:(n + 1) * 256], qx[:, b, 2 * c + n, :],
                                        kx[:, b, 2 * c + n, :, :].rearrange("p a b -> p (a b)"), start=True, stop=True)
                    mm.then_inc(x_s.sem, 1)

                def maxima_T():
                    g = t - X_SCORE
                    eng.wait_ge(x_topp.sem, after(x_topp, g))
                    eng.wait_ge(x_exp.sem, after(x_exp, g - 1))
                    eng.matmul(ps[0:3 * HX, 0, 0:128], topp[:, :, :].rearrange("p s h -> p (s h)"), identb[:, :],
                               start=True, stop=True).then_inc(x_topt.sem, 1)

                def scores_T(c):
                    g, b = t - X_WEIGH, (p - X_WEIGH) % 2
                    if c == 0:
                        eng.wait_ge(x_toptc.sem, after(x_toptc, g))
                    if c < HX // CH:
                        eng.wait_ge(x_exp.sem, after(x_exp, g - 1, c + 3))
                    if c > 1:
                        eng.wait_ge(x_exp.sem, after(x_exp, g, c - 1))
                    if c == 2:
                        eng.wait_ge(x_v.sem, after(x_v, g))
                        eng.wait_ge(x_pvc.sem, after(x_pvc, g - 1))
                    for i in range(CH):
                        h, hv = c * CH + i, (c - 2) * CH + i
                        if c < HX // CH:
                            dst = ps[:, 6 * (1 - c % 2), i * 128:(i + 1) * 128]
                            eng.matmul(dst, sel[:, h, :], topT[:, :], start=True, stop=False)
                            st = eng.matmul(dst, kx[:, b, h // 2, h % 2, :], qx[:, b, h // 2, :],
                                            start=False, stop=True)
                            if i == CH - 1:
                                st.then_inc(x_st.sem, 1)
                        if c > 1:
                            s, n = hv // (HX // 2), hv % (HX // 2)
                            pv = eng.matmul(ps[:, 7, s * 128:(s + 1) * 128],
                                            vx[:, b, s, n * 128:(n + 1) * 128], probT[:, hv, :],
                                            start=(n == 0), stop=(n == HX // 2 - 1))
                            if i == CH - 1:
                                pv.then_inc(x_pv.sem, 1)

                if active(X_WEIGH):
                    scores_T(0)
                if active(X_SCORE):
                    scores(0)
                if active(X_WEIGH):
                    scores_T(1)
                if active(X_SCORE):
                    scores(1)
                if active(X_WEIGH):
                    scores_T(2)
                if active(X_SCORE):
                    scores(2)
                if active(X_WEIGH):
                    scores_T(3)
                if active(X_SCORE):
                    scores(3)
                if active(X_PARTS):
                    parts_T(0)
                    parts_T(1)
                if active(X_WEIGH):
                    scores_T(4)
                if active(X_PARTS):
                    project_v()
                if active(X_OUT):
                    project_out()
                if active(X_PROJ):
                    project_in()
                if active(X_PARTS):
                    parts_T(2)
                    parts_T(3)
                if active(X_WEIGH):
                    scores_T(5)
                if active(X_SCORE):
                    maxima_T()
                if active(X_PROJ):
                    project_qk()

            pipeline(eng, step_x, NS, X_Y)

            with eng.Fori(0, LAYERS) as layer:
                base = layer * NS

                def step_l(t, p, active):
                    def tokens_T():
                        g, b = base + t - L_PROJ, (p - L_PROJ) % 2
                        eng.wait_ge(l_yb.sem, after(l_yb, g))
                        eng.wait_ge(l_htc.sem, after(l_htc, g - 1))
                        if active(L_OUT + 1):
                            eng.wait_ge(y_attn.sem, after(y_attn, g - L_OUT - 1))
                        eng.transpose(ps[:, 0, 0:128], yb[:, b, :], ident[:, :]).then_inc(l_ht.sem, 1)

                    def project(dst, b, c):
                        w = slice(c * INNER, (c + 1) * INNER)
                        eng.matmul(dst, hr[:, b, 0, :], wr[:, 0, w], start=True, stop=False)
                        eng.matmul(dst, hr[:, b, 0, :], wr[:, 1, w], start=False, stop=False)
                        return eng.matmul(dst, hr[:, b, 1, :], wr[:, 0, w], start=False, stop=True)

                    def project_qk():
                        g, b = base + t - L_PROJ, (p - L_PROJ) % 2
                        eng.wait_ge(l_hr.sem, after(l_hr, g))
                        eng.wait_ge(l_hi.sem, after(l_hi, g))
                        eng.wait_ge(l_sq.sem, after(l_sq, g - 1))
                        if not active(L_ROT):
                            eng.wait_ge(w_split, (layer + 1) * 2)
                        for c in range(2):
                            mm = project(ps[:, 1 + c, :], b, c)
                        mm.then_inc(l_qk.sem, 1)

                    def project_v():
                        g, b = base + t - L_ROT, (p - L_ROT) % 2
                        eng.wait_ge(l_hr.sem, after(l_hr, g))
                        eng.wait_ge(l_hi.sem, after(l_hi, g))
                        eng.wait_ge(l_v.sem, after(l_v, g - 1))
                        eng.wait_ge(l_otc.sem, after(l_otc, g - 3))
                        project(ps[:, 3, :], b, 2).then_inc(l_vp.sem, 1)

                    def qk_T():
                        g, b = base + t - L_SCORE, (p - L_SCORE) % 2
                        eng.wait_ge(l_rot.sem, after(l_rot, g))
                        eng.wait_ge(l_sub.sem, after(l_sub, g - 1))
                        for i in range(2 * INNER // 128):
                            mm = eng.transpose(ps[:, 4 + i // 4, (i % 4) * 128:(i % 4 + 1) * 128],
                                               rot[:, b, i * 128:(i + 1) * 128], ident[:, :])
                        mm.then_inc(l_qkt.sem, 1)

                    def scores():
                        g, b = base + t - L_SCORE, (p - L_SCORE) % 2
                        eng.wait_ge(l_qktc.sem, after(l_qktc, g))
                        for c in range(2):
                            eng.matmul(ps[:, 4 + c, :], identb[:, :], bandm[:, :], start=True, stop=True)
                        for h in range(HL):
                            r, c, s = DL * (h % 2), h % 2, h // 2
                            q = qkT[r:r + DL, b, s * 128:(s + 1) * 128]
                            k = qkT[r:r + DL, b, INNER + s * 128:INNER + (s + 1) * 128]
                            mm = eng.matmul(ps[:, 4 + c, s * 128:(s + 1) * 128], q, k,
                                            start=False, stop=True, skip_group_check=True)
                            if s == CH - 1:
                                mm.then_inc(l_s.sem, 1)

                    def prob_T(c):
                        g, b = base + t - L_WEIGH, (p - L_WEIGH) % 2
                        eng.wait_ge(l_exp.sem, after(l_exp, g, c + 1))
                        eng.wait_ge(l_o.sem, after(l_o, g - 1, c + 1))
                        for h in range(c * CH, (c + 1) * CH):
                            mm = eng.transpose(ps[:, 6 + c, (h % CH) * 128:(h % CH + 1) * 128],
                                               prob[:, b, h, :], ident[:, :])
                        mm.then_inc(l_pt.sem, 1)

                    def weigh(c):
                        g, b = base + t - L_WEIGH, (p - L_WEIGH) % 2
                        eng.wait_ge(l_ptc.sem, after(l_ptc, g, c + 1))
                        if c == 0:
                            eng.wait_ge(l_v.sem, after(l_v, g))
                        for s in range(CH):
                            mm = eng.matmul(ps[:, 6 + c, s * (DL + 1):(s + 1) * (DL + 1)],
                                            probT[:, c * CH + s, :], vl[:, b, 2 * s + c, :], start=True, stop=True)
                        mm.then_inc(l_pv.sem, 1)

                    def o_T():
                        g = base + t - L_OUT
                        eng.wait_ge(l_o.sem, after(l_o, g))
                        if active(L_SCORE):
                            eng.wait_ge(l_v.sem, after(l_v, g + 2))
                        for i in range(INNER // 128):
                            mm = eng.transpose(ps[:, 3, i * 128:(i + 1) * 128],
                                               o_sb[:, i * 128:(i + 1) * 128], ident[:, :])
                        mm.then_inc(l_ot.sem, 1)

                    def project_out():
                        g = base + t - L_OUT
                        eng.wait_ge(l_otc.sem, after(l_otc, g))
                        eng.wait_ge(y_attn.sem, after(y_attn, g - 1))
                        if active(L_PROJ):
                            eng.wait_ge(l_htc.sem, after(l_htc, g + L_OUT))
                        NB = INNER // 128
                        for i in range(NB):
                            mm = eng.matmul(ps[:, 0, 128:256], oT[:, i * 128:(i + 1) * 128], wol[:, i, :],
                                            start=(i == 0), stop=(i == NB - 1))
                        mm.then_inc(l_wo.sem, 1)

                    if active(L_SCORE):
                        qk_T()
                    if active(L_WEIGH):
                        prob_T(0)
                    if active(L_PROJ):
                        tokens_T()
                    if active(L_WEIGH):
                        prob_T(1)
                    if active(L_OUT):
                        o_T()
                    if active(L_SCORE):
                        scores()
                    if active(L_PROJ):
                        project_qk()
                    if active(L_WEIGH):
                        weigh(0)
                        weigh(1)
                    if active(L_OUT):
                        project_out()
                    if active(L_ROT):
                        project_v()

                eng.wait_ge(wl_in, (layer + 1) * (16 * N_WL))
                pipeline(eng, step_l, NS, L_OUT)

                def step_f(t, p, active):
                    def shift():
                        g, b = base + t - F_SHIFT, (p - F_SHIFT) % UNROLL
                        eng.wait_ge(f_yb.sem, after(f_yb, g))
                        eng.wait_ge(f_shc.sem, after(f_shc, g - 1))
                        eng.matmul(ps[:, 0, 0:D // 2], shiftm[:, :], yb[:, b, D // 2:D], start=True, stop=True)\
                           .then_inc(f_sh.sem, 1)

                    def tokens_T():
                        g, b = base + t - F_NORM, (p - F_NORM) % 2
                        eng.wait_ge(f_norm.sem, after(f_norm, g))
                        eng.wait_ge(f_tc.sem, after(f_tc, g - 1))
                        eng.transpose(ps[:, 1, 0:128], xn[:, b, :], ident[:, :]).then_inc(f_t.sem, 1)

                    def expand():
                        g, b = base + t - F_UP, (p - F_UP) % 2
                        eng.wait_ge(f_tc.sem, after(f_tc, g))
                        eng.wait_ge(f_hid.sem, after(f_hid, g - 2))
                        for half, bank in ((1, 3 + 4 * b), (0, 2 + 4 * b)):
                            for j in range(NJ):
                                lo = half * HID + 128 * j
                                mm = eng.matmul(ps[0:rows(j), bank, j * 128:(j + 1) * 128],
                                                w1[:, lo:lo + rows(j)], hT[:, b, 0, :], start=True, stop=True)
                            mm.then_inc(f_w1.sem, 1)

                    def contract():
                        g, b = base + t - F_DOWN, (p - F_DOWN) % 2
                        eng.wait_ge(f_hid.sem, after(f_hid, g))
                        eng.wait_ge(y_in.sem, after(y_in, g + NS - 1))
                        for j in range(NJ):
                            k = rows(j) + (j == NJ - 1)
                            mm = eng.matmul(ps[:, 4, 0:128], hid[0:k, b, j, :], w2[0:k, j, :],
                                            start=(j == 0), stop=(j == NJ - 1))
                        mm.then_inc(f_w2.sem, 1)

                    if active(F_SHIFT):
                        shift()
                    if active(F_UP):
                        expand()
                    if active(F_DOWN):
                        contract()
                    if active(F_NORM):
                        tokens_T()

                eng.wait_ge(wf_in, (layer + 1) * (16 * N_WF_IN))
                eng.wait_ge(y_attn.sem, after(y_attn, base + NS - 1))
                pipeline(eng, step_f, NS, F_DOWN)

        @block.scalar
        def _(eng):
            begin(eng, x_trc, x_hi, x_qkc, x_toptc, x_exp, x_pvc, l_htc, l_hi, l_raw, l_sq, l_v, l_qktc, l_exp, l_ptc, l_otc,
                  f_shc, f_tc, f_gate)
            eng.wait_ge(setup_t, 1)
            eng.activation(wx[:, :, :].rearrange("p a b -> p (a b)"), ps[:, 0, :], ACT.Copy).then_inc(setup_e, 1)

            def step_x(t, p, active):
                def tokens_T():
                    g, b = t - X_PROJ, (p - X_PROJ) % 2
                    eng.wait_ge(x_tr.sem, after(x_tr, g))
                    eng.wait_ge(x_proj.sem, after(x_proj, g - 2))
                    eng.wait_ge(x_vproj.sem, after(x_vproj, g - 2))
                    eng.activation(hT[:, b, :, :].rearrange("p a b -> p (a b)"), ps[:, 1, 0:256], ACT.Copy)\
                       .then_inc(x_trc.sem, 1)

                def high_parts(i):
                    g, b = t - X_ROT, (p - X_ROT) % 2
                    eng.wait_ge(x_rot.sem, after(x_rot, g))
                    eng.wait_ge(x_qkt.sem, after(x_qkt, g - 2))
                    eng.activation(parts[:, b, i, :, HIGH[i], :],
                                   bc(rot[:, b, i * D:(i + 1) * D].rearrange("p (g d) -> p g d", d=GW).unsqueeze(2),
                                      [128, NG, 3, GW]), ACT.Copy).then_inc(x_hi.sem, 1)

                def parts_T(i, lag=X_PARTS):
                    g, b = t - lag, (p - lag) % 2
                    eng.wait_ge(x_qkt.sem, after(x_qkt, g, i + 1))
                    eng.wait_ge(x_st.sem, after(x_st, g - 2))
                    src = ps[0:KG, 2 + i % 2, :].rearrange("p (g t) -> p g t", t=128)
                    if i < 2:
                        eng.activation(qx[:, b, 4 * i:4 * i + 4, :], src, ACT.Copy).then_inc(x_qkc.sem, 1)
                    else:
                        n = 4 * (i - 2)
                        eng.activation(kx[:, b, n:n + 4, 0, :], src, ACT.Copy, scale=gmask[0:KG, 0:1])
                        eng.activation(kx[:, b, n:n + 4, 1, :], src, ACT.Copy, scale=gmask[0:KG, 1:2])\
                           .then_inc(x_qkc.sem, 1)

                def maxima_T():
                    g = t - X_SCORE
                    eng.wait_ge(x_topt.sem, after(x_topt, g))
                    eng.wait_ge(x_st.sem, after(x_st, g - 1))
                    eng.activation(topT[:, :], ps[0:3 * HX, 0, 0:128], ACT.Copy).then_inc(x_toptc.sem, 1)

                def exps(c):
                    g = t - X_WEIGH
                    eng.wait_ge(x_st.sem, after(x_st, g, c + 1))
                    eng.wait_ge(x_pv.sem, after(x_pv, g - 1, c + 1))
                    eng.activation(probT[:, c * CH:(c + 1) * CH, :].rearrange("p a b -> p (a b)"),
                                   ps[:, 6 * (1 - c % 2), :], ACT.Exp, scale=SCALE_X).then_inc(x_exp.sem, 1)

                def outputs():
                    g = t - X_WEIGH
                    eng.wait_ge(x_pv.sem, after(x_pv, g))
                    eng.wait_ge(x_o.sem, after(x_o, g - 1))
                    for s in range(2):
                        own, other = slice(64 * s, 64 * (s + 1)), slice(64 * (1 - s), 64 * (2 - s))
                        for i, part in enumerate((own, other)):
                            eng.activation(ox[own, i, :], ps[part, 7, s * 128:(s + 1) * 128], ACT.Copy)\
                               .then_inc(x_pvc.sem, 1)

                def constants_in_bf16():
                    eng.wait_ge(const_in, 16 * N_CONST)
                    eng.activation(identb[:, :], ident[:, :], ACT.Copy).then_inc(setup_a, 1)
                    eng.activation(sel[:, :, :], bc(selin[:, :].unsqueeze(2), [3 * HX, HX, 128]), ACT.Copy).then_inc(setup_a, 1)
                    eng.activation(bandm[:, :].rearrange("p (a b) -> p a b", a=CH),
                                   bc(sq[:, 0:128].unsqueeze(1), [128, CH, 128]), ACT.Copy).then_inc(setup_a, 1)

                if active(X_WEIGH):
                    exps(0)
                    exps(1)
                if active(X_SCORE):
                    parts_T(3, X_SCORE)
                if active(X_WEIGH):
                    exps(2)
                if active(X_ROT):
                    high_parts(0)
                    high_parts(1)
                if active(X_WEIGH):
                    exps(3)
                if active(X_PARTS):
                    parts_T(0)
                    parts_T(1)
                if active(X_PROJ):
                    tokens_T()
                if active(X_PROJ) and not active(X_ROT):
                    constants_in_bf16()
                if active(X_PARTS):
                    parts_T(2)
                if active(X_SCORE):
                    maxima_T()
                if active(X_WEIGH):
                    outputs()

            pipeline(eng, step_x, NS, X_Y)

            with eng.Fori(0, LAYERS) as layer:
                base = layer * NS

                def step_l(t, p, active):
                    def tokens_T():
                        g, b = base + t - L_PROJ, (p - L_PROJ) % 2
                        eng.wait_ge(l_ht.sem, after(l_ht, g))
                        eng.wait_ge(l_hr.sem, after(l_hr, g - 2))
                        H = D // 2
                        eng.activation(hT[0:H, b, 0, :], ps[0:H, 0, 0:128], ACT.Copy).then_inc(l_htc.sem, 1)
                        eng.activation(hT[H:D, b, 0, 1:128], ps[H:D, 0, 0:127], ACT.Copy).then_inc(l_htc.sem, 1)

                    def prob_T(c):
                        g = base + t - L_WEIGH
                        eng.wait_ge(l_pt.sem, after(l_pt, g, c + 1))
                        eng.wait_ge(l_pv.sem, after(l_pv, g - 1, c + 1))
                        eng.activation(probT[:, c * CH:(c + 1) * CH, :].rearrange("p a b -> p (a b)"),
                                       ps[:, 6 + c, :], ACT.Copy).then_inc(l_ptc.sem, 1)

                    def high_part():
                        g, b = base + t - L_PROJ, (p - L_PROJ) % 2
                        eng.wait_ge(l_hh.sem, after(l_hh, g))
                        eng.wait_ge(l_vp.sem, after(l_vp, g - 2))
                        eng.activation(hr[:, b, 0, :], hhi[:, :].bitcast(fp32), ACT.Copy).then_inc(l_hi.sem, 1)

                    def raw_qk():
                        g, b = base + t - L_PROJ, (p - L_PROJ) % 2
                        eng.wait_ge(l_qk.sem, after(l_qk, g))
                        eng.wait_ge(l_t1.sem, after(l_t1, g - 2))
                        eng.wait_ge(l_t2.sem, after(l_t2, g - 2))
                        eng.activation(raw[:, b, :, :].rearrange("p a b -> p (a b)"),
                                       ps[:, 1:3, :].rearrange("p a b -> p (a b)"), ACT.Copy).then_inc(l_raw.sem, 1)

                    def square_qk():
                        g = base + t - L_PROJ
                        eng.wait_ge(l_ss.sem, after(l_ss, g - 1))
                        eng.activation(sq[:, :], ps[:, 1:3, :].rearrange("p a b -> p (a b)"), ACT.Square)\
                           .then_inc(l_sq.sem, 1)

                    def value():
                        g, b = base + t - L_ROT, (p - L_ROT) % 2
                        eng.wait_ge(l_vp.sem, after(l_vp, g))
                        eng.wait_ge(l_pv.sem, after(l_pv, g - 2))
                        eng.activation(vl[:, b, :, 0:DL], ps[:, 3, :].rearrange("p (h d) -> p h d", d=DL), ACT.Copy)\
                           .then_inc(l_v.sem, 1)

                    def qk_T():
                        g, b = base + t - L_SCORE, (p - L_SCORE) % 2
                        eng.wait_ge(l_qkt.sem, after(l_qkt, g))
                        eng.wait_ge(l_s.sem, after(l_s, g - 2))
                        eng.activation(qkT[:, b, :], ps[:, 4:6, :].rearrange("p a b -> p (a b)"), ACT.Copy)\
                           .then_inc(l_qktc.sem, 1)

                    def exps(c):
                        g, b = base + t - L_SCORE, (p - L_SCORE) % 2
                        eng.wait_ge(l_sub.sem, after(l_sub, g, c + 1))
                        s = prob[:, b, c * CH:(c + 1) * CH, :].rearrange("p a b -> p (a b)")
                        eng.activation(s, s, ACT.Exp, scale=SCALE_L).then_inc(l_exp.sem, 1)

                    def o_T():
                        g = base + t - L_OUT
                        eng.wait_ge(l_ot.sem, after(l_ot, g))
                        eng.wait_ge(l_wo.sem, after(l_wo, g - 1))
                        eng.activation(oT[:, :], ps[:, 3, :], ACT.Copy).then_inc(l_otc.sem, 1)

                    if active(L_SCORE):
                        qk_T()
                    if active(L_PROJ):
                        tokens_T()
                    if active(L_WEIGH):
                        prob_T(0)
                        prob_T(1)
                    if active(L_OUT):
                        o_T()
                    if active(L_PROJ):
                        high_part()
                        raw_qk()
                        square_qk()
                    if active(L_SCORE):
                        exps(0)
                        exps(1)
                    if active(L_ROT):
                        value()

                eng.wait_ge(w_high, layer + 1)
                eng.activation(wr[:, 0, :], whi[:, :].bitcast(fp32), ACT.Copy).then_inc(w_split, 1)
                eng.wait_ge(shift_zero, layer + 1)
                pipeline(eng, step_l, NS, L_OUT)

                def step_f(t, p, active):
                    def shifted():
                        g, b = base + t - F_SHIFT, (p - F_SHIFT) % UNROLL
                        eng.wait_ge(f_sh.sem, after(f_sh, g))
                        eng.activation(yb[:, b, D // 2:D], ps[:, 0, 0:D // 2], ACT.Copy).then_inc(f_shc.sem, 1)

                    def tokens_T():
                        g, b = base + t - F_NORM, (p - F_NORM) % 2
                        eng.wait_ge(f_t.sem, after(f_t, g))
                        eng.wait_ge(f_w1.sem, after(f_w1, g - 2))
                        eng.activation(hT[:, b, 0, :], ps[:, 1, 0:128], ACT.Identity, scale=lgb[:, 0:1],
                                       bias=lgb[:, 1:2]).then_inc(f_tc.sem, 1)

                    def gates():
                        g, b = base + t - F_UP, (p - F_UP) % 2
                        eng.wait_ge(f_w1.sem, after(f_w1, g, 1))
                        eng.wait_ge(f_hid.sem, after(f_hid, g - 2))
                        for j in range(NJ):
                            eng.activation(gate[0:rows(j), b, j, :], ps[0:rows(j), 3 + 4 * b, j * 128:(j + 1) * 128],
                                           ACT.Gelu, bias=b1[0:rows(j), 1, j:j + 1]).then_inc(f_gate.sem, 1)

                    if active(F_SHIFT):
                        shifted()
                    if active(F_UP):
                        gates()
                    if active(F_NORM):
                        tokens_T()

                eng.wait_ge(wf_in, (layer + 1) * (16 * N_WF_IN))
                pipeline(eng, step_f, NS, F_DOWN)

        @block.vector
        def _(eng):
            begin(eng, x_stat, x_mv, x_ve, x_norm, x_bias, x_v, x_rot, x_rest, x_mid, x_lo, x_max, x_rsum, x_o, x_res,
                  x_stat2, x_mv2, x_ve2, y_in, l_hh, l_hr, l_ss, l_t1, l_add, l_rot, l_max, l_sub, l_rsum, l_o, y_attn,
                  f_stat, f_mv, f_ve, f_norm, f_hid)
            eng.memset(nhalf[:, :], -0.5).then_inc(setup_v, 1)
            eng.memset(vl[:, :, :, DL:DL + 1], 1.0).then_inc(setup_v, 1)
            eng.memset(hid[:, :, NJ - 1, :], 1.0).then_inc(setup_v, 1)

            def step_x(t, p, active):
                def stats(k):
                    g, b = t - X_STAT, (p - X_STAT) % 2
                    if k == 0:
                        eng.wait_ge(x_in[b], 8 * (g - b + 2))
                        settle(eng)
                        eng.bn_stats(st[:, b, :], x_all[:, bass.ds(t, 1), :]).then_inc(x_stat.sem, 1)
                    if k == 1:
                        eng.wait_ge(x_stat.sem, after(x_stat, g))
                        settle(eng)
                        eng.bn_aggr(mv[:, b, :], st[:, b, :]).then_inc(x_mv.sem, 1)
                    if k == 2:
                        eng.wait_ge(x_mv.sem, after(x_mv, g))
                        eng.wait_ge(x_rstd.sem, after(x_rstd, g - 2))
                        eng.tensor_scalar(ve[:, b, :], mv[:, b, 1:2], EPS, None, ALU.add).then_inc(x_ve.sem, 1)

                def normalise():
                    g, b = t - X_PROJ, (p - X_PROJ) % 2
                    eng.wait_ge(x_rstd.sem, after(x_rstd, g))
                    eng.wait_ge(x_tr.sem, after(x_tr, g - 2))
                    eng.tensor_scalar(xn[:, b, :].unsqueeze(1), x_all[:, bass.ds(g, 1), :], mv[:, b, 0:1],
                                      rstd[:, b, :], ALU.subtract, ALU.mult).then_inc(x_norm.sem, 1)

                def bank1_written():
                    if active(X_PROJ):
                        eng.wait_ge(x_proj.sem, after(x_proj, t - X_PROJ))
                    else:
                        eng.wait_ge(x_wo.sem, after(x_wo, t - X_OUT))

                def bias_qk():
                    g = t - X_PROJ
                    eng.wait_ge(const_in, 16 * N_CONST)
                    bank1_written()
                    eng.wait_ge(x_t.sem, after(x_t, g - 1))
                    eng.tensor_tensor(raw[:, 0, 0, 0:256], ps[:, 1, 0:256], biasx[:, 0:256], ALU.add)\
                       .then_inc(x_bias.sem, 1)

                def bias_v():
                    g, b = t - X_PARTS, (p - X_PARTS) % 2
                    bank1_written()
                    eng.wait_ge(setup_p, N_SETUP_P)
                    eng.wait_ge(x_vproj.sem, after(x_vproj, g))
                    eng.wait_ge(x_pv.sem, after(x_pv, g - 2))
                    for s in range(2):
                        lo = 64 * s
                        eng.tensor_tensor(vdiag[:, b, s, :, lo:lo + DX],
                                          ps[:, 1, 256 + lo:320 + lo].rearrange("p (h d) -> p h d", d=DX),
                                          biasx[:, 256 + lo:320 + lo].rearrange("p (h d) -> p h d", d=DX), ALU.add)\
                           .then_inc(x_v.sem, 1)

                def rotate():
                    g, b = t - X_ROT, (p - X_ROT) % 2
                    eng.wait_ge(x_t.sem, after(x_t, g))
                    eng.wait_ge(x_rest.sem, after(x_rest, g - 2))
                    eng.tensor_tensor(rot[:, b, 0:256], t1[:, b, 0, 0:256], t2[:, b, 0, 0:256], ALU.add)\
                       .then_inc(x_rot.sem, 1)

                def remainder():
                    g, b = t - X_ROT, (p - X_ROT) % 2
                    eng.wait_ge(x_hi.sem, after(x_hi, g))
                    eng.wait_ge(x_lo.sem, after(x_lo, g - 1))
                    eng.tensor_tensor(rest[:, :].rearrange("p (a g d) -> p a g d", a=2, d=GW),
                                      rot[:, b, 0:256].rearrange("p (a g d) -> p a g d", a=2, d=GW),
                                      parts[:, b, :, :, 2, :], ALU.subtract).then_inc(x_rest.sem, 1)

                def middle_parts(i):
                    g, b = t - X_ROT, (p - X_ROT) % 2
                    eng.wait_ge(x_rest.sem, after(x_rest, g))
                    eng.tensor_copy(parts[:, b, i, :, MID[i], :],
                                    bc(rest[:, i * D:(i + 1) * D].rearrange("p (g d) -> p g d", d=GW).unsqueeze(2),
                                       [128, NG, 2, GW])).then_inc(x_mid.sem, 1)

                def low_parts(i):
                    g, b = t - X_ROT, (p - X_ROT) % 2
                    eng.wait_ge(x_mid.sem, after(x_mid, g, i + 1))
                    eng.tensor_tensor(parts[:, b, i, :, LOW[i], :],
                                      rest[:, i * D:(i + 1) * D].rearrange("p (g d) -> p g d", d=GW),
                                      parts[:, b, i, :, 5, :], ALU.subtract).then_inc(x_lo.sem, 1)

                def maxima(c):
                    g, b = t - X_SCORE, (p - X_SCORE) % 2
                    eng.wait_ge(x_s.sem, after(x_s, g, c + 1))
                    if c == 0:
                        eng.wait_ge(x_topp.sem, after(x_topp, g - 2))
                    eng.tensor_reduce(top[:, b, c * CH:(c + 1) * CH],
                                      ps[:, 4 + c % 2, :].rearrange("p (h k) -> p h k", k=128), AX.X, ALU.max)\
                       .then_inc(x_max.sem, 1)

                def inv_sums():
                    g = t - X_OUT
                    eng.wait_ge(x_pvc.sem, after(x_pvc, g))
                    eng.wait_ge(x_o.sem, after(x_o, g - 1))
                    eng.reciprocal(rsx[:, :], ox[:, 1, :]).then_inc(x_rsum.sem, 1)

                def o_norm():
                    g = t - X_OUT
                    eng.wait_ge(x_rsum.sem, after(x_rsum, g))
                    eng.wait_ge(x_wo.sem, after(x_wo, g - 1))
                    eng.tensor_tensor(oT[:, 0:128], ox[:, 0, :], rsx[:, :], ALU.mult).then_inc(x_o.sem, 1)

                def residual():
                    g = t - X_OUT
                    bank1_written()
                    eng.wait_ge(x_wo.sem, after(x_wo, g))
                    eng.wait_ge(x_bo.sem, after(x_bo, g))
                    xi = x_all[:, bass.ds(g, 1), :]
                    eng.tensor_tensor(xi, ps[:, 1, 384:512].unsqueeze(1), xi, ALU.add).then_inc(x_res.sem, 1)

                def stats2(k):
                    g, b = t - X_Y, (p - X_Y) % 2
                    if k == 0:
                        eng.wait_ge(x_res.sem, after(x_res, g))
                        settle(eng)
                        eng.bn_stats(st2[:, b, :], x_all[:, bass.ds(g, 1), :]).then_inc(x_stat2.sem, 1)
                    if k == 1:
                        eng.wait_ge(x_stat2.sem, after(x_stat2, g))
                        settle(eng)
                        eng.bn_aggr(mv2[:, b, :], st2[:, b, :]).then_inc(x_mv2.sem, 1)
                    if k == 2:
                        eng.wait_ge(x_mv2.sem, after(x_mv2, g))
                        eng.wait_ge(x_rstd2.sem, after(x_rstd2, g - 2))
                        eng.tensor_scalar(ve2[:, b, :], mv2[:, b, 1:2], EPS, None, ALU.add).then_inc(x_ve2.sem, 1)

                def normalise_y():
                    g, b = t - X_Y, (p - X_Y) % 2
                    eng.wait_ge(x_rstd2.sem, after(x_rstd2, g))
                    eng.tensor_scalar(y_all[:, bass.ds(g, 1), :], x_all[:, bass.ds(g, 1), :],
                                      mv2[:, b, 0:1], rstd2[:, b, :], ALU.subtract, ALU.mult).then_inc(y_in.sem, 1)

                if active(X_PROJ):
                    normalise()
                if active(X_SCORE):
                    maxima(0)
                if active(X_STAT):
                    stats(0)
                if active(X_Y):
                    stats2(0)
                if active(X_STAT):
                    stats(1)
                if active(X_Y):
                    stats2(1)
                if active(X_SCORE):
                    maxima(1)
                if active(X_STAT):
                    stats(2)
                if active(X_ROT):
                    rotate()
                if active(X_Y):
                    stats2(2)
                if active(X_OUT):
                    inv_sums()
                    o_norm()
                if active(X_SCORE):
                    maxima(2)
                if active(X_ROT):
                    remainder()
                if active(X_SCORE):
                    maxima(3)
                if active(X_ROT):
                    middle_parts(0)
                    middle_parts(1)
                if active(X_Y):
                    normalise_y()
                if active(X_ROT):
                    low_parts(0)
                    low_parts(1)
                if active(X_PROJ):
                    bias_qk()
                if active(X_PARTS):
                    bias_v()
                if active(X_OUT):
                    residual()

            pipeline(eng, step_x, NS, X_Y)

            with eng.Fori(0, LAYERS) as layer:
                base = layer * NS
                eng.memset(hT[:, :, 0, 0:1], 0.0).then_inc(shift_zero, 1)
                eng.wait_ge(wl_in, (layer + 1) * (16 * N_WL))
                eng.tensor_scalar(whi[:, :], wqkv[:, :].bitcast(i32), HIGH_BITS, None, ALU.bitwise_and).then_inc(w_high, 1)
                eng.wait_ge(w_high, layer + 1)
                eng.tensor_tensor(wr[:, 1, :], wqkv[:, :], whi[:, :].bitcast(fp32), ALU.subtract).then_inc(w_split, 1)
                eng.wait_ge(l_t2.sem, after(l_t2, base - 1))
                for i in range(4):
                    eng.tensor_tensor(tab[:, i, :], ropel[:, i, :], scales[:, i, :], ALU.mult).then_inc(tab_ready, 1)
                eng.wait_ge(tab_ready, (layer + 1) * 4)

                def step_l(t, p, active):
                    flat = t1[:, 0, :, :].rearrange("p a b -> p (a b)")

                    def split_tokens():
                        g, b = base + t - L_PROJ, (p - L_PROJ) % 2
                        eng.wait_ge(l_htc.sem, after(l_htc, g))
                        eng.wait_ge(l_hr.sem, after(l_hr, g - 1))
                        eng.wait_ge(l_hi.sem, after(l_hi, g - 1))
                        eng.tensor_scalar(hhi[:, :], hT[:, b, 0, :].bitcast(i32), HIGH_BITS, None, ALU.bitwise_and)\
                           .then_inc(l_hh.sem, 1)
                        eng.wait_ge(l_hh.sem, after(l_hh, g))
                        eng.wait_ge(l_vp.sem, after(l_vp, g - 2))
                        eng.tensor_tensor(hr[:, b, 1, :], hT[:, b, 0, :], hhi[:, :].bitcast(fp32), ALU.subtract)\
                           .then_inc(l_hr.sem, 1)

                    def cosines():
                        g, b = base + t - L_ROT, (p - L_ROT) % 2
                        eng.wait_ge(l_raw.sem, after(l_raw, g))
                        eng.wait_ge(l_rot.sem, after(l_rot, g - 1))
                        eng.tensor_tensor(t1[:, 0, :, :].rearrange("p a (h d) -> p a h d", d=DL),
                                          raw[:, b, :, :].rearrange("p a (h d) -> p a h d", d=DL),
                                          bc(tab[:, 0:4:2, :].unsqueeze(2), [128, 2, HL, DL]), ALU.mult)\
                           .then_inc(l_t1.sem, 1)

                    def squares():
                        g, b = base + t - L_ROT, (p - L_ROT) % 2
                        eng.wait_ge(l_sq.sem, after(l_sq, g))
                        eng.wait_ge(l_ssc.sem, after(l_ssc, g - 2))
                        eng.tensor_reduce(ss[:, b, :], sq[:, :].rearrange("p (h d) -> p h d", d=DL), AX.X, ALU.add)\
                           .then_inc(l_ss.sem, 1)

                    def add_sines():
                        g, b = base + t - L_ROT, (p - L_ROT) % 2
                        eng.wait_ge(l_t1.sem, after(l_t1, g))
                        eng.wait_ge(l_t2.sem, after(l_t2, g))
                        eng.tensor_tensor(flat, flat, t2[:, b, :, :].rearrange("p a b -> p (a b)"), ALU.add)\
                           .then_inc(l_add.sem, 1)

                    def unit_norm():
                        g, b = base + t - L_ROT, (p - L_ROT) % 2
                        eng.wait_ge(l_add.sem, after(l_add, g))
                        eng.wait_ge(l_rn.sem, after(l_rn, g))
                        eng.wait_ge(l_qkt.sem, after(l_qkt, g - 2))
                        eng.tensor_tensor(rot[:, b, :].rearrange("p (h d) -> p h d", d=DL),
                                          flat.rearrange("p (h d) -> p h d", d=DL),
                                          bc(rn[:, b, :].unsqueeze(2), [128, 2 * HL, DL]), ALU.mult)\
                           .then_inc(l_rot.sem, 1)

                    def maxima(c):
                        g, b = base + t - L_SCORE, (p - L_SCORE) % 2
                        eng.wait_ge(l_s.sem, after(l_s, g, c + 1))
                        eng.tensor_reduce(top[:, b, c * CH:(c + 1) * CH],
                                          ps[:, 4 + c, :].rearrange("p (h k) -> p h k", k=128), AX.X, ALU.max)\
                           .then_inc(l_max.sem, 1)

                    def subtract(c):
                        g, b = base + t - L_SCORE, (p - L_SCORE) % 2
                        eng.wait_ge(l_max.sem, after(l_max, g, c + 1))
                        eng.wait_ge(l_pt.sem, after(l_pt, g - 2, c + 1))
                        eng.tensor_tensor(prob[:, b, c * CH:(c + 1) * CH, :],
                                          ps[:, 4 + c, :].rearrange("p (h k) -> p h k", k=128),
                                          bc(top[:, b, c * CH:(c + 1) * CH].unsqueeze(2), [128, CH, 128]),
                                          ALU.subtract).then_inc(l_sub.sem, 1)

                    def inv_sums(c):
                        g = base + t - L_WEIGH
                        o = ps[:, 6 + c, 0:CH * (DL + 1)].rearrange("p (h d) -> p h d", d=DL + 1)
                        eng.wait_ge(l_pv.sem, after(l_pv, g, c + 1))
                        eng.reciprocal(rsum[:, c * CH:(c + 1) * CH].unsqueeze(2), o[:, :, DL:DL + 1])\
                           .then_inc(l_rsum.sem, 1)

                    def o_norm(c):
                        g = base + t - L_WEIGH
                        o = ps[:, 6 + c, 0:CH * (DL + 1)].rearrange("p (h d) -> p h d", d=DL + 1)
                        eng.wait_ge(l_rsum.sem, after(l_rsum, g, c + 1))
                        eng.wait_ge(l_ot.sem, after(l_ot, g - 1))
                        eng.tensor_tensor(o_sb[:, :].rearrange("p (s c d) -> p c s d", c=2, d=DL)[:, c, :, :],
                                          o[:, :, 0:DL],
                                          bc(rsum[:, c * CH:(c + 1) * CH].unsqueeze(2), [128, CH, DL]),
                                          ALU.mult).then_inc(l_o.sem, 1)

                    def residual():
                        g = base + t - L_OUT
                        yi = y_all[:, bass.ds(t - L_OUT, 1), :]
                        eng.wait_ge(l_wo.sem, after(l_wo, g))
                        eng.wait_ge(l_yb.sem, after(l_yb, g))
                        eng.tensor_tensor(yi, ps[:, 0, 128:256].unsqueeze(1), yi, ALU.add).then_inc(y_attn.sem, 1)

                    if active(L_ROT):
                        squares()
                        cosines()
                    if active(L_PROJ):
                        split_tokens()
                    if active(L_ROT):
                        add_sines()
                    if active(L_SCORE):
                        maxima(0)
                        maxima(1)
                        subtract(0)
                        subtract(1)
                    if active(L_ROT):
                        unit_norm()
                    if active(L_WEIGH):
                        inv_sums(0)
                        inv_sums(1)
                        o_norm(0)
                        o_norm(1)
                    if active(L_OUT):
                        residual()

                pipeline(eng, step_l, NS, L_OUT)

                def step_f(t, p, active):
                    def stats(k):
                        g, b = base + t - F_STAT, (p - F_STAT) % 2
                        if k == 0:
                            eng.wait_ge(f_shc.sem, after(f_shc, g))
                            settle(eng)
                            eng.bn_stats(st[:, b, :], yb[:, (p - F_STAT) % UNROLL, :]).then_inc(f_stat.sem, 1)
                        if k == 1:
                            eng.wait_ge(f_stat.sem, after(f_stat, g))
                            settle(eng)
                            eng.bn_aggr(mv[:, b, :], st[:, b, :]).then_inc(f_mv.sem, 1)
                        if k == 2:
                            eng.wait_ge(f_mv.sem, after(f_mv, g))
                            eng.wait_ge(f_rstd.sem, after(f_rstd, g - 2))
                            eng.tensor_scalar(ve[:, b, :], mv[:, b, 1:2], EPS, None, ALU.add).then_inc(f_ve.sem, 1)

                    def normalise():
                        g, b = base + t - F_NORM, (p - F_NORM) % 2
                        eng.wait_ge(f_rstd.sem, after(f_rstd, g))
                        eng.wait_ge(f_t.sem, after(f_t, g - 2))
                        eng.tensor_scalar(xn[:, b, :], yb[:, (p - F_NORM) % UNROLL, :], mv[:, b, 0:1], rstd[:, b, :],
                                          ALU.subtract, ALU.mult).then_inc(f_norm.sem, 1)

                    def gated(j):
                        g, b = base + t - F_UP, (p - F_UP) % 2
                        if j == 0:
                            eng.wait_ge(f_w1.sem, after(f_w1, g))
                            eng.wait_ge(f_w2.sem, after(f_w2, g - 2))
                        n = rows(j)
                        eng.wait_ge(f_gate.sem, after(f_gate, g, j + 1))
                        eng.scalar_tensor_tensor(hid[0:n, b, j, :], ps[0:n, 2 + 4 * b, j * 128:(j + 1) * 128],
                                                 b1[0:n, 0, j:j + 1], gate[0:n, b, j, :], ALU.add, ALU.mult)\
                           .then_inc(f_hid.sem, 1)

                    def residual():
                        g = base + t - F_DOWN
                        yi = y_all[:, bass.ds(t - F_DOWN, 1), :]
                        eng.wait_ge(f_w2.sem, after(f_w2, g))
                        eng.wait_ge(f_yb.sem, after(f_yb, g))
                        eng.tensor_tensor(yi, ps[:, 4, 0:128].unsqueeze(1), yi, ALU.add).then_inc(y_in.sem, 1)

                    if active(F_STAT):
                        stats(0)
                    if active(F_NORM):
                        normalise()
                    if active(F_STAT):
                        stats(1)
                    if active(F_UP):
                        gated(0)
                    if active(F_STAT):
                        stats(2)
                    if active(F_UP):
                        gated(1)
                        gated(2)
                    if active(F_DOWN):
                        residual()

                assert NJ == 3
                eng.wait_ge(wf_in, (layer + 1) * (16 * N_WF_IN))
                pipeline(eng, step_f, NS, F_DOWN)

            n = NS // OUT_CHUNKS
            eng.wait_ge(y_in.sem, after(y_in, (LAYERS + 1) * NS - 1))
            for c in range(OUT_CHUNKS - OUT_GPSIMD):
                part = x_all[:, c * n:(c + 1) * n, :]
                eng.tensor_tensor(part, part, y_all[:, c * n:(c + 1) * n, :], ALU.add).then_inc(out_add, 1)

        @block.gpsimd
        def _(eng):
            begin(eng, x_rstd, x_t, x_topp, x_bo, x_rstd2, l_yb, l_ssc, l_rn, l_t2, f_yb, f_rstd)
            eng.memset(vx[:, :, :, :], 0.0).then_inc(setup_p, 1)
            eng.wait_ge(setup_p, 1)
            for s in range(2):
                eng.memset(vdiag[:, :, s, :, 64 * (1 - s):64 * (1 - s) + DX], 1.0).then_inc(setup_p, 1)
            eng.wait_ge(setup_v, N_SETUP_V)

            def step_x(t, p, active):
                def inv_std():
                    g, b = t - X_STAT, (p - X_STAT) % 2
                    eng.wait_ge(x_ve.sem, after(x_ve, g))
                    eng.wait_ge(x_norm.sem, after(x_norm, g - 2))
                    eng.tensor_tensor(rstd[:, b, :], ve[:, b, :], nhalf[:, 0:1], ALU.pow).then_inc(x_rstd.sem, 1)

                def rotary():
                    g, b = t - X_PROJ, (p - X_PROJ) % 2
                    eng.wait_ge(const_in, 16 * N_CONST)
                    eng.wait_ge(x_bias.sem, after(x_bias, g))
                    eng.wait_ge(x_rot.sem, after(x_rot, g - 2))
                    r = raw[:, 0, 0, 0:256].rearrange("p (h d) -> p h d", d=DX)
                    u = t1[:, b, 0, 0:256].rearrange("p (h d) -> p h d", d=DX)
                    w = t2[:, b, 0, 0:256].rearrange("p (h d) -> p h d", d=DX)
                    H2, NH = DX // 2, 2 * HX
                    eng.tensor_tensor(u, r, bc(ropex[:, 0:1, :], [128, NH, DX]), ALU.mult).then_inc(x_t.sem, 1)
                    eng.tensor_tensor(w[:, :, 0:H2], r[:, :, H2:DX], bc(ropex[:, 1:2, 0:H2], [128, NH, H2]),
                                      ALU.mult).then_inc(x_t.sem, 1)
                    eng.tensor_tensor(w[:, :, H2:DX], r[:, :, 0:H2], bc(ropex[:, 1:2, H2:DX], [128, NH, H2]),
                                      ALU.mult).then_inc(x_t.sem, 1)

                def split_maxima():
                    g, b = t - X_SCORE, (p - X_SCORE) % 2
                    eng.wait_ge(x_max.sem, after(x_max, g))
                    eng.wait_ge(x_topt.sem, after(x_topt, g - 1))
                    settle(eng)
                    eng.tensor_copy(topp[:, 0, :], top[:, b, :]).then_inc(x_topp.sem, 1)
                    eng.wait_ge(x_topp.sem, after(x_topp, g, 1))
                    eng.tensor_tensor(topr[:, :], top[:, b, :], topp[:, 0, :], ALU.subtract).then_inc(x_topp.sem, 1)
                    eng.wait_ge(x_topp.sem, after(x_topp, g, 2))
                    settle(eng)
                    eng.tensor_copy(topp[:, 1, :], topr[:, :]).then_inc(x_topp.sem, 1)
                    eng.wait_ge(x_topp.sem, after(x_topp, g, 3))
                    eng.tensor_tensor(topp[:, 2, :], topr[:, :], topp[:, 1, :], ALU.subtract).then_inc(x_topp.sem, 1)

                def add_bo():
                    g = t - X_ROT
                    xi = x_all[:, bass.ds(g, 1), :]
                    eng.wait_ge(x_norm.sem, after(x_norm, g))
                    eng.tensor_tensor(xi, xi, box[:, :].unsqueeze(1), ALU.add).then_inc(x_bo.sem, 1)

                def inv_std2():
                    g, b = t - X_Y, (p - X_Y) % 2
                    eng.wait_ge(x_ve2.sem, after(x_ve2, g))
                    eng.wait_ge(y_in.sem, after(y_in, g - 2))
                    eng.tensor_tensor(rstd2[:, b, :], ve2[:, b, :], nhalf[:, 0:1], ALU.pow).then_inc(x_rstd2.sem, 1)

                if active(X_STAT):
                    inv_std()
                if active(X_Y):
                    inv_std2()
                if active(X_ROT):
                    add_bo()
                if active(X_SCORE):
                    split_maxima()
                if active(X_PROJ):
                    rotary()

            pipeline(eng, step_x, NS, X_Y)

            with eng.Fori(0, LAYERS) as layer:
                base = layer * NS

                def step_l(t, p, active):
                    def copy_y():
                        g, b = base + t - L_PROJ, (p - L_PROJ) % 2
                        eng.wait_ge(y_in.sem, after(y_in, g))
                        eng.wait_ge(l_ht.sem, after(l_ht, g - 2))
                        settle(eng)
                        eng.tensor_copy(yb[:, b:b + 1, :], y_all[:, bass.ds(t - L_PROJ, 1), :]).then_inc(l_yb.sem, 1)

                    def rotary():
                        g, b = base + t - L_ROT, (p - L_ROT) % 2
                        H2 = DL // 2
                        if not active(L_SCORE):
                            eng.wait_ge(tab_ready, (layer + 1) * 4)
                        eng.wait_ge(l_raw.sem, after(l_raw, g))
                        eng.wait_ge(l_add.sem, after(l_add, g - 2))
                        r = raw[:, b, :, :].rearrange("p a (h d) -> p a h d", d=DL)
                        w = t2[:, b, :, :].rearrange("p a (h d) -> p a h d", d=DL)
                        for dst, src in ((slice(0, H2), slice(H2, DL)), (slice(H2, DL), slice(0, H2))):
                            eng.tensor_tensor(w[:, :, :, dst], r[:, :, :, src],
                                              bc(tab[:, 1:4:2, dst].unsqueeze(2), [128, 2, HL, H2]), ALU.mult)\
                               .then_inc(l_t2.sem, 1)

                    def inv_norm():
                        g, b = base + t - L_ROT, (p - L_ROT) % 2
                        eng.wait_ge(l_ss.sem, after(l_ss, g))
                        settle(eng)
                        eng.tensor_scalar(ssc[:, :], ss[:, b, :], 1e-24, 1.0, ALU.max, ALU.mult).then_inc(l_ssc.sem, 1)
                        eng.wait_ge(l_ssc.sem, after(l_ssc, g))
                        eng.wait_ge(l_rot.sem, after(l_rot, g - 2))
                        eng.tensor_tensor(rn[:, b, :], ssc[:, :], nhalf[:, :], ALU.pow).then_inc(l_rn.sem, 1)

                    if active(L_PROJ):
                        copy_y()
                    if active(L_ROT):
                        rotary()
                        inv_norm()

                pipeline(eng, step_l, NS, L_OUT)

                def step_f(t, p, active):
                    def copy_y():
                        g, b = base + t - F_COPY, (p - F_COPY) % UNROLL
                        eng.wait_ge(y_attn.sem, after(y_attn, g))
                        eng.wait_ge(f_norm.sem, after(f_norm, g - UNROLL))
                        settle(eng)
                        eng.tensor_copy(yb[:, b:b + 1, :], y_all[:, bass.ds(t - F_COPY, 1), :]).then_inc(f_yb.sem, 1)

                    def inv_std():
                        g, b = base + t - F_STAT, (p - F_STAT) % 2
                        eng.wait_ge(f_ve.sem, after(f_ve, g))
                        eng.wait_ge(f_norm.sem, after(f_norm, g - 2))
                        eng.tensor_tensor(rstd[:, b, :], ve[:, b, :], nhalf[:, 0:1], ALU.pow).then_inc(f_rstd.sem, 1)

                    if active(F_COPY):
                        copy_y()
                    if active(F_STAT):
                        inv_std()

                pipeline(eng, step_f, NS, F_DOWN)

            n = NS // OUT_CHUNKS
            eng.wait_ge(y_in.sem, after(y_in, (LAYERS + 1) * NS - 1))
            for c in range(OUT_CHUNKS - OUT_GPSIMD, OUT_CHUNKS):
                part = x_all[:, c * n:(c + 1) * n, :]
                eng.tensor_tensor(part, part, y_all[:, c * n:(c + 1) * n, :], ALU.add).then_inc(out_add_p, 1)


_INS = ["x", "ctx_1024", "L0_xattn_Wq", "L0_xattn_bq", "L0_xattn_Wk", "L0_xattn_bk", "L0_xattn_Wv", "L0_xattn_bv",
        "L0_xattn_Wo", "L0_xattn_bo", "L0_ffn_wqkv", "L0_ffn_q_scale", "L0_ffn_k_scale", "L0_ffn_wo", "L0_ffn_ln_g",
        "L0_ffn_ln_b", "L0_ffn_w1", "L0_ffn_b1", "L0_ffn_w2", "L0_ffn_b2"]


def constants(T, DX, HX, DL):
    import numpy as np

    f = np.float32
    ident = np.eye(128, dtype=f)
    shift = np.eye(128, k=1, dtype=f)
    i, j = np.arange(T)[:, None], np.arange(T)[None, :]
    band = np.where((i < j) | (i > j + 64), f(-1e30), f(0))
    t = np.arange(T, dtype=f)
    inv = (f(1.0) / f(10000.0) ** (np.arange(0, DX, 2, dtype=f) / f(DX))).astype(f)
    ang = t[:, None] * inv[None, :]
    ang = np.concatenate([ang, ang], axis=-1).astype(f)
    sign = np.concatenate([-np.ones(DX // 2, f), np.ones(DX // 2, f)])
    ropex = np.stack([np.cos(ang), np.sin(ang) * sign], axis=1)
    half = np.arange(0, DL, 2, dtype=f)
    inv = (f(1.0) / f(10000.0) ** (half / f(DL))).astype(f)
    ang = t[:, None] * inv[None, :]
    ang = np.concatenate([ang, ang], axis=-1).astype(f)
    base = (half + f(0.4 * DL)) / f(1.4 * DL)
    power = (t - f(T // 2)) / f(32.0)
    scale = (base[None, :] ** power[:, None]).astype(f)
    scale = np.concatenate([scale, scale], axis=-1)
    sign = np.concatenate([-np.ones(DL // 2, f), np.ones(DL // 2, f)])
    cos, sin = np.cos(ang), np.sin(ang) * sign
    ropel = np.stack([cos * scale, sin * scale, cos / scale, sin / scale], axis=1)
    gmask = (np.arange(128)[:, None] // DX % 2 == np.arange(2)[None, :]).astype(f)
    sel = -(np.arange(3 * HX)[:, None] % HX == np.arange(HX)[None, :]).astype(f)
    return {"c_ident": ident, "c_shift": shift, "c_band": band, "c_ropex": ropex.astype(f),
            "c_ropel": ropel.astype(f), "c_gmask": gmask, "c_sel": sel}


def kernel(**inputs):
    import numpy as np
    import concourse.bacc as bacc
    from concourse.bass_utils import run_bass_kernel_spmd

    nc = bacc.Bacc("TRN2", target_bir_lowering=False, num_devices=1)
    arrays = {name: np.ascontiguousarray(inputs[name]) for name in _INS}
    arrays.update({k: np.ascontiguousarray(v) for k, v in constants(128, 8, 16, 64).items()})
    ins = {name: nc.dram_tensor(name + "_dram", a.shape, mybir.dt.from_np(a.dtype), kind="ExternalInput").ap()
           for name, a in arrays.items()}
    out = nc.dram_tensor("out_dram", inputs["x"].shape, fp32, kind="ExternalOutput").ap()
    build(nc, ins, out)
    r = run_bass_kernel_spmd(nc, [{name + "_dram": a for name, a in arrays.items()}], core_ids=[0])
    return r.results[0]["out_dram"]
```
